# Optimizing a Trainium2 kernel written in Bass

```python
import numpy as np
import jax
import jax.numpy as jnp

def _softmax(x, axis=-1):
    return jax.nn.softmax(x, axis=axis)

def _gelu(x):
    return jax.nn.gelu(x, approximate=True)

def _silu(x):
    return jax.nn.silu(x)

def _sigmoid(x):
    return jax.nn.sigmoid(x)

def _layernorm(x, axis=-1, eps=1e-05):
    m = jnp.mean(x, axis=axis, keepdims=True)
    v = jnp.var(x, axis=axis, keepdims=True)
    return (x - m) / jnp.sqrt(v + eps)

def _scatter_add(tgt, idx, src, axis=0):
    return tgt.at[idx].add(src)

def _segment_sum(src, seg, n):
    return jax.ops.segment_sum(src, seg, n)
kernel_name = 'mk_decoder_postln_d2_seqx_r8_7ba2c5'

def setup_inputs(seed: int=0):
    np.random.seed(seed)
    _w = jnp.asarray

    def _rec_inputs():
        import jax
        import jax.numpy as jnp
        _rk = jax.random.key(seed)
        x = -0.0002928 + 1 * jax.random.normal(jax.random.fold_in(_rk, 1), (4, 256, 128), jnp.float32)
        _lenS = 256 - jax.random.randint(jax.random.fold_in(_rk, 7), (4,), 0, max(1, 256 // 4) + 1, jnp.int32)
        _lenS2 = 1601 - jax.random.randint(jax.random.fold_in(_rk, 8), (4,), 0, max(1, 1601 // 4) + 1, jnp.int32)
        _ctx_512P = jax.random.normal(jax.random.fold_in(_rk, 11), (4, 16, 64), jnp.float32)
        _ctx_512c = jax.random.dirichlet(jax.random.fold_in(_rk, 511), 0.3 * jnp.ones((16,), jnp.float32), (4, 1601))
        _ctx_512t = jnp.einsum('bsk,bkd->bsd', _ctx_512c, _ctx_512P)
        _ctx_512t = _ctx_512t * jax.lax.rsqrt(jnp.mean(jnp.square(_ctx_512t)) + 1e-12) * 0.953939
        ctx_512 = 0.00222621 + 0.99962 * (_ctx_512t + 0.3 * jax.random.normal(jax.random.fold_in(_rk, 611), (4, 1601, 64), jnp.float32))
        return (x, ctx_512)
    x, ctx_512 = _rec_inputs()

    def _L0_attn_setup():
        import jax, jax.numpy as jnp
        import numpy as np
        B, S, D = (4, 256, 128)
        GAMMA = 1.0
        key = jax.random.key(seed)
        ks = jax.random.split(key, 9)
        scale = 1.0 / np.sqrt(D)
        return {'x': jax.random.normal(ks[0], (B, S, D), dtype=jnp.float32), 'Wq': jax.random.normal(ks[1], (D, D), dtype=jnp.float32) * scale, 'bq': jax.random.normal(ks[2], (D,), dtype=jnp.float32) * 0.01, 'Wk': jax.random.normal(ks[3], (D, D), dtype=jnp.float32) * scale, 'bk': jax.random.normal(ks[4], (D,), dtype=jnp.float32) * 0.01, 'Wv': jax.random.normal(ks[5], (D, D), dtype=jnp.float32) * scale, 'bv': jax.random.normal(ks[6], (D,), dtype=jnp.float32) * 0.01, 'Wo': jax.random.normal(ks[7], (D, D), dtype=jnp.float32) * scale, 'bo': jax.random.normal(ks[8], (D,), dtype=jnp.float32) * 0.01}
    _L0_attn_all = _L0_attn_setup()
    _L0_attn_in = {k: v for k, v in _L0_attn_all.items() if k in ('Wq', 'bq', 'Wk', 'bk', 'Wv', 'bv', 'Wo', 'bo')}
    del _L0_attn_all

    def _L0_xattn_setup():
        import jax, jax.numpy as jnp
        import numpy as np
        B, T, TC, C, CC, H = (2, 256, 64, 128, 64, 16)
        D = C // H

        def _heads(t):
            b, l, _ = t.shape
            return t.reshape(b, l, H, D).transpose(0, 2, 1, 3)
        key = jax.random.key(seed)
        ks = jax.random.split(key, 18)
        w = lambda k, i, o: jax.random.normal(k, (i, o), jnp.float32) / np.sqrt(i).astype(np.float32)
        return {'x': jax.random.normal(ks[0], (B, T, C), jnp.float32), 'cross_input': jax.random.normal(ks[1], (B, TC, CC), jnp.float32), 'Wk': w(ks[2], C, C), 'bk': jnp.zeros((C,), jnp.float32), 'Wq': w(ks[3], C, C), 'bq': jnp.zeros((C,), jnp.float32), 'Wv': w(ks[4], C, C), 'bv': jnp.zeros((C,), jnp.float32), 'Wck': w(ks[5], CC, C), 'bck': jnp.zeros((C,), jnp.float32), 'Wcq': w(ks[6], C, C), 'bcq': jnp.zeros((C,), jnp.float32), 'Wcv': w(ks[7], CC, C), 'bcv': jnp.zeros((C,), jnp.float32), 'Wp': w(ks[8], C, C), 'bp': jnp.zeros((C,), jnp.float32)}
    _L0_xattn_all = _L0_xattn_setup()
    _L0_xattn_in = {k: v for k, v in _L0_xattn_all.items() if k in ('Wk', 'bk', 'Wq', 'bq', 'Wv', 'bv', 'Wck', 'bck', 'Wcq', 'bcq', 'Wcv', 'bcv', 'Wp', 'bp')}
    del _L0_xattn_all

    def _L0_ffn_setup():
        import jax, jax.numpy as jnp
        import numpy as np
        B, S, H, DFF, E, K = (2, 256, 128, 256, 8, 2)

        def _moe(x, Wg, W1, b1, W2, b2, W3, b3):
            Bm, Sm, Hm = x.shape
            xt = x.reshape(-1, Hm)
            gout = xt @ Wg.T
            topv, topi = jax.lax.top_k(gout, K)
            w = jax.nn.softmax(topv, axis=-1)
            comb = jnp.einsum('tke,tk->te', jax.nn.one_hot(topi, E, dtype=x.dtype), w)
            g = jnp.einsum('th,efh->etf', xt, W1) + b1[:, None, :]
            v = jnp.einsum('th,efh->etf', xt, W2) + b2[:, None, :]
            h = jax.nn.silu(g) * v
            eo = jnp.einsum('etf,ehf->eth', h, W3) + b3[:, None, :]
            out = jnp.einsum('eth,te->th', eo, comb)
            return out.reshape(Bm, Sm, Hm)
        key = jax.random.key(seed)
        ks = jax.random.split(key, 8)
        sc_h = 1.0 / np.sqrt(H)
        sc_f = 1.0 / np.sqrt(DFF)
        x = jax.random.normal(ks[0], (B, S, H), dtype=jnp.float32)
        Wg = jax.random.uniform(ks[1], (E, H), jnp.float32, -sc_h, sc_h)
        W1 = jax.random.uniform(ks[2], (E, DFF, H), jnp.float32, -sc_h, sc_h)
        b1 = jax.random.uniform(ks[3], (E, DFF), jnp.float32, -sc_h, sc_h)
        W2 = jax.random.uniform(ks[4], (E, DFF, H), jnp.float32, -sc_h, sc_h)
        b2 = jax.random.uniform(ks[5], (E, DFF), jnp.float32, -sc_h, sc_h)
        W3 = jax.random.uniform(ks[6], (E, H, DFF), jnp.float32, -sc_f, sc_f)
        b3 = jax.random.uniform(ks[7], (E, H), jnp.float32, -sc_f, sc_f)
        return {'x': x, 'Wg': Wg, 'W1': W1, 'b1': b1, 'W2': W2, 'b2': b2, 'W3': W3, 'b3': b3}
    _L0_ffn_all = _L0_ffn_setup()
    _L0_ffn_in = {k: v for k, v in _L0_ffn_all.items() if k in ('Wg', 'W1', 'b1', 'W2', 'b2', 'W3', 'b3')}
    del _L0_ffn_all

    def _L1_attn_setup():
        import jax, jax.numpy as jnp
        import numpy as np
        B, S, D_IN = (4, 512, 128)
        D_HID = 256
        D_INNER = D_HID // 2
        NB = 8
        LOG_A_SCALE = -8.0
        R_MIN, R_MAX = (0.9, 0.999)

        def _bdl(x, w, b):
            Bb, Ss, d = x.shape
            nb, bin_, bout = w.shape
            xb = x.reshape(Bb, Ss, nb, bin_)
            y = jnp.einsum('bsni,nio->bsno', xb, w) + b.reshape(nb, bout)
            return y.reshape(Bb, Ss, nb * bout)

        def _reference_tuple_inner(x, w_in, b_in, w_gx, b_gx, w_ga, b_ga, a_real_param, a_imag_param, w_out, b_out):
            xh = x @ w_in + b_in
            gate_x = jax.nn.sigmoid(_bdl(xh, w_gx, b_gx))
            gate_a = jax.nn.sigmoid(_bdl(xh, w_ga, b_ga))
            log_a = LOG_A_SCALE * gate_a * jax.nn.softplus(a_real_param)
            log_a_imag = a_imag_param * gate_a
            a = jnp.exp(jax.lax.complex(log_a, log_a_imag))
            xc = jax.lax.complex(xh[..., :D_INNER], xh[..., D_INNER:])
            xc = gate_x * xc
            norm = jnp.sqrt(jnp.maximum(1.0 - jnp.exp(2.0 * log_a), 1e-06))
            xc = norm * xc

            def combine(l, r):
                return (r[0] * l[0], r[0] * l[1] + r[1])
            _, h = jax.lax.associative_scan(combine, (a, xc), axis=1)
            h_m = jnp.concatenate([h.real, h.imag], axis=-1)
            y = h_m @ w_out + b_out
            h_last = h_m[:, -1]
            return (y, h_last)
        key = jax.random.key(seed)
        ks = jax.random.split(key, 10)
        x = jax.random.normal(ks[0], (B, S, D_IN), dtype=jnp.float32)
        w_in = jax.random.normal(ks[1], (D_IN, D_HID), dtype=jnp.float32) / np.sqrt(D_IN)
        b_in = jnp.zeros((D_HID,), jnp.float32)
        bin_, bout = (D_HID // NB, D_INNER // NB)
        w_gx = jax.random.normal(ks[2], (NB, bin_, bout), dtype=jnp.float32) / np.sqrt(bin_)
        b_gx = jnp.zeros((D_INNER,), jnp.float32)
        w_ga = jax.random.normal(ks[3], (NB, bin_, bout), dtype=jnp.float32) / np.sqrt(bin_)
        b_ga = jnp.zeros((D_INNER,), jnp.float32)
        u = jax.random.uniform(ks[4], (D_INNER,))
        a_real = 0.5 * jnp.log(u * (R_MAX ** 2 - R_MIN ** 2) + R_MIN ** 2 + 1e-08)
        a_real_param = jnp.log(jnp.exp(-a_real) - 1.0)
        a_imag_param = jnp.pi * 0.1 * jax.random.uniform(ks[5], (D_INNER,))
        w_out = jax.random.normal(ks[6], (D_HID, D_IN), dtype=jnp.float32) / np.sqrt(D_HID)
        b_out = jnp.zeros((D_IN,), jnp.float32)
        return dict(x=x, w_in=w_in, b_in=b_in, w_gx=w_gx, b_gx=b_gx, w_ga=w_ga, b_ga=b_ga, a_real_param=a_real_param, a_imag_param=a_imag_param, w_out=w_out, b_out=b_out)
    _L1_attn_all = _L1_attn_setup()
    _L1_attn_in = {k: v for k, v in _L1_attn_all.items() if k in ('w_in', 'b_in', 'w_gx', 'b_gx', 'w_ga', 'b_ga', 'a_real_param', 'a_imag_param', 'w_out', 'b_out')}
    del _L1_attn_all

    def _L1_xattn_setup():
        import jax, jax.numpy as jnp
        import numpy as np
        B, LQ, LK = (8, 256, 256)
        QD, KD, VD = (128, 64, 64)
        key = jax.random.key(seed)
        ks = jax.random.split(key, 9)
        s = 0.02
        return {'query': jax.random.normal(ks[0], (B, LQ, QD), jnp.float32), 'key': jax.random.normal(ks[1], (B, LK, KD), jnp.float32), 'value': jax.random.normal(ks[2], (B, LK, VD), jnp.float32), 'Wq': jax.random.normal(ks[3], (QD, QD), jnp.float32) * s, 'bq': jnp.zeros((QD,), jnp.float32), 'Wk': jax.random.normal(ks[4], (KD, QD), jnp.float32) * s, 'bk': jnp.zeros((QD,), jnp.float32), 'Wv': jax.random.normal(ks[5], (VD, QD), jnp.float32) * s, 'bv': jnp.zeros((QD,), jnp.float32)}
    _L1_xattn_all = _L1_xattn_setup()
    _L1_xattn_in = {k: v for k, v in _L1_xattn_all.items() if k in ('Wq', 'bq', 'Wk', 'bk', 'Wv', 'bv')}
    del _L1_xattn_all

    def _L1_ffn_setup():
        import jax, jax.numpy as jnp
        import numpy as np
        D_IN, D_HID = (128, 512)

        def _ternary(key, shape):
            return jax.random.randint(key, shape, -1, 2).astype(jnp.float32)

        def _tlin(x, w, s):
            return jnp.einsum('bsi,oi->bso', x, w) * s
        key = jax.random.key(seed)
        ks = jax.random.split(key, 12)
        inv = lambda fan: 1.0 / np.sqrt(fan).astype(np.float32)
        return {'x': jax.random.normal(ks[0], (4, 256, D_IN), dtype=jnp.float32), 'w1_w': _ternary(ks[1], (D_HID, D_IN)), 'w1_s': jax.random.uniform(ks[2], (D_HID,), dtype=jnp.float32) * inv(D_IN), 'w2_w': _ternary(ks[3], (D_HID, D_IN)), 'w2_s': jax.random.uniform(ks[4], (D_HID,), dtype=jnp.float32) * inv(D_IN), 'h1_w': _ternary(ks[5], (D_HID, D_HID)), 'h1_s': jax.random.uniform(ks[6], (D_HID,), dtype=jnp.float32) * inv(D_HID), 'h2_w': _ternary(ks[7], (D_HID, D_HID)), 'h2_s': jax.random.uniform(ks[8], (D_HID,), dtype=jnp.float32) * inv(D_HID), 'w3_w': _ternary(ks[9], (D_IN, D_HID)), 'w3_s': jax.random.uniform(ks[10], (D_IN,), dtype=jnp.float32) * inv(D_HID)}
    _L1_ffn_all = _L1_ffn_setup()
    _L1_ffn_in = {k: v for k, v in _L1_ffn_all.items() if k in ('w1_w', 'w1_s', 'w2_w', 'w2_s', 'h1_w', 'h1_s', 'h2_w', 'h2_s', 'w3_w', 'w3_s')}
    del _L1_ffn_all
    return {'x': x, 'ctx_512': ctx_512, 'L0_attn_Wq': _L0_attn_in['Wq'], 'L0_attn_bq': _L0_attn_in['bq'], 'L0_attn_Wk': _L0_attn_in['Wk'], 'L0_attn_bk': _L0_attn_in['bk'], 'L0_attn_Wv': _L0_attn_in['Wv'], 'L0_attn_bv': _L0_attn_in['bv'], 'L0_attn_Wo': _L0_attn_in['Wo'], 'L0_attn_bo': _L0_attn_in['bo'], 'L0_xattn_Wk': _L0_xattn_in['Wk'], 'L0_xattn_bk': _L0_xattn_in['bk'], 'L0_xattn_Wq': _L0_xattn_in['Wq'], 'L0_xattn_bq': _L0_xattn_in['bq'], 'L0_xattn_Wv': _L0_xattn_in['Wv'], 'L0_xattn_bv': _L0_xattn_in['bv'], 'L0_xattn_Wck': _L0_xattn_in['Wck'], 'L0_xattn_bck': _L0_xattn_in['bck'], 'L0_xattn_Wcq': _L0_xattn_in['Wcq'], 'L0_xattn_bcq': _L0_xattn_in['bcq'], 'L0_xattn_Wcv': _L0_xattn_in['Wcv'], 'L0_xattn_bcv': _L0_xattn_in['bcv'], 'L0_xattn_Wp': _L0_xattn_in['Wp'], 'L0_xattn_bp': _L0_xattn_in['bp'], 'L0_ffn_Wg': _L0_ffn_in['Wg'], 'L0_ffn_W1': _L0_ffn_in['W1'], 'L0_ffn_b1': _L0_ffn_in['b1'], 'L0_ffn_W2': _L0_ffn_in['W2'], 'L0_ffn_b2': _L0_ffn_in['b2'], 'L0_ffn_W3': _L0_ffn_in['W3'], 'L0_ffn_b3': _L0_ffn_in['b3'], 'L1_attn_w_in': _L1_attn_in['w_in'], 'L1_attn_b_in': _L1_attn_in['b_in'], 'L1_attn_w_gx': _L1_attn_in['w_gx'], 'L1_attn_b_gx': _L1_attn_in['b_gx'], 'L1_attn_w_ga': _L1_attn_in['w_ga'], 'L1_attn_b_ga': _L1_attn_in['b_ga'], 'L1_attn_a_real_param': _L1_attn_in['a_real_param'], 'L1_attn_a_imag_param': _L1_attn_in['a_imag_param'], 'L1_attn_w_out': _L1_attn_in['w_out'], 'L1_attn_b_out': _L1_attn_in['b_out'], 'L1_xattn_Wq': _L1_xattn_in['Wq'], 'L1_xattn_bq': _L1_xattn_in['bq'], 'L1_xattn_Wk': _L1_xattn_in['Wk'], 'L1_xattn_bk': _L1_xattn_in['bk'], 'L1_xattn_Wv': _L1_xattn_in['Wv'], 'L1_xattn_bv': _L1_xattn_in['bv'], 'L1_ffn_w1_w': _L1_ffn_in['w1_w'], 'L1_ffn_w1_s': _L1_ffn_in['w1_s'], 'L1_ffn_w2_w': _L1_ffn_in['w2_w'], 'L1_ffn_w2_s': _L1_ffn_in['w2_s'], 'L1_ffn_h1_w': _L1_ffn_in['h1_w'], 'L1_ffn_h1_s': _L1_ffn_in['h1_s'], 'L1_ffn_h2_w': _L1_ffn_in['h2_w'], 'L1_ffn_h2_s': _L1_ffn_in['h2_s'], 'L1_ffn_w3_w': _L1_ffn_in['w3_w'], 'L1_ffn_w3_s': _L1_ffn_in['w3_s']}

def reference(x, ctx_512, L0_attn_Wq, L0_attn_bq, L0_attn_Wk, L0_attn_bk, L0_attn_Wv, L0_attn_bv, L0_attn_Wo, L0_attn_bo, L0_xattn_Wk, L0_xattn_bk, L0_xattn_Wq, L0_xattn_bq, L0_xattn_Wv, L0_xattn_bv, L0_xattn_Wck, L0_xattn_bck, L0_xattn_Wcq, L0_xattn_bcq, L0_xattn_Wcv, L0_xattn_bcv, L0_xattn_Wp, L0_xattn_bp, L0_ffn_Wg, L0_ffn_W1, L0_ffn_b1, L0_ffn_W2, L0_ffn_b2, L0_ffn_W3, L0_ffn_b3, L1_attn_w_in, L1_attn_b_in, L1_attn_w_gx, L1_attn_b_gx, L1_attn_w_ga, L1_attn_b_ga, L1_attn_a_real_param, L1_attn_a_imag_param, L1_attn_w_out, L1_attn_b_out, L1_xattn_Wq, L1_xattn_bq, L1_xattn_Wk, L1_xattn_bk, L1_xattn_Wv, L1_xattn_bv, L1_ffn_w1_w, L1_ffn_w1_s, L1_ffn_w2_w, L1_ffn_w2_s, L1_ffn_h1_w, L1_ffn_h1_s, L1_ffn_h2_w, L1_ffn_h2_s, L1_ffn_w3_w, L1_ffn_w3_s):
    import jax
    import jax.numpy as jnp

    def _L0_attn_ref(x, Wq, bq, Wk, bk, Wv, bv, Wo, bo):
        import jax, jax.numpy as jnp
        import numpy as np
        B, S, D = (4, 256, 128)
        GAMMA = 1.0
        q = x @ Wq + bq
        k = x @ Wk + bk
        v = x @ Wv + bv
        q_sq = jnp.sum(q * q, axis=-1)
        k_sq = jnp.sum(k * k, axis=-1)
        qk = jnp.einsum('bqd,bkd->bqk', q, k)
        dist_sq = q_sq[:, :, None] + k_sq[:, None, :] - 2.0 * qk
        scores = jnp.exp(-GAMMA * dist_sq)
        attn = jax.nn.softmax(scores, axis=-1)
        out = jnp.einsum('bqk,bkd->bqd', attn, v)
        return out @ Wo + bo

    def _L0_xattn_ref(x, cross_input, Wk, bk, Wq, bq, Wv, bv, Wck, bck, Wcq, bcq, Wcv, bcv, Wp, bp):
        import jax, jax.numpy as jnp
        import numpy as np
        B, T, TC, C, CC, H = (2, 256, 64, 128, 64, 16)
        D = C // H

        def _heads(t):
            b, l, _ = t.shape
            return t.reshape(b, l, H, D).transpose(0, 2, 1, 3)
        scale = np.float32(1.0 / np.sqrt(D))
        q = _heads(x @ Wq + bq)
        k = _heads(x @ Wk + bk)
        v = _heads(x @ Wv + bv)
        att = jnp.einsum('bhqd,bhkd->bhqk', q, k) * scale
        causal = jnp.tril(jnp.ones((T, T), bool))
        att = jnp.where(causal[None, None], att, -jnp.inf)
        y = jnp.einsum('bhqk,bhkd->bhqd', jax.nn.softmax(att, axis=-1), v)
        qc = _heads(x @ Wcq + bcq)
        kc = _heads(cross_input @ Wck + bck)
        vc = _heads(cross_input @ Wcv + bcv)
        attc = jnp.einsum('bhqd,bhkd->bhqk', qc, kc) * scale
        y = y + jnp.einsum('bhqk,bhkd->bhqd', jax.nn.softmax(attc, axis=-1), vc)
        y = y.transpose(0, 2, 1, 3).reshape(x.shape[0], T, C)
        return y @ Wp + bp

    def _L0_ffn_ref(x, Wg, W1, b1, W2, b2, W3, b3):
        import jax, jax.numpy as jnp
        import numpy as np
        B, S, H, DFF, E, K = (2, 256, 128, 256, 8, 2)

        def _moe(x, Wg, W1, b1, W2, b2, W3, b3):
            Bm, Sm, Hm = x.shape
            xt = x.reshape(-1, Hm)
            gout = xt @ Wg.T
            topv, topi = jax.lax.top_k(gout, K)
            w = jax.nn.softmax(topv, axis=-1)
            comb = jnp.einsum('tke,tk->te', jax.nn.one_hot(topi, E, dtype=x.dtype), w)
            g = jnp.einsum('th,efh->etf', xt, W1) + b1[:, None, :]
            v = jnp.einsum('th,efh->etf', xt, W2) + b2[:, None, :]
            h = jax.nn.silu(g) * v
            eo = jnp.einsum('etf,ehf->eth', h, W3) + b3[:, None, :]
            out = jnp.einsum('eth,te->th', eo, comb)
            return out.reshape(Bm, Sm, Hm)
        return _moe(x, Wg, W1, b1, W2, b2, W3, b3)

    def _L1_attn_ref(x, w_in, b_in, w_gx, b_gx, w_ga, b_ga, a_real_param, a_imag_param, w_out, b_out):
        import jax, jax.numpy as jnp
        import numpy as np
        B, S, D_IN = (4, 512, 128)
        D_HID = 256
        D_INNER = D_HID // 2
        NB = 8
        LOG_A_SCALE = -8.0
        R_MIN, R_MAX = (0.9, 0.999)

        def _bdl(x, w, b):
            Bb, Ss, d = x.shape
            nb, bin_, bout = w.shape
            xb = x.reshape(Bb, Ss, nb, bin_)
            y = jnp.einsum('bsni,nio->bsno', xb, w) + b.reshape(nb, bout)
            return y.reshape(Bb, Ss, nb * bout)

        def _reference_tuple_inner(x, w_in, b_in, w_gx, b_gx, w_ga, b_ga, a_real_param, a_imag_param, w_out, b_out):
            xh = x @ w_in + b_in
            gate_x = jax.nn.sigmoid(_bdl(xh, w_gx, b_gx))
            gate_a = jax.nn.sigmoid(_bdl(xh, w_ga, b_ga))
            log_a = LOG_A_SCALE * gate_a * jax.nn.softplus(a_real_param)
            log_a_imag = a_imag_param * gate_a
            a = jnp.exp(jax.lax.complex(log_a, log_a_imag))
            xc = jax.lax.complex(xh[..., :D_INNER], xh[..., D_INNER:])
            xc = gate_x * xc
            norm = jnp.sqrt(jnp.maximum(1.0 - jnp.exp(2.0 * log_a), 1e-06))
            xc = norm * xc

            def combine(l, r):
                return (r[0] * l[0], r[0] * l[1] + r[1])
            _, h = jax.lax.associative_scan(combine, (a, xc), axis=1)
            h_m = jnp.concatenate([h.real, h.imag], axis=-1)
            y = h_m @ w_out + b_out
            h_last = h_m[:, -1]
            return (y, h_last)
        return _reference_tuple_inner(x, w_in, b_in, w_gx, b_gx, w_ga, b_ga, a_real_param, a_imag_param, w_out, b_out)[0]

    def _L1_xattn_ref(query, key, value, Wq, bq, Wk, bk, Wv, bv):
        import jax, jax.numpy as jnp
        import numpy as np
        B, LQ, LK = (8, 256, 256)
        QD, KD, VD = (128, 64, 64)
        q = jnp.einsum('bld,de->ble', query, Wq) + bq
        k = jnp.einsum('bld,de->ble', key, Wk) + bk
        v = jnp.einsum('bld,de->ble', value, Wv) + bv
        scores = jnp.einsum('bqe,bke->bqk', q, k)
        attn = jax.nn.softmax(scores, axis=-1)
        out = jnp.einsum('bqk,bke->bqe', attn, v)
        return out

    def _L1_ffn_ref(x, w1_w, w1_s, w2_w, w2_s, h1_w, h1_s, h2_w, h2_s, w3_w, w3_s):
        import jax, jax.numpy as jnp
        import numpy as np
        D_IN, D_HID = (128, 512)

        def _ternary(key, shape):
            return jax.random.randint(key, shape, -1, 2).astype(jnp.float32)

        def _tlin(x, w, s):
            return jnp.einsum('bsi,oi->bso', x, w) * s
        h = jax.nn.silu(_tlin(x, w1_w, w1_s)) * _tlin(x, w2_w, w2_s)
        h = jax.nn.gelu(_tlin(h, h1_w, h1_s), approximate=False)
        h = jax.nn.gelu(_tlin(h, h2_w, h2_s), approximate=False)
        return _tlin(h, w3_w, w3_s)
    x = _layernorm(x + _L0_attn_ref(x, L0_attn_Wq, L0_attn_bq, L0_attn_Wk, L0_attn_bk, L0_attn_Wv, L0_attn_bv, L0_attn_Wo, L0_attn_bo), axis=-1)
    x = _layernorm(x + _L0_xattn_ref(x, ctx_512, L0_xattn_Wk, L0_xattn_bk, L0_xattn_Wq, L0_xattn_bq, L0_xattn_Wv, L0_xattn_bv, L0_xattn_Wck, L0_xattn_bck, L0_xattn_Wcq, L0_xattn_bcq, L0_xattn_Wcv, L0_xattn_bcv, L0_xattn_Wp, L0_xattn_bp), axis=-1)
    x = _layernorm(x + _L0_ffn_ref(x, L0_ffn_Wg, L0_ffn_W1, L0_ffn_b1, L0_ffn_W2, L0_ffn_b2, L0_ffn_W3, L0_ffn_b3), axis=-1)
    x = _layernorm(x + _L1_attn_ref(x, L1_attn_w_in, L1_attn_b_in, L1_attn_w_gx, L1_attn_b_gx, L1_attn_w_ga, L1_attn_b_ga, L1_attn_a_real_param, L1_attn_a_imag_param, L1_attn_w_out, L1_attn_b_out), axis=-1)
    x = _layernorm(x + _L1_xattn_ref(x, ctx_512, ctx_512, L1_xattn_Wq, L1_xattn_bq, L1_xattn_Wk, L1_xattn_bk, L1_xattn_Wv, L1_xattn_bv), axis=-1)
    x = _layernorm(x + _L1_ffn_ref(x, L1_ffn_w1_w, L1_ffn_w1_s, L1_ffn_w2_w, L1_ffn_w2_s, L1_ffn_h1_w, L1_ffn_h1_s, L1_ffn_h2_w, L1_ffn_h2_s, L1_ffn_w3_w, L1_ffn_w3_s), axis=-1)
    return x

_drawn_inputs = setup_inputs


def setup_inputs(seed=0):
    import zlib

    import numpy as np

    out = dict(_drawn_inputs(seed))
    spreads = {'L0_xattn_bk': (0.0, 0.8),
     'L0_xattn_bq': (0.0, 0.36),
     'L0_xattn_bv': (0.0, 0.1),
     'L0_xattn_bck': (0.0, 0.8),
     'L0_xattn_bcq': (0.0, 0.291),
     'L0_xattn_bcv': (0.0, 0.1),
     'L0_xattn_bp': (0.0, 0.1),
     'L1_attn_b_in': (0.0, 0.1),
     'L1_attn_b_gx': (0.0, 0.279),
     'L1_attn_b_ga': (0.0, 0.403),
     'L1_attn_b_out': (0.0, 0.1),
     'L1_xattn_bq': (0.0, 0.8),
     'L1_xattn_bk': (0.0, 0.8),
     'L1_xattn_bv': (0.0, 0.1)}
    factors = {'L0_attn_bo': 2.937,
     'L0_ffn_b1': 8.0,
     'L0_ffn_b2': 8.0,
     'L1_xattn_Wq': 4.141,
     'L1_xattn_Wk': 4.244,
     'L1_ffn_w1_w': 8.0,
     'L1_ffn_w1_s': 8.0,
     'L1_ffn_w2_w': 8.0,
     'L1_ffn_w2_s': 8.0,
     'L1_ffn_h1_w': 8.0,
     'L1_ffn_h1_s': 8.0,
     'L1_ffn_h2_w': 8.0,
     'L1_ffn_h2_s': 8.0,
     'L1_ffn_w3_w': 8.0,
     'L1_ffn_w3_s': 8.0}
    for name, (base, spread) in spreads.items():
        noise = np.random.default_rng([zlib.crc32(name.encode()), seed]).standard_normal(out[name].shape)
        drawn = base * np.exp(spread * noise) if base else spread * noise
        out[name] = jnp.asarray(drawn.astype(out[name].dtype))
    for name, factor in factors.items():
        out[name] = (out[name] * factor).astype(out[name].dtype)
    return out
```

```python
from contextlib import ExitStack

import numpy as np

import concourse.bass as bass
from concourse import mybir

ALU = mybir.AluOpType
ACT = mybir.ActivationFunctionType
AX = mybir.AxisListType
F32 = mybir.dt.float32
BF16 = mybir.dt.bfloat16
U32 = mybir.dt.uint32

NB, TQ, C = 4, 256, 128
T = NB * TQ
H, HD = 16, 8
TK, CC = 1601, 64
NKT = (TK + 127) // 128
KLAST = TK - 128 * (NKT - 1)
NG = H // 4
NU = NB * NG
NST = NKT + 2
ROWS = 6 * HD
KROWS = ROWS + 2
VW = 16
E, DFF = 8, 256
HID = 512
CH = 512
NCH = T // CH
EPS = 1e-5
SCALE = float(np.float32(1.0 / np.sqrt(HD)))
KPART = (0, 0, 0, 1, 1, 2)
QPART = (0, 1, 2, 0, 1, 0)
SLOTS = 3
MASKED = -1e30
ROUND = 12582912.0
ROUND12 = 3072.0
PI = float(np.pi)


def decoder_program(nc, a, out):
    persistent = ExitStack()
    with persistent:
        def keep(name, shape, dt=F32):
            return persistent.enter_context(nc.sbuf_tensor(name, shape, dt))

        first_sems = ExitStack()
        sem_owner = [first_sems]
        first_named = []

        def sems(stack, *names):
            made = [sem_owner[0].enter_context(nc.semaphore(n)) for n in names]
            if sem_owner[0] is first_sems:
                first_named.extend(made)
            return made

        X = keep("X", [C, T])
        R = keep("R", [C, T])
        mean_out = keep("mean_out", [C, C])
        averager = keep("averager", [C, C])
        ctx_t = keep("ctx_t", [CC + 2, NB, TK])
        biases = keep("biases", [C, a["biases"].shape[1]])
        col = {n: biases[:, i:i + 1] for i, n in enumerate(BIAS_COLUMNS)}

        kc_scr = nc.dram_tensor("kc_scr", [NB, 8, 6, 16, TK], BF16).ap()
        vc_scr = nc.dram_tensor("vc_scr", [NB, NG, 128, NKT * 64], F32).ap()
        xs_scr = {n: nc.dram_tensor(f"{n}_scr", [NB, 8, 6, 16, TQ], BF16).ap() for n in ("ks", "qs", "qc")}
        vs_scr = nc.dram_tensor("vs_scr", [NB, NG, 128, 128], F32).ap()
        comb_scr = nc.dram_tensor("comb_scr", [E, T], F32).ap()

        def ln_parts(stack, tag, psum_c, psum_v, r_ready):
            sq = stack.enter_context(nc.sbuf_tensor(f"{tag}_sq", [C, T], F32))
            lnv = stack.enter_context(nc.sbuf_tensor(f"{tag}_ln", [C, T], F32))
            rstd = stack.enter_context(nc.sbuf_tensor(f"{tag}_rstd", [C, T], F32))
            centred, squared, var_ready, lnv_ready, rstd_ready, x_ready = sems(
                stack, *[f"{tag}_{n}" for n in ("centred", "squared", "var", "lnv", "rstd", "x")])

            def pe(c):
                nc.tensor.wait_ge(r_ready, c + 1)
                nc.tensor.matmul(psum_c[:, c, :], mean_out[:], R[:, c * CH:(c + 1) * CH],
                                 start=True, stop=True).then_inc(centred, 1)

            def pe2(c):
                nc.tensor.wait_ge(squared, c + 1)
                nc.tensor.matmul(psum_v[:, c, :], averager[:], sq[:, c * CH:(c + 1) * CH],
                                 start=True, stop=True).then_inc(var_ready, 1)

            def act(c):
                nc.scalar.wait_ge(centred, c + 1)
                nc.scalar.activation(sq[:, c * CH:(c + 1) * CH], psum_c[:, c, :], ACT.Square).then_inc(squared, 1)

            def act2(c):
                s = slice(c * CH, (c + 1) * CH)
                nc.scalar.wait_ge(var_ready, c + 1)
                nc.scalar.activation(lnv[:, s], psum_v[:, c, :], ACT.Ln, bias=col["eps"]).then_inc(lnv_ready, 1)
                nc.scalar.wait_ge(lnv_ready, c + 1)
                nc.scalar.activation(rstd[:, s], lnv[:, s], ACT.Exp, scale=-0.5).then_inc(rstd_ready, 1)

            def dve(c):
                s = slice(c * CH, (c + 1) * CH)
                nc.vector.wait_ge(rstd_ready, c + 1)
                nc.vector.tensor_tensor(X[:, s], psum_c[:, c, :], rstd[:, s], ALU.mult).then_inc(x_ready, 1)

            return pe, pe2, act, act2, dve, x_ready

        with ExitStack() as st:
            def sb(name, shape, dt=F32):
                return st.enter_context(nc.sbuf_tensor(name, shape, dt))

            wqkv = sb("wqkv", [C, 4, C])
            wx = sb("wx", [C, 3, C])
            wv_pad = sb("wv_pad", [C, H * VW])
            bv_pad = sb("bv_pad", [128, H * VW])
            wck = sb("wck", [CC + 1, C])
            wcv = sb("wcv", [CC + 1, H * VW])
            bv0 = sb("bv0", [128, C])
            half_neg = sb("half_neg", [C, C])
            ones = sb("ones", [C, C])
            neg_col = sb("neg_col", [C, 2])
            qt = sb("qt", [C, T])
            kt = sb("kt", [C, T])
            qsq = sb("qsq", [C, T])
            ksq = sb("ksq", [C, T])
            ksum = sb("ksum", [128, 8])
            v0 = sb("v0", [128, 8, C])
            e1 = sb("e1", [128, 2, 2 * TQ])
            p0 = sb("p0", [128, 2, 2 * TQ])
            lden = sb("lden", [C, 2, TQ])
            rden = sb("rden", [C, 2, TQ])
            ot = sb("ot", [C, 2, TQ])
            hi = sb("hi", [C, 2, 512], BF16)
            mid = sb("mid", [C, 2, 512], BF16)
            low = sb("low", [C, 2, 512], BF16)
            rem = sb("rem", [C, 2, 512])
            rem2 = sb("rem2", [C, 2, 512])
            full = sb("full", [C, 2, 512])
            vst = sb("vst", [128, NG, NKT, 64])
            vss = sb("vss", [128, NB, NG, 2, 64])
            ps = st.enter_context(nc.psum_tensor("ps1", [128, 8, 512], F32))

            (ld_att, ld_ctx, ld_x, cleared) = sems(st, "ld_att", "ld_ctx", "ld_x", "cleared")
            (g_qk, g_qk_sb, g_sq, g_ksum, g_ksum_sb, g_v, g_v_sb, g_s, g_e1, g_p, g_o, g_lden, g_rden, g_ot,
             g_wo, g_r) = sems(st, *[f"g_{n}" for n in (
                 "qk", "qk_sb", "sq", "ksum", "ksum_sb", "v", "v_sb", "s", "e1", "p", "o", "lden", "rden", "ot",
                 "wo", "r")])
            (j_ps, j_hi, j_rem, j_mid, j_rem2, j_low, j_full) = sems(st, *[f"j_{n}" for n in (
                "ps", "hi", "rem", "mid", "rem2", "low", "full")])
            j_out = sems(st, "j_out0", "j_out1")
            (v_ps, v_sb, v_out, w_ps, w_sb, w_out) = sems(st, "v_ps", "v_sb", "v_out", "w_ps", "w_sb", "w_out")

            pieces = [("kc", b, c0, min(512, TK - c0)) for b in range(NB) for c0 in range(0, TK, 512)]
            NPC = len(pieces)
            pieces += [(n, i, b * TQ, TQ) for i, n in enumerate(("ks", "qs", "qc")) for b in range(NB)]
            NPX = len(pieces)

            pe_ln, pe_ln2, act_ln, act_ln2, dve_ln, x_ready = ln_parts(st, "ln1", ps[:, 4:6, :], ps[:, 6:8, :], g_r)

            def piece_target(j):
                kind, i, c0, w = pieces[j]
                if kind == "kc":
                    return [kc_scr[i, :, r, :, c0:c0 + w] for r in range(6)], KPART
                return [xs_scr[kind][c0 // TQ, :, r, :, :] for r in range(6)], (KPART if kind == "ks" else QPART)

            with nc.Block() as block:
                @block.sync
                def _(sp):
                    sp.dma_start(X[:], a["x_t"]).then_inc(ld_x, 16)
                    for dst, src in ((wqkv, "w_att"), (bv0, "bv0"), (half_neg, "half_neg"), (ones, "ones"),
                                     (neg_col, "neg_col"), (biases, "biases"), (mean_out, "mean_out"),
                                     (averager, "averager")):
                        sp.dma_start(dst[:], a[src]).then_inc(ld_att, 16)
                    for j in range(NPX):
                        sp.wait_ge(j_low, j + 1)
                        sp.wait_ge(j_mid, j + 1)
                        sp.wait_ge(j_hi, j + 1)
                        w = pieces[j][3]
                        targets, part = piece_target(j)
                        for r in range(6):
                            src = (hi, mid, low)[part[r]][:, j % 2, 0:w]
                            sp.dma_start(targets[r], src).then_inc(j_out[j % 2], 16)
                    sp.wait_ge(j_out[0], 96 * ((NPX + 1) // 2))
                    sp.wait_ge(j_out[1], 96 * (NPX // 2))

                @block.gpsimd
                def _(pool):
                    pool.memset(vst[:], 0.0).then_inc(cleared, 1)
                    for dst, src in ((wck, "wck"), (wcv, "wcv")):
                        pool.dma_start(dst[:], a[src]).then_inc(ld_ctx, 16)
                    for b in range(NB):
                        pool.dma_start(ctx_t[:, b, :], a["ctx_t"][:, b, :]).then_inc(ld_ctx, 16)
                    for dst, src in ((wx, "wx"), (wv_pad, "wv_pad"), (bv_pad, "bv_pad")):
                        pool.dma_start(dst[:], a[src]).then_inc(ld_ctx, 16)
                    for b in range(NB):
                        pool.wait_ge(v_sb, NKT * (b + 1))
                        pool.dma_start(vc_scr[b].rearrange("g p n -> p g n"),
                                       vst[:].rearrange("p g t n -> p g (t n)")).then_inc(v_out, 16)
                    pool.wait_ge(w_sb, 8)
                    for b in range(NB):
                        pool.dma_start(vs_scr[b].rearrange("g p n -> p g n"),
                                       vss[:, b].rearrange("p g t n -> p g (t n)")).then_inc(w_out, 16)
                    pool.wait_ge(v_out, 16 * NB)
                    pool.wait_ge(w_out, 16 * NB)

                @block.tensor
                def _(pe):
                    pe.wait_ge(ld_x, 16)
                    pe.wait_ge(ld_att, 16 * 8)
                    for i in range(2):
                        for c in range(NCH):
                            pe.matmul(ps[:, 4 + 2 * i + c, :], wqkv[:, i, :], X[:, c * CH:(c + 1) * CH],
                                      start=True, stop=True).then_inc(g_qk, 1)
                    for t in range(8):
                        last = pe.matmul(ps[:, 2 + t // 4, (t % 4) * C:(t % 4 + 1) * C],
                                         X[:, t * 128:(t + 1) * 128], wqkv[:, 2, :], start=True, stop=True)
                        if t % 4 == 3:
                            last.then_inc(g_v, 1)
                    pe.wait_ge(ld_ctx, 16 * (5 + NB))

                    def piece(j):
                        if j >= 2:
                            pe.wait_ge(j_rem if j < NPC + 2 else j_full, j - 1 if j < NPC + 2 else j - 1 - NPC)
                        kind, i, c0, w = pieces[j]
                        if kind == "kc":
                            pe.matmul(ps[:, j % 2, 0:w], wck[:], ctx_t[0:CC + 1, i, c0:c0 + w],
                                      start=True, stop=True).then_inc(j_ps, 1)
                        else:
                            pe.matmul(ps[:, j % 2, 0:w], wx[:, i, :], X[:, c0:c0 + w],
                                      start=True, stop=True).then_inc(j_ps, 1)

                    def values(n):
                        b, t = n // NKT, n % NKT
                        k = 128 if t < NKT - 1 else KLAST
                        if n < 2:
                            pe.wait_ge(g_v_sb, n + 1)
                        else:
                            pe.wait_ge(v_sb, n - 1)
                        pe.matmul(ps[0:k, 2 + n % 2, 0:H * VW], ctx_t[0:CC + 1, b, t * 128:t * 128 + k], wcv[:],
                                  start=True, stop=True).then_inc(v_ps, 1)

                    pe.wait_ge(g_sq, 4)
                    for t in range(8):
                        last = pe.matmul(ps[:, 4, t:t + 1], ksq[:, t * 128:(t + 1) * 128], neg_col[:, 0:1],
                                         start=True, stop=True)
                    last.then_inc(g_ksum, 1)
                    for b in range(NB):
                        q = slice(b * TQ, (b + 1) * TQ)
                        if b >= 2:
                            pe.wait_ge(g_e1, 2 * (b - 1))
                        for t in range(2):
                            o = ps[:, 5 + b % 2, t * TQ:(t + 1) * TQ]
                            pe.matmul(o, kt[:, b * TQ + t * 128:b * TQ + (t + 1) * 128], qt[:, q],
                                      start=True, stop=False)
                            last = pe.matmul(o, half_neg[:], qsq[:, q], start=False, stop=True)
                        last.then_inc(g_s, 1)
                        for n in range(b * NKT, (b + 1) * NKT):
                            values(n)
                        for j in range(4 * b, 4 * b + 4):
                            piece(j)
                        pe.wait_ge(g_p, b + 1)
                        if b == 0:
                            pe.wait_ge(g_v_sb, 2)
                        if b >= 1:
                            pe.wait_ge(g_ot, b)
                            pe.wait_ge(g_lden, b)
                        for t in range(2):
                            pe.matmul(ps[:, 7, 0:TQ], v0[:, 2 * b + t, :], p0[:, b % 2, t * TQ:(t + 1) * TQ],
                                      start=(t == 0), stop=(t == 1))
                        for t in range(2):
                            last = pe.matmul(ps[:, 7, TQ:2 * TQ], ones[:], p0[:, b % 2, t * TQ:(t + 1) * TQ],
                                             start=(t == 0), stop=(t == 1))
                        last.then_inc(g_o, 1)
                        pe.wait_ge(g_ot, b + 1)
                        if b == 0:
                            pe.wait_ge(g_ksum_sb, 1)
                        if b == 2:
                            pe.wait_ge(g_r, 1)
                        pe.matmul(ps[:, 4, (b % 2) * TQ:(b % 2 + 1) * TQ], wqkv[:, 3, :], ot[:, b % 2, :],
                                  start=True, stop=True).then_inc(g_wo, 1)
                    pe.wait_ge(g_r, 2)
                    pe_ln(0)
                    pe_ln(1)
                    pe_ln2(0)
                    pe_ln2(1)
                    for c in range(NCH):
                        pe.wait_ge(x_ready, c + 1)
                    for j in range(NPC, NPX):
                        piece(j)
                    for t in range(8):
                        if t < 2:
                            pe.wait_ge(v_sb, NB * NKT - 1 + t)
                        else:
                            pe.wait_ge(w_sb, t - 1)
                        pe.matmul(ps[:, 2 + t % 2, 0:H * VW], X[:, t * 128:(t + 1) * 128], wv_pad[:],
                                  start=True, stop=True).then_inc(w_ps, 1)

                @block.scalar
                def _(act):
                    act.wait_ge(ld_att, 16 * 8)
                    for i in range(4):
                        act.wait_ge(g_qk, i + 1)
                        dst, c = (qt, kt)[i // 2], i % 2
                        act.activation(dst[:, c * CH:(c + 1) * CH], ps[:, 4 + i, :], ACT.Identity,
                                       bias=col[("bq0", "bk0")[i // 2]]).then_inc(g_qk_sb, 1)
                    for i in range(4):
                        act.wait_ge(g_qk_sb, i + 1)
                        src, dst, c = (qt, kt)[i // 2], (qsq, ksq)[i // 2], i % 2
                        act.activation(dst[:, c * CH:(c + 1) * CH], src[:, c * CH:(c + 1) * CH],
                                       ACT.Square).then_inc(g_sq, 1)

                    def hi_mid(j):
                        w = pieces[j][3]
                        act.wait_ge(j_ps, j + 1)
                        if j >= 2:
                            act.wait_ge(j_out[j % 2], 96 * (j // 2))
                        if pieces[j][0] == "kc":
                            act.activation(hi[:, j % 2, 0:w], ps[:, j % 2, 0:w], ACT.Copy).then_inc(j_hi, 1)
                        else:
                            act.activation(full[:, j % 2, 0:w], ps[:, j % 2, 0:w], ACT.Identity,
                                           bias=col[("bks", "bqs", "bqc")[pieces[j][1]]]).then_inc(j_full, 1)
                            act.wait_ge(j_full, j - NPC + 1)
                            act.activation(hi[:, j % 2, 0:w], full[:, j % 2, 0:w], ACT.Copy).then_inc(j_hi, 1)
                        act.wait_ge(j_rem, j + 1)
                        act.activation(mid[:, j % 2, 0:w], rem[:, j % 2, 0:w], ACT.Copy).then_inc(j_mid, 1)

                    def values(n):
                        b, t = n // NKT, n % NKT
                        k = 128 if t < NKT - 1 else KLAST
                        act.wait_ge(v_ps, n + 1)
                        if n == 0:
                            act.wait_ge(cleared, 1)
                        if t == 0 and b:
                            act.wait_ge(v_out, 16 * b)
                        act.activation(vst[0:k, :, t, :], ps[0:k, 2 + n % 2, 0:H * VW].rearrange(
                            "p (g n) -> p g n", g=NG), ACT.Copy).then_inc(v_sb, 1)

                    for b in range(NB):
                        act.wait_ge(g_s, b + 1)
                        if b == 0:
                            act.wait_ge(g_ksum_sb, 1)
                        for t in range(2):
                            act.activation(e1[:, b % 2, t * TQ:(t + 1) * TQ], ps[:, 5 + b % 2, t * TQ:(t + 1) * TQ],
                                           ACT.Exp, bias=ksum[:, 2 * b + t:2 * b + t + 1], scale=2.0).then_inc(g_e1, 1)
                        act.wait_ge(g_e1, 2 * (b + 1))
                        act.activation(p0[:, b % 2, :], e1[:, b % 2, :], ACT.Exp).then_inc(g_p, 1)
                        for n in range(b * NKT, (b + 1) * NKT):
                            values(n)
                        for j in range(4 * b, 4 * b + 4):
                            hi_mid(j)
                        act.wait_ge(g_o, b + 1)
                        act.activation(lden[:, b % 2, :], ps[:, 7, TQ:2 * TQ], ACT.Ln).then_inc(g_lden, 1)
                        act.wait_ge(g_lden, b + 1)
                        act.activation(rden[:, b % 2, :], lden[:, b % 2, :], ACT.Exp, scale=-1.0).then_inc(g_rden, 1)
                    act_ln(0)
                    act_ln(1)
                    act_ln2(0)
                    act_ln2(1)
                    for j in range(NPC, NPX):
                        hi_mid(j)

                @block.vector
                def _(dve):
                    dve.wait_ge(ld_att, 16 * 8)
                    for i in range(2):
                        dve.wait_ge(g_v, i + 1)
                        for t in range(4):
                            last = dve.tensor_tensor(v0[:, 4 * i + t, :], ps[:, 2 + i, t * C:(t + 1) * C], bv0[:],
                                                     ALU.add)
                        last.then_inc(g_v_sb, 1)
                    dve.wait_ge(g_ksum, 1)
                    dve.tensor_copy(ksum[:], ps[:, 4, 0:8]).then_inc(g_ksum_sb, 1)

                    def split(j):
                        w = pieces[j][3]
                        s = (slice(None), j % 2, slice(0, w))
                        whole = ps[s] if pieces[j][0] == "kc" else full[s]
                        dve.wait_ge(j_hi, j + 1)
                        if j >= 2:
                            dve.wait_ge(j_mid, j - 1)
                        dve.tensor_tensor(rem[s], whole, hi[s], ALU.subtract).then_inc(j_rem, 1)
                        dve.wait_ge(j_mid, j + 1)
                        dve.tensor_tensor(low[s], rem[s], mid[s], ALU.subtract).then_inc(j_low, 1)

                    for b in range(NB):
                        for j in range(4 * b, 4 * b + 4):
                            split(j)
                        dve.wait_ge(g_rden, b + 1)
                        if b >= 2:
                            dve.wait_ge(g_wo, b - 1)
                        dve.tensor_tensor(ot[:, b % 2, :], ps[:, 7, 0:TQ], rden[:, b % 2, :],
                                          ALU.mult).then_inc(g_ot, 1)
                        if b % 2 == 1:
                            c = b // 2
                            dve.wait_ge(g_wo, b + 1)
                            dve.scalar_tensor_tensor(out=R[:, c * CH:(c + 1) * CH], in0=ps[:, 4, :],
                                                     scalar=col["bo0"], in1=X[:, c * CH:(c + 1) * CH],
                                                     op0=ALU.add, op1=ALU.add).then_inc(g_r, 1)
                    dve_ln(0)
                    dve_ln(1)
                    for j in range(NPC, NPX):
                        split(j)
                    for t in range(8):
                        dve.wait_ge(w_ps, t + 1)
                        dve.tensor_tensor(vss[:, t // 2, :, t % 2, :],
                                          ps[:, 2 + t % 2, 0:H * VW].rearrange("p (g n) -> p g n", g=NG),
                                          bv_pad[:].rearrange("p (g n) -> p g n", g=NG), ALU.add).then_inc(w_sb, 1)

        sem_owner[0] = persistent
        o_all = keep("o_all", [128, NU, 2 * TQ])
        with ExitStack() as st:
            def sb(name, shape, dt=F32):
                return st.enter_context(nc.sbuf_tensor(name, shape, dt))

            kc = [sb(f"kc{s}", [128, 2, TK], BF16) for s in range(SLOTS)]
            ks = [sb(f"ks{s}", [128, 2, TQ], BF16) for s in range(SLOTS)]
            qq = [sb(f"qq{s}", [128, 2, 2, TQ], BF16) for s in range(SLOTS)]
            vv = [sb(f"vv{s}", [128, NST, 64]) for s in range(SLOTS)]
            prob = sb("prob", [128, 3, 4, TQ])
            nm_a = sb("nm_a", [128, 8])
            nm_b = sb("nm_b", [128, 8])
            nm = sb("nm", [128, 16])
            mrow = [sb(f"mrow{s}", [16, 2, 128], BF16) for s in range(SLOTS)]
            ident = sb("ident", [128, 128])
            ident_b = sb("ident_b", [128, 128], BF16)
            mask_kq = sb("mask_kq", [128, 128], BF16)
            mask_qk = sb("mask_qk", [128, 128], BF16)
            masks_f = sb("masks_f", [128, 2, 128])
            s1 = st.enter_context(nc.psum_tensor("s1", [128, 4, 512], F32))
            s2 = st.enter_context(nc.psum_tensor("s2", [128, 3, 512], F32))
            o_ps = st.enter_context(nc.psum_tensor("o_ps", [128, 2 * TQ], F32))
            (consts, consts_b, filled, s1_ready, s1_read, nm_ready, nm_t, m1_done, mrow_ready, s2_ready, exp_done, av_done,
             o_copied) = sems(st, "consts", "consts_b", "filled", "s1_ready", "s1_read", "nm_ready", "nm_t", "m1_done",
                              "mrow_ready", "s2_ready", "exp_done", "av_done", "o_copied")
            slot_in = sems(st, *[f"slot_in{s}" for s in range(SLOTS)])
            max_in = sems(st, *[f"max_in{s}" for s in range(SLOTS)])
            SLOT_INC = 16 * 10
            MAX_INC = 16 * 8
            HALVES = 2 * NST
            JOBS = 16
            S2_FREE, P_FREE, S1_FREE = 3, 3, 2
            head = [(hh % 2, hh // 2) for hh in range(4)]

            with nc.Block() as block:
                @block.gpsimd
                def _(pool):
                    for s in range(SLOTS):
                        pool.memset(kc[s][:], 1.0)
                        last = pool.memset(ks[s][:], 1.0)
                    last.then_inc(filled, 1)
                    pool.wait_ge(consts, 16 * 2)
                    for dst, src in ((ident_b, ident[:]), (mask_kq, masks_f[:, 0, :]), (mask_qk, masks_f[:, 1, :])):
                        pool.tensor_copy(dst[:], src).then_inc(consts_b, 1)
                    for done in first_named:
                        pool.sem_clear(done)

                @block.sync
                def _(sp):
                    for dst, src in ((ident, "ident"), (masks_f, "masks")):
                        sp.dma_start(dst[:], a[src]).then_inc(consts, 16)
                    sp.wait_ge(filled, 1)

                    pairs = {n: scr.rearrange("b g r c t -> (b g) r c t") for n, scr in (("kc", kc_scr), *xs_scr.items())}
                    values_c, values_s = (v.rearrange("b g p n -> (b g) p n") for v in (vc_scr, vs_scr))

                    def rows(name, at):
                        return pairs[name][bass.ds(at, 1)].rearrange("o r c t -> (o r c) t").rearrange(
                            "(q j) t -> q j t", j=2)

                    def load(n, s):
                        for e in range(2):
                            r0 = 64 * e
                            for dst, src in ((kc[s][r0:r0 + ROWS, :, :], "kc"), (ks[s][r0:r0 + ROWS, :, :], "ks"),
                                             (qq[s][r0:r0 + ROWS, 0, :, :], "qc"), (qq[s][r0:r0 + ROWS, 1, :, :], "qs")):
                                sp.dma_start(dst, rows(src, n * 2 + e)).then_inc(slot_in[s], 16)
                        for t0, t1, src in ((0, NKT, values_c), (NKT, NST, values_s)):
                            sp.dma_start(vv[s][:, t0:t1, :].rearrange("p t n -> p (t n)"),
                                         src[bass.ds(n, 1)].rearrange("o p n -> (o p) n")).then_inc(slot_in[s], 16)

                    def max_rows(s):
                        for kind in range(2):
                            for e in range(2):
                                for part in range(2):
                                    r0 = 8 * kind + 4 * e
                                    p0_ = 64 * e + ROWS + part
                                    sp.dma_start(qq[s][p0_:p0_ + 1, kind, :, :].rearrange("o j (t q) -> o (j t) q", t=2),
                                                 mrow[s][r0:r0 + 4, part, :]).then_inc(max_in[s], 16)

                    def step(i, u):
                        sp.wait_ge(av_done, i * (3 * NST) + (P_FREE + NST * u))
                        load(i * 3 + (u + 2), (u + 2) % SLOTS)
                        sp.wait_ge(mrow_ready, i * 3 + (u + 2))
                        max_rows((u + 1) % SLOTS)

                    load(0, 0)
                    load(1, 1)
                    sp.wait_ge(mrow_ready, 1)
                    max_rows(0)
                    with sp.Fori(0, 4) as i:
                        for u in range(3):
                            step(i, u)
                    step(4, 0)
                    step(4, 1)
                    sp.wait_ge(mrow_ready, NU)
                    max_rows((NU - 1) % SLOTS)

                @block.tensor
                def _(pe):
                    pe.sem_inc(av_done, P_FREE)
                    pe.wait_ge(consts, 16 * 2)
                    pe.wait_ge(consts_b, 3)

                    def score_half(s, k, base):
                        hh, t = k // 4, (k // 2) % 2
                        j, e = head[hh]
                        r0 = 64 * e
                        pe.wait_ge(s1_read, base[0] + (base[1] + k + 1))
                        q = qq[s][r0:r0 + ROWS, 0, j, t * 128:(t + 1) * 128]
                        if k % 2 == 0:
                            for i in range(2):
                                last = pe.matmul(s1[:, i, :], q, kc[s][r0:r0 + ROWS, j, i * 512:(i + 1) * 512],
                                                 start=True, stop=True)
                        else:
                            pe.matmul(s1[:, 2, :], q, kc[s][r0:r0 + ROWS, j, 1024:1536], start=True, stop=True)
                            pe.matmul(s1[:, 3, 0:TK - 1536], q, kc[s][r0:r0 + ROWS, j, 1536:TK], start=True, stop=True)
                            qs_ = qq[s][r0:r0 + ROWS, 1, j, t * 128:(t + 1) * 128]
                            w = 128 * (t + 1)
                            pe.matmul(s1[:, 3, 128:128 + w], qs_, ks[s][r0:r0 + ROWS, j, 0:w], start=True, stop=False)
                            last = pe.matmul(s1[:, 3, w:w + 128], ident_b[:], mask_qk[:], start=False, stop=True)
                        last.then_inc(s1_ready, 1)

                    def scores_t(s, t, half, base):
                        k = 2 * t + half
                        pe.wait_ge(exp_done, base[0] + (base[1] + k + 1))
                        bank = k % 3
                        for i in range(2):
                            j, e = head[2 * half + i]
                            r0 = 64 * e
                            if t < NKT:
                                m = 128 if t < NKT - 1 else KLAST
                                last = pe.matmul(s2[0:m, bank, i * TQ:(i + 1) * TQ],
                                                 kc[s][r0:r0 + KROWS, j, t * 128:t * 128 + m],
                                                 qq[s][r0:r0 + KROWS, 0, j, :], start=True, stop=True)
                            else:
                                q0 = 128 * (t - NKT)
                                w = TQ - q0
                                pe.matmul(s2[:, bank, i * w:(i + 1) * w], ks[s][r0:r0 + KROWS, j, q0:q0 + 128],
                                          qq[s][r0:r0 + KROWS, 1, j, q0:TQ], start=True, stop=False)
                                last = pe.matmul(s2[:, bank, i * w:i * w + 128], ident_b[:], mask_kq[:],
                                                 start=False, stop=True)
                        last.then_inc(s2_ready, 1)

                    def outputs(s, t, base):
                        pe.wait_ge(exp_done, base[0] + (base[1] + S2_FREE + 2 * t + 2))
                        k = KLAST if t == NKT - 1 else 128
                        kind, q0 = (0, 0) if t < NKT else (1, 128 * (t - NKT))
                        for hh in range(4):
                            last = pe.matmul(o_ps[32 * hh:32 * hh + VW, kind * TQ + q0:(kind + 1) * TQ],
                                             vv[s][0:k, t, hh * VW:(hh + 1) * VW],
                                             prob[0:k, t % 3, hh, q0:TQ],
                                             start=t in (0, NKT), stop=t in (NKT - 1, NST - 1))
                        last.then_inc(av_done, 1)

                    def unit(i, u, last_unit=False):
                        nxt = (u + 1) % SLOTS
                        pe.wait_ge(max_in[u], i * MAX_INC + MAX_INC)
                        s2_base = (i * (3 * HALVES), u * HALVES)
                        s1_base = (i * (3 * JOBS), (u + 1) * JOBS)
                        scores_t(u, 0, 0, s2_base)
                        scores_t(u, 0, 1, s2_base)
                        if not last_unit:
                            pe.wait_ge(slot_in[nxt], i * SLOT_INC + SLOT_INC * (2 if nxt == 0 else 1))
                        k = 0
                        for t in range(NST):
                            if t + 1 < NST:
                                scores_t(u, t + 1, 0, s2_base)
                            if not last_unit and k < JOBS:
                                score_half(nxt, k, s1_base)
                                k += 1
                            if t + 1 < NST:
                                scores_t(u, t + 1, 1, s2_base)
                            if t == 0:
                                pe.wait_ge(o_copied, i * 3 + (u + 1))
                            outputs(u, t, s2_base)
                            if not last_unit and t < 4 and k < JOBS:
                                score_half(nxt, k, s1_base)
                                k += 1
                            if not last_unit and k == JOBS:
                                k += 1
                                turn_maxima(i * 3 + (u + 2))

                    def turn_maxima(count):
                        pe.wait_ge(nm_ready, count)
                        pe.transpose(s1[0:16, 3, 384:512], nm[:], ident[:]).then_inc(nm_t, 1)

                    pe.wait_ge(slot_in[0], SLOT_INC)
                    for k in range(JOBS):
                        score_half(0, k, (0, 0))
                    turn_maxima(1)
                    with pe.Fori(0, NU // SLOTS) as i:
                        for u in range(SLOTS):
                            unit(i, u)
                    unit(NU // SLOTS, 0, last_unit=True)

                @block.scalar
                def _(act):
                    act.sem_inc(exp_done, S2_FREE)

                    def unit(i, u):
                        for k in range(HALVES):
                            t, half = k // 2, k % 2
                            if half == 0:
                                act.wait_ge(av_done, i * (3 * NST) + (u * NST + t + 1))
                            act.wait_ge(s2_ready, i * (3 * HALVES) + (u * HALVES + k + 1))
                            p = KLAST if t == NKT - 1 else 128
                            q0 = 0 if t < NKT else 128 * (t - NKT)
                            w = TQ - q0
                            act.activation(prob[0:p, t % 3, 2 * half:2 * half + 2, q0:TQ],
                                           s2[0:p, k % 3, 0:2 * w].rearrange("p (i q) -> p i q", i=2),
                                           ACT.Exp, scale=SCALE).then_inc(exp_done, 1)
                        act.wait_ge(av_done, i * (3 * NST) + (P_FREE + (u + 1) * NST))
                        act.activation(o_all[:, bass.ds(i * 3 + u, 1), :].rearrange("p o q -> p (o q)"), o_ps[:],
                                       ACT.Copy).then_inc(o_copied, 1)

                    with act.Fori(0, NU // SLOTS) as i:
                        for u in range(SLOTS):
                            unit(i, u)
                    unit(NU // SLOTS, 0)

                @block.vector
                def _(dve):
                    dve.memset(o_ps[:], 0.0).then_inc(o_copied, 1)
                    dve.sem_inc(s1_read, S1_FREE)

                    def unit(i3, u):
                        for k in range(JOBS):
                            hh, t = k // 4, (k // 2) % 2
                            j, e = head[hh]
                            i = 4 * e + 2 * j + t
                            dve.wait_ge(s1_ready, i3 * (3 * JOBS) + (u * JOBS + k + 1))
                            if k % 2 == 0:
                                dve.tensor_reduce(nm_a[:, i:i + 1], s1[:, 0:2, :], AX.XY, ALU.max,
                                                  negate=True).then_inc(s1_read, 1)
                            else:
                                dve.tensor_reduce(nm_b[:, i:i + 1],
                                                  s1[:, 2:4, :].rearrange("p b n -> p (b n)")[:, 0:TK - 1024],
                                                  AX.X, ALU.max, negate=True)
                                dve.tensor_reduce(nm[:, 8 + i:9 + i], s1[:, 3, 128:128 + 128 * (t + 1)], AX.X,
                                                  ALU.max, negate=True).then_inc(s1_read, 1)
                        dve.wait_ge(s1_read, i3 * (3 * JOBS) + (S1_FREE + (u + 1) * JOBS))
                        dve.tensor_tensor(nm[:, 0:8], nm_a[:], nm_b[:], ALU.min).then_inc(nm_ready, 1)
                        dve.wait_ge(nm_t, i3 * 3 + (u + 1))
                        dve.tensor_copy(mrow[u][:, 0, :], s1[0:16, 3, 384:512]).then_inc(m1_done, 1)
                        dve.wait_ge(m1_done, i3 * 3 + (u + 1))
                        dve.tensor_tensor(mrow[u][:, 1, :], s1[0:16, 3, 384:512], mrow[u][:, 0, :],
                                          ALU.subtract).then_inc(mrow_ready, 1)

                    with dve.Fori(0, NU // SLOTS) as i3:
                        for u in range(SLOTS):
                            unit(i3, u)
                    unit(NU // SLOTS, 0)

        first_sems.close()
        emit_rest(nc, a, out, keep, sems, ln_parts, X, R, ctx_t, col, o_all, comb_scr)


def emit_rest(nc, a, out, keep, sems, ln_parts, X, R, ctx_t, col, o_all, comb_scr):
    with ExitStack() as st:
        def sb(name, shape, dt=F32):
            return st.enter_context(nc.sbuf_tensor(name, shape, dt))

        spread = sb("spread", [128, 128])
        wp = sb("wp", [128, NG, C])
        wg = sb("wg", [C, E])
        ident = sb("ident3", [128, 128])
        iota = sb("iota", [128, 8 * E])
        lden = sb("lden3", [128, 2, 512])
        rden = sb("rden3", [128, 2, 512])
        y2 = sb("y2", [128, 2, 512])
        y = sb("y", [128, 4, TQ])
        gout = sb("gout", [128, 8, E])
        top = sb("top", [128, 8, 8])
        idx = sb("idx", [128, 8, 8], U32)
        idxf = sb("idxf", [128, 8, 8])
        w12 = sb("w12", [128, 8, 4])
        w2 = sb("w2", [128, 8, 1])
        c1 = sb("c1", [128, 8, E])
        c2 = sb("c2", [128, 8, E])
        comb = sb("comb", [128, 8, E])
        comb_t = sb("comb_t", [E, T])
        ps = st.enter_context(nc.psum_tensor("ps3", [128, 8, 512], F32))
        (ld, den, dlog, drec, y2s, ys, proj, r_ready, gates, chain, expd, combs, comb_ps, comb_sb, stored) = sems(
            st, "b3_ld", "den", "dlog", "drec", "y2s", "ys", "proj", "b3_r", "gates", "b3_chain", "expd", "combs",
            "comb_ps", "comb_sb", "stored")
        pe_ln, pe_ln2, act_ln, act_ln2, dve_ln, x_ready = ln_parts(st, "ln2", ps[:, 4:6, :], ps[:, 6:8, :], r_ready)

        with nc.Block() as block:
            @block.sync
            def _(sp):
                for dst, src in ((spread, "spread"), (wp, "wp"), (wg, "wg"), (ident, "ident"), (iota, "iota")):
                    sp.dma_start(dst[:], a[src]).then_inc(ld, 16)
                sp.wait_ge(comb_sb, 2)
                sp.dma_start(comb_scr, comb_t[:]).then_inc(stored, 16)
                sp.wait_ge(stored, 16)

            @block.tensor
            def _(pe):
                pe.wait_ge(ld, 16 * 5)

                def denominators(n):
                    if n >= 2:
                        pe.wait_ge(dlog, n - 1)
                    pe.matmul(ps[:, n % 2, :], spread[:], o_all[:, n, :], start=True, stop=True).then_inc(den, 1)

                denominators(0)
                denominators(1)
                for n in range(NU):
                    b, g = n // NG, n % NG
                    if n + 2 < NU:
                        denominators(n + 2)
                    pe.wait_ge(ys, n + 1)
                    last = pe.matmul(ps[:, 2 + b // 2, (b % 2) * TQ:(b % 2 + 1) * TQ], wp[:, g, :], y[:, n % 4, :],
                                     start=(g == 0), stop=(g == NG - 1))
                    last.then_inc(proj, 1)
                pe_ln(0)
                pe_ln(1)
                pe_ln2(0)
                pe_ln2(1)
                for t in range(8):
                    if t % 4 == 0:
                        pe.wait_ge(x_ready, t // 4 + 1)
                    last = pe.matmul(ps[:, 0, t * E:(t + 1) * E], X[:, t * 128:(t + 1) * 128], wg[:],
                                     start=True, stop=True)
                last.then_inc(gates, 1)
                pe.wait_ge(combs, 1)
                for t in range(8):
                    last = pe.transpose(ps[0:E, 2 + t // 4, (t % 4) * 128:(t % 4 + 1) * 128], comb[:, t, :], ident[:])
                    if t % 4 == 3:
                        last.then_inc(comb_ps, 1)

            @block.scalar
            def _(act):
                for n in range(NU):
                    act.wait_ge(den, n + 1)
                    act.activation(lden[:, n % 2, :], ps[:, n % 2, :], ACT.Ln).then_inc(dlog, 1)
                    act.wait_ge(dlog, n + 1)
                    if n >= 2:
                        act.wait_ge(y2s, n - 1)
                    act.activation(rden[:, n % 2, :], lden[:, n % 2, :], ACT.Exp, scale=-1.0).then_inc(drec, 1)
                act_ln(0)
                act_ln(1)
                act_ln2(0)
                act_ln2(1)
                act.wait_ge(chain, 18)
                act.activation(w12[:, :, 1:2], w12[:, :, 0:1], ACT.Exp).then_inc(expd, 1)

            @block.vector
            def _(dve):
                for n in range(NU):
                    dve.wait_ge(drec, n + 1)
                    dve.tensor_tensor(y2[:, n % 2, :], o_all[:, n, :], rden[:, n % 2, :], ALU.mult).then_inc(y2s, 1)
                    dve.wait_ge(y2s, n + 1)
                    if n >= 4:
                        dve.wait_ge(proj, n - 3)
                    dve.tensor_tensor(y[:, n % 4, :], y2[:, n % 2, 0:TQ], y2[:, n % 2, TQ:2 * TQ],
                                      ALU.add).then_inc(ys, 1)
                    if n % 8 == 7:
                        c = n // 8
                        dve.wait_ge(proj, n + 1)
                        dve.scalar_tensor_tensor(out=R[:, c * CH:(c + 1) * CH], in0=ps[:, 2 + c, :], scalar=col["bp"],
                                                 in1=X[:, c * CH:(c + 1) * CH], op0=ALU.add,
                                                 op1=ALU.add).then_inc(r_ready, 1)
                dve_ln(0)
                dve_ln(1)
                count = [0]

                def link(ins):
                    count[0] += 1
                    ins.then_inc(chain, 1)
                    dve.wait_ge(chain, count[0])

                dve.wait_ge(gates, 1)
                link(dve.tensor_copy(gout[:].rearrange("p t e -> p (t e)"), ps[:, 0, 0:8 * E]))
                for t in range(8):
                    link(dve.max(top[:, t, :], gout[:, t, :]))
                for t in range(8):
                    link(dve.max_index(idx[:, t, :], top[:, t, :], gout[:, t, :]))
                link(dve.tensor_tensor(w12[:, :, 0:1], top[:, :, 1:2], top[:, :, 0:1], ALU.subtract))
                link(dve.tensor_copy(idxf[:], idx[:]))
                link(dve.tensor_tensor(c1[:], iota[:].rearrange("p (t e) -> p t e", t=8),
                                       idxf[:, :, 0:1].to_broadcast([128, 8, E]), ALU.is_equal))
                link(dve.tensor_tensor(c2[:], iota[:].rearrange("p (t e) -> p t e", t=8),
                                       idxf[:, :, 1:2].to_broadcast([128, 8, E]), ALU.is_equal))
                dve.wait_ge(expd, 1)
                link(dve.tensor_scalar(w12[:, :, 2:3], w12[:, :, 1:2], 1.0, None, ALU.add))
                link(dve.reciprocal(w12[:, :, 3:4], w12[:, :, 2:3]))
                link(dve.tensor_tensor(w2[:], w12[:, :, 1:2], w12[:, :, 3:4], ALU.mult))
                link(dve.tensor_tensor(c1[:], c1[:], w12[:, :, 3:4].to_broadcast([128, 8, E]), ALU.mult))
                link(dve.tensor_tensor(c2[:], c2[:], w2[:].to_broadcast([128, 8, E]), ALU.mult))
                dve.tensor_tensor(comb[:], c1[:], c2[:], ALU.add).then_inc(combs, 1)
                for c in range(NCH):
                    dve.wait_ge(comb_ps, c + 1)
                    dve.tensor_copy(comb_t[:, c * CH:(c + 1) * CH], ps[0:E, 2 + c, :]).then_inc(comb_sb, 1)

    with ExitStack() as st:
        def sb(name, shape, dt=F32):
            return st.enter_context(nc.sbuf_tensor(name, shape, dt))

        NF = DFF // 128
        WCOLS = 3 * DFF + 2 * NF
        wexp = [sb(f"wexp{s}", [128, WCOLS]) for s in range(2)]
        comb_bc = [sb(f"comb_bc{s}", [128, T]) for s in range(2)]
        b3 = sb("b3", [E, C])
        comb_r = sb("comb_r", [E, T])
        sg = sb("sg", [128, 2, CH])
        hv = sb("hv", [128, 2, CH])
        hh = sb("hh", [128, 4, CH])
        ps = st.enter_context(nc.psum_tensor("ps4", [128, 8, 512], F32))
        exp_in = sems(st, "exp_in0", "exp_in1")
        (ld, gv_ready, sg_done, hv_done, h_done, w3_done, out_done, r_ready) = sems(
            st, "b4_ld", "gv_ready", "sg_done", "hv_done", "h_done", "w3_done", "moe_out", "b4_r")
        pe_ln, pe_ln2, act_ln, act_ln2, dve_ln, x_ready = ln_parts(st, "ln3", ps[:, 0:2, :], ps[:, 2:4, :], r_ready)
        GV_FREE, H_FREE = 2, 4
        tiles = [(f, c) for f in range(NF) for c in range(NCH)]
        NT = len(tiles)

        with nc.Block() as block:
            @block.sync
            def _(sp):
                sp.dma_start(b3[:], a["b3"]).then_inc(ld, 16)
                sp.dma_start(comb_r[:], comb_scr).then_inc(ld, 16)

                def load(e, s):
                    sp.dma_start(wexp[s][:], a["wexp"][bass.ds(e, 1)].rearrange("o p n -> (o p) n")).then_inc(exp_in[s], 16)
                    sp.dma_start(comb_bc[s][:], comb_scr[bass.ds(e, 1), :].to_broadcast([128, T])).then_inc(exp_in[s], 16)

                load(0, 0)
                load(1, 1)
                with sp.Fori(1, E // 2) as i:
                    for s in range(2):
                        sp.wait_ge(w3_done, i * (2 * NT) + (H_FREE + (s - 1) * NT))
                        load(i * 2 + s, s)

            @block.tensor
            def _(pe):
                pe.sem_inc(w3_done, H_FREE)
                pe.wait_ge(ld, 32)
                for c in range(NCH):
                    pe.matmul(ps[:, 4 + c, :], b3[:], comb_r[:, c * CH:(c + 1) * CH], start=True, stop=False,
                              skip_group_check=True)

                def up(i, s, k):
                    f, c = tiles[k]
                    done = i * (2 * NT) + (s * NT + k + 1)
                    pe.wait_ge(sg_done, done)
                    pe.wait_ge(hv_done, done)
                    for m in range(2):
                        last = pe.matmul(ps[:, 2 * m + k % 2, :], wexp[s][:, m * DFF + f * 128:m * DFF + (f + 1) * 128],
                                         X[:, c * CH:(c + 1) * CH], start=True, stop=True)
                    last.then_inc(gv_ready, 1)

                def down(i, s, k):
                    f, c = tiles[k]
                    pe.wait_ge(h_done, i * (2 * NT) + (s * NT + k + 1))
                    pe.matmul(ps[:, 4 + c, :], wexp[s][:, 2 * DFF + f * 128:2 * DFF + (f + 1) * 128], hh[:, k, :],
                              start=False, stop=False, skip_group_check=True).then_inc(w3_done, 1)

                def expert(i, s, before):
                    up(i, s, 0)
                    before()
                    up(i, s, 1)
                    up(i, s, 2)
                    down(i, s, 0)
                    up(i, s, 3)
                    down(i, s, 1)
                    down(i, s, 2)

                pe.wait_ge(exp_in[0], 32)
                expert(0, 0, lambda: None)
                pe.wait_ge(exp_in[1], 32)
                expert(0, 1, lambda: down(0, 0, 3))
                with pe.Fori(1, E // 2) as i:
                    pe.wait_ge(exp_in[0], i * 32 + 32)
                    expert(i, 0, lambda: down(i - 1, 1, 3))
                    pe.wait_ge(exp_in[1], i * 32 + 32)
                    expert(i, 1, lambda: down(i, 0, 3))
                down(E // 2 - 1, 1, 3)
                pe.wait_ge(r_ready, 2)
                pe_ln(0)
                pe_ln(1)
                pe_ln2(0)
                pe_ln2(1)

            @block.scalar
            def _(act):
                act.sem_inc(sg_done, GV_FREE)
                with act.Fori(0, E // 2) as i:
                    for s in range(2):
                        act.wait_ge(exp_in[s], i * 32 + 32)
                        for k, (f, c) in enumerate(tiles):
                            act.wait_ge(gv_ready, i * (2 * NT) + (s * NT + k + 1))
                            act.wait_ge(hv_done, i * (2 * NT) + (s * NT + k + 1))
                            act.activation(sg[:, k % 2, :], ps[:, k % 2, :], ACT.Silu,
                                           bias=wexp[s][:, 3 * DFF + f:3 * DFF + f + 1]).then_inc(sg_done, 1)
                act_ln(0)
                act_ln(1)
                act_ln2(0)
                act_ln2(1)

            @block.vector
            def _(dve):
                dve.sem_inc(hv_done, GV_FREE)
                with dve.Fori(0, E // 2) as i:
                    for s in range(2):
                        dve.wait_ge(exp_in[s], i * 32 + 32)
                        for k, (f, c) in enumerate(tiles):
                            n = i * (2 * NT)
                            dve.wait_ge(sg_done, n + (GV_FREE + s * NT + k + 1))
                            dve.scalar_tensor_tensor(out=hv[:, k % 2, :], in0=ps[:, 2 + k % 2, :],
                                                     scalar=wexp[s][:, 3 * DFF + NF + f:3 * DFF + NF + f + 1],
                                                     in1=sg[:, k % 2, :], op0=ALU.add, op1=ALU.mult).then_inc(hv_done, 1)
                            dve.wait_ge(hv_done, n + (GV_FREE + s * NT + k + 1))
                            dve.wait_ge(w3_done, n + (s * NT + k + 1))
                            dve.tensor_tensor(hh[:, k, :], hv[:, k % 2, :], comb_bc[s][:, c * CH:(c + 1) * CH],
                                              ALU.mult).then_inc(h_done, 1)
                dve.wait_ge(w3_done, H_FREE + E * NT)
                for c in range(NCH):
                    dve.tensor_tensor(R[:, c * CH:(c + 1) * CH], ps[:, 4 + c, :], X[:, c * CH:(c + 1) * CH],
                                      ALU.add).then_inc(r_ready, 1)
                dve_ln(0)
                dve_ln(1)

    with ExitStack() as st:
        def sb(name, shape, dt=F32):
            return st.enter_context(nc.sbuf_tensor(name, shape, dt))

        win = sb("win", [C, 2, C])
        wgate = sb("wgate", [C, 2, 2, C])
        wout = sb("wout", [C, 2, C])
        carry = sb("carry", [C, T])
        names = ("xre", "xim", "gx", "ga", "mag", "nrm", "tau", "tk", "thi", "tlo", "chi", "clo", "s", "c", "sn", "cs",
                 "t1", "t2", "t3", "t4")
        v = {n: sb(f"r_{n}", [C, T]) for n in names}
        sp_ = sb("sp_", [C, 8])
        ps = st.enter_context(nc.psum_tensor("ps5", [128, 8, 512], F32))
        (ld, xh, xh_sb, gate_ps, gate_sb, spc, spd, mags, nrm_in, nrm_out, th_ready, trig, h_ready, y_ps, r_ready,
         chain, act_chain) = sems(st, "b5_ld", "xh", "xh_sb", "gate_ps", "gate_sb", "spc", "spd", "mags", "nrm_in",
                                  "nrm_out", "th_ready", "trig", "h_ready", "y_ps", "b5_r", "b5_chain", "b5_act")
        pe_ln, pe_ln2, act_ln, act_ln2, dve_ln, x_ready = ln_parts(st, "ln4", ps[:, 0:2, :], ps[:, 2:4, :], r_ready)

        with nc.Block() as block:
            @block.sync
            def _(sp):
                for dst, src in ((win, "win"), (wgate, "wgate"), (wout, "wout"), (carry, "carry")):
                    sp.dma_start(dst[:], a[src]).then_inc(ld, 16)

            @block.tensor
            def _(pe):
                pe.wait_ge(ld, 16 * 4)
                for c in range(NCH):
                    for i in range(2):
                        pe.matmul(ps[:, 2 * c + i, :], win[:, i, :], X[:, c * CH:(c + 1) * CH],
                                  start=True, stop=True).then_inc(xh, 1)
                for c in range(NCH):
                    pe.wait_ge(xh_sb, 2 * c + 2)
                    for i in range(2):
                        pe.matmul(ps[:, 4 + 2 * c + i, :], wgate[:, i, 0, :], v["xre"][:, c * CH:(c + 1) * CH],
                                  start=True, stop=False)
                        pe.matmul(ps[:, 4 + 2 * c + i, :], wgate[:, i, 1, :], v["xim"][:, c * CH:(c + 1) * CH],
                                  start=False, stop=True).then_inc(gate_ps, 1)
                for c in range(NCH):
                    pe.wait_ge(h_ready, c + 1)
                    pe.matmul(ps[:, 4 + c, :], wout[:, 0, :], v["t3"][:, c * CH:(c + 1) * CH], start=True, stop=False)
                    pe.matmul(ps[:, 4 + c, :], wout[:, 1, :], v["t4"][:, c * CH:(c + 1) * CH],
                              start=False, stop=True).then_inc(y_ps, 1)
                pe_ln(0)
                pe_ln(1)
                pe_ln2(0)
                pe_ln2(1)

            @block.scalar
            def _(act):
                act.activation(sp_[:, 0:1], col["a_real"], ACT.Abs).then_inc(act_chain, 1)
                act.wait_ge(act_chain, 1)
                act.activation(sp_[:, 1:2], sp_[:, 0:1], ACT.Exp, scale=-1.0).then_inc(act_chain, 1)
                act.wait_ge(act_chain, 2)
                act.activation(sp_[:, 2:3], sp_[:, 1:2], ACT.Ln, bias=col["one"]).then_inc(spc, 1)
                for c in range(NCH):
                    for i, (dst, b) in enumerate((("xre", "b_in0"), ("xim", "b_in1"))):
                        act.wait_ge(xh, 2 * c + i + 1)
                        act.activation(v[dst][:, c * CH:(c + 1) * CH], ps[:, 2 * c + i, :], ACT.Identity,
                                       bias=col[b]).then_inc(xh_sb, 1)
                for c in range(NCH):
                    for i, (dst, b) in enumerate((("gx", "bgx"), ("ga", "bga"))):
                        act.wait_ge(gate_ps, 2 * c + i + 1)
                        act.activation(v[dst][:, c * CH:(c + 1) * CH], ps[:, 4 + 2 * c + i, :], ACT.Sigmoid,
                                       bias=col[b]).then_inc(gate_sb, 1)
                act.wait_ge(spd, 1)
                for c in range(NCH):
                    s = slice(c * CH, (c + 1) * CH)
                    act.wait_ge(gate_sb, 2 * c + 2)
                    act.activation(v["nrm"][:, s], v["ga"][:, s], ACT.Exp, scale=sp_[:, 6:7]).then_inc(mags, 1)
                    act.activation(v["mag"][:, s], v["ga"][:, s], ACT.Exp, scale=sp_[:, 5:6]).then_inc(mags, 1)
                for c in range(NCH):
                    s = slice(c * CH, (c + 1) * CH)
                    act.wait_ge(nrm_in, c + 1)
                    act.activation(v["nrm"][:, s], v["nrm"][:, s], ACT.Sqrt).then_inc(nrm_out, 1)
                for c in range(NCH):
                    s = slice(c * CH, (c + 1) * CH)
                    act.wait_ge(th_ready, c + 1)
                    act.activation(v["tk"][:, s], v["tau"][:, s], ACT.Abs).then_inc(act_chain, 1)
                    act.activation(v["s"][:, s], v["tau"][:, s], ACT.Sin, scale=PI).then_inc(trig, 1)
                    act.wait_ge(act_chain, 3 + c)
                    act.activation(v["c"][:, s], v["tk"][:, s], ACT.Sin, scale=-PI, bias=col["half_pi"]).then_inc(trig, 1)
                act_ln(0)
                act_ln(1)
                act_ln2(0)
                act_ln2(1)

            @block.vector
            def _(dve):
                count = [0]

                def link(ins):
                    count[0] += 1
                    ins.then_inc(chain, 1)
                    dve.wait_ge(chain, count[0])

                dve.wait_ge(spc, 1)
                dve.wait_ge(ld, 16 * 4)
                link(dve.tensor_scalar(sp_[:, 3:4], col["a_real"], 0.0, None, ALU.max))
                link(dve.tensor_tensor(sp_[:, 4:5], sp_[:, 3:4], sp_[:, 2:3], ALU.add))
                link(dve.tensor_scalar(sp_[:, 5:6], sp_[:, 4:5], -8.0, None, ALU.mult))
                dve.tensor_scalar(sp_[:, 6:7], sp_[:, 4:5], -16.0, None, ALU.mult).then_inc(spd, 1)
                for c in range(NCH):
                    w = {n: t[:, c * CH:(c + 1) * CH] for n, t in v.items()}
                    dve.wait_ge(gate_sb, 2 * c + 2)
                    link(dve.tensor_scalar(w["tau"], w["ga"], col["a_imag"], 1.0 / (2.0 * PI), ALU.mult, ALU.mult))
                    link(dve.tensor_scalar(w["tk"], w["tau"], ROUND, ROUND, ALU.add, ALU.subtract))
                    link(dve.tensor_tensor(w["t1"], w["tau"], w["tk"], ALU.subtract))
                    link(dve.tensor_scalar(w["thi"], w["t1"], ROUND12, ROUND12, ALU.add, ALU.subtract))
                    link(dve.tensor_tensor(w["tlo"], w["t1"], w["thi"], ALU.subtract))
                    keep_ = carry[:, c * CH:(c + 1) * CH]
                    link(dve.tensor_tensor_scan(w["chi"], keep_, w["thi"], 0.0, ALU.mult, ALU.add))
                    link(dve.tensor_tensor_scan(w["clo"], keep_, w["tlo"], 0.0, ALU.mult, ALU.add))
                    link(dve.tensor_scalar(w["tk"], w["chi"], ROUND, ROUND, ALU.add, ALU.subtract))
                    link(dve.tensor_tensor(w["t1"], w["chi"], w["tk"], ALU.subtract))
                    dve.tensor_tensor(w["tau"], w["t1"], w["clo"], ALU.add).then_inc(th_ready, 1)
                    dve.wait_ge(mags, 2 * c + 2)
                    link(dve.tensor_scalar(w["t2"], w["nrm"], -1.0, 1.0, ALU.mult, ALU.add))
                    dve.tensor_scalar(w["nrm"], w["t2"], 1e-6, None, ALU.max).then_inc(nrm_in, 1)
                for c in range(NCH):
                    w = {n: t[:, c * CH:(c + 1) * CH] for n, t in v.items()}

                    def times(o, x, y, op=ALU.mult):
                        return dve.tensor_tensor(w[o], w[x], w[y], op)

                    link(dve.tensor_tensor(w["mag"], w["mag"], carry[:, c * CH:(c + 1) * CH], ALU.mult))
                    dve.wait_ge(nrm_out, c + 1)
                    link(times("t1", "nrm", "gx"))
                    link(times("xre", "xre", "t1"))
                    link(times("xim", "xim", "t1"))
                    dve.wait_ge(trig, 2 * c + 2)
                    link(dve.scalar_tensor_tensor(out=w["sn"], in0=w["s"], scalar=2.0, in1=w["c"], op0=ALU.mult,
                                                  op1=ALU.mult))
                    link(dve.scalar_tensor_tensor(out=w["t1"], in0=w["s"], scalar=-2.0, in1=w["s"], op0=ALU.mult,
                                                  op1=ALU.mult))
                    link(dve.tensor_scalar(w["cs"], w["t1"], 1.0, None, ALU.add))
                    link(times("t1", "xre", "cs"))
                    link(times("t2", "xim", "sn"))
                    link(times("t1", "t1", "t2", ALU.add))
                    link(times("t3", "xim", "cs"))
                    link(times("t2", "xre", "sn"))
                    link(times("t3", "t3", "t2", ALU.subtract))
                    link(dve.tensor_tensor_scan(w["xre"], w["mag"], w["t1"], 0.0, ALU.mult, ALU.add))
                    link(dve.tensor_tensor_scan(w["xim"], w["mag"], w["t3"], 0.0, ALU.mult, ALU.add))
                    link(times("t1", "xre", "cs"))
                    link(times("t2", "xim", "sn"))
                    link(times("t3", "t1", "t2", ALU.subtract))
                    link(times("t1", "xre", "sn"))
                    link(times("t2", "xim", "cs"))
                    times("t4", "t1", "t2", ALU.add).then_inc(h_ready, 1)
                for c in range(NCH):
                    dve.wait_ge(y_ps, c + 1)
                    dve.scalar_tensor_tensor(out=R[:, c * CH:(c + 1) * CH], in0=ps[:, 4 + c, :], scalar=col["b_out"],
                                             in1=X[:, c * CH:(c + 1) * CH], op0=ALU.add, op1=ALU.add).then_inc(r_ready, 1)
                dve_ln(0)
                dve_ln(1)

    with ExitStack() as st:
        def sb(name, shape, dt=F32):
            return st.enter_context(nc.sbuf_tensor(name, shape, dt))

        wq = sb("wq6", [C, C])
        wk = sb("wk6", [C, CC + 2])
        wv = sb("wv6", [CC + 1, C])
        den_sel = sb("den_sel", [CC + 1, C])
        ident = sb("ident6", [128, 128])
        ctx_k = sb("ctx_k", [128, NB, NKT, CC + 1])
        q = sb("q6", [C, T])
        qk = sb("qk6", [CC + 2, T])
        prob = sb("prob6", [128, 3, 2, TQ])
        nm = sb("nm6", [128, 2 * NB])
        osb = sb("osb6", [CC + 1, 2, TQ])
        lden = sb("lden6", [C, 2, TQ])
        rden = sb("rden6", [C, 2, TQ])
        att = sb("att6", [C, 2, TQ])
        s1 = st.enter_context(nc.psum_tensor("s1_6", [128, 4, 512], F32))
        s2 = st.enter_context(nc.psum_tensor("s2_6", [128, 2, 512], F32))
        o_ps = st.enter_context(nc.psum_tensor("o6", [128, 512], F32))
        fin = st.enter_context(nc.psum_tensor("fin6", [128, 512], F32))
        (ld, q_ps, q_sb, qk_ps, qk_sb, s1_ready, s1_red, row_ps, row_sb, s2_ready, exp_done, av_done, o_sb, fin_ps, dlog,
         drec, att_done, r_ready) = sems(st, *[f"b6_{n}" for n in (
             "ld", "q_ps", "q_sb", "qk_ps", "qk_sb", "s1_ready", "s1_red", "row_ps", "row_sb", "s2_ready", "exp_done",
             "av_done", "o_sb", "fin_ps", "dlog", "drec", "att_done", "r")])
        pe_ln, pe_ln2, act_ln, act_ln2, dve_ln, x_ready = ln_parts(st, "ln5", s1[:, 0:2, :], s1[:, 2:4, :], r_ready)
        PAIRS = (NKT + 1) // 2

        with nc.Block() as block:
            @block.sync
            def _(sp):
                for dst, src in ((wq, "wq6"), (wk, "wk6"), (wv, "wv6"), (den_sel, "den_sel"), (ident, "ident"),
                                 (ctx_k, "ctx_k")):
                    sp.dma_start(dst[:], a[src]).then_inc(ld, 16)

            @block.tensor
            def _(pe):
                pe.wait_ge(ld, 16 * 6)
                for c in range(NCH):
                    pe.matmul(s1[:, c, :], wq[:], X[:, c * CH:(c + 1) * CH], start=True, stop=True).then_inc(q_ps, 1)
                for c in range(NCH):
                    pe.wait_ge(q_sb, c + 1)
                    pe.matmul(s1[0:CC + 2, 2 + c, :], wk[:], q[:, c * CH:(c + 1) * CH],
                              start=True, stop=True).then_inc(qk_ps, 1)
                pe.wait_ge(qk_sb, 2)

                def query_major(b, t):
                    n = 2 * b + t
                    if n:
                        pe.wait_ge(s1_red, n)
                    for i in range(4):
                        w = min(512, TK - 512 * i)
                        last = pe.matmul(s1[:, i, 0:w], qk[:, n * 128:(n + 1) * 128], ctx_t[:, b, i * 512:i * 512 + w],
                                         start=True, stop=True)
                    last.then_inc(s1_ready, 1)

                def max_row(b):
                    pe.wait_ge(s1_red, 2 * b + 2)
                    if b:
                        pe.wait_ge(att_done, b)
                    for t in range(2):
                        last = pe.matmul(fin[CC:CC + 1, t * 128:(t + 1) * 128], nm[:, 2 * b + t:2 * b + t + 1], ident[:],
                                         start=True, stop=True)
                    last.then_inc(row_ps, 1)

                def scores_t(b, p):
                    k = b * PAIRS + p
                    if k >= 2:
                        pe.wait_ge(exp_done, k - 1)
                    for t in range(2 * p, min(2 * p + 2, NKT)):
                        m = 128 if t < NKT - 1 else KLAST
                        last = pe.matmul(s2[0:m, k % 2, (t % 2) * TQ:(t % 2 + 1) * TQ],
                                         ctx_t[:, b, t * 128:t * 128 + m], qk[:, b * TQ:(b + 1) * TQ],
                                         start=True, stop=True)
                    last.then_inc(s2_ready, 1)

                def outputs(b, p):
                    k = b * PAIRS + p
                    pe.wait_ge(exp_done, k + 1)
                    for t in range(2 * p, min(2 * p + 2, NKT)):
                        m = 128 if t < NKT - 1 else KLAST
                        last = pe.matmul(o_ps[0:CC + 1, 0:TQ], ctx_k[0:m, b, t, :], prob[0:m, k % 3, t % 2, :],
                                         start=(t == 0), stop=(t == NKT - 1))
                    last.then_inc(av_done, 1)

                query_major(0, 0)
                query_major(0, 1)
                max_row(0)
                for b in range(NB):
                    pe.wait_ge(row_sb, b + 1)
                    scores_t(b, 0)
                    for p in range(PAIRS):
                        if p + 1 < PAIRS:
                            scores_t(b, p + 1)
                        if p == 0 and b:
                            pe.wait_ge(o_sb, b)
                        if b + 1 < NB and p in (0, 2):
                            query_major(b + 1, p // 2)
                        outputs(b, p)
                    pe.wait_ge(o_sb, b + 1)
                    if b:
                        pe.wait_ge(att_done, b)
                    pe.matmul(fin[:, 0:TQ], wv[:], osb[:, b % 2, :], start=True, stop=True)
                    pe.matmul(fin[:, TQ:2 * TQ], den_sel[:], osb[:, b % 2, :], start=True, stop=True).then_inc(fin_ps, 1)
                    if b + 1 < NB:
                        max_row(b + 1)
                pe_ln(0)
                pe_ln(1)
                pe_ln2(0)
                pe_ln2(1)

            @block.scalar
            def _(act):
                for c in range(NCH):
                    act.wait_ge(q_ps, c + 1)
                    act.activation(q[:, c * CH:(c + 1) * CH], s1[:, c, :], ACT.Identity, bias=col["bq6"]).then_inc(q_sb, 1)

                for b in range(NB):
                    for p in range(PAIRS):
                        k = b * PAIRS + p
                        act.wait_ge(s2_ready, k + 1)
                        if k >= 3:
                            act.wait_ge(av_done, k - 2)
                        m, w = (128, 2 * TQ) if p < PAIRS - 1 or NKT % 2 == 0 else (KLAST, TQ)
                        act.activation(prob[0:m, k % 3].rearrange("p i q -> p (i q)")[:, 0:w], s2[0:m, k % 2, 0:w],
                                       ACT.Exp).then_inc(exp_done, 1)
                    act.wait_ge(fin_ps, b + 1)
                    act.activation(lden[:, b % 2, :], fin[:, TQ:2 * TQ], ACT.Ln).then_inc(dlog, 1)
                    act.wait_ge(dlog, b + 1)
                    act.activation(rden[:, b % 2, :], lden[:, b % 2, :], ACT.Exp, scale=-1.0).then_inc(drec, 1)
                act_ln(0)
                act_ln(1)
                act_ln2(0)
                act_ln2(1)

            @block.vector
            def _(dve):
                for c in range(NCH):
                    dve.wait_ge(qk_ps, c + 1)
                    dve.tensor_copy(qk[:, c * CH:(c + 1) * CH], s1[0:CC + 2, 2 + c, :]).then_inc(qk_sb, 1)

                def maxima(b):
                    for t in range(2):
                        n = 2 * b + t
                        dve.wait_ge(s1_ready, n + 1)
                        dve.tensor_reduce(nm[:, n:n + 1], s1[:].rearrange("p b n -> p (b n)")[:, 0:TK], AX.X, ALU.max,
                                          negate=True).then_inc(s1_red, 1)

                def row(b):
                    dve.wait_ge(row_ps, b + 1)
                    dve.tensor_copy(qk[CC:CC + 1, b * TQ:(b + 1) * TQ], fin[CC:CC + 1, 0:TQ]).then_inc(row_sb, 1)

                maxima(0)
                row(0)
                for b in range(NB):
                    if b + 1 < NB:
                        maxima(b + 1)
                    dve.wait_ge(av_done, PAIRS * (b + 1))
                    dve.tensor_copy(osb[:, b % 2, :], o_ps[0:CC + 1, 0:TQ]).then_inc(o_sb, 1)
                    dve.wait_ge(drec, b + 1)
                    dve.tensor_tensor(att[:, b % 2, :], fin[:, 0:TQ], rden[:, b % 2, :], ALU.mult).then_inc(att_done, 1)
                    dve.wait_ge(att_done, b + 1)
                    s = slice(b * TQ, (b + 1) * TQ)
                    last = dve.tensor_tensor(R[:, s], att[:, b % 2, :], X[:, s], ALU.add)
                    if b % 2:
                        last.then_inc(r_ready, 1)
                    if b + 1 < NB:
                        row(b + 1)
                dve_ln(0)
                dve_ln(1)

    with ExitStack() as st:
        def sb(name, shape, dt=F32):
            return st.enter_context(nc.sbuf_tensor(name, shape, dt))

        NM = HID // 128
        w12 = sb("w12_7", [C, 2, HID])
        h1w = sb("h1w", [128, NM, HID])
        h2w = sb("h2w", [128, NM, HID])
        w3 = sb("w3_7", [128, NM, C])
        ha = sb("ha", [128, NM, T])
        hb = sb("hb", [128, NM, T])
        sg = sb("sg7", [128, 2, CH])
        ps = st.enter_context(nc.psum_tensor("ps7", [128, 8, 512], F32))
        (ld, up_ps, sg_done, ha_done, h1_ps, hb_done, h2_ps, hc_done, y_ps, r_ready, stored) = sems(
            st, *[f"b7_{n}" for n in ("ld", "up_ps", "sg_done", "ha_done", "h1_ps", "hb_done", "h2_ps", "hc_done", "y_ps",
                                      "r", "stored")])
        pe_ln, pe_ln2, act_ln, act_ln2, dve_ln, x_ready = ln_parts(st, "ln6", ps[:, 2:4, :], ps[:, 4:6, :], r_ready)
        tiles = [(c, m) for c in range(NCH) for m in range(NM)]

        with nc.Block() as block:
            @block.sync
            def _(sp):
                for dst, src in ((w12, "w12"), (h1w, "h1w"), (h2w, "h2w"), (w3, "w3")):
                    sp.dma_start(dst[:], a[src]).then_inc(ld, 16)
                for c in range(NCH):
                    sp.wait_ge(x_ready, c + 1)
                    sp.dma_start(out[:, c * CH:(c + 1) * CH], X[:, c * CH:(c + 1) * CH]).then_inc(stored, 16)
                sp.wait_ge(stored, 16 * NCH)

            @block.tensor
            def _(pe):
                pe.wait_ge(ld, 16 * 4)
                for k, (c, m) in enumerate(tiles):
                    if k >= 2:
                        pe.wait_ge(ha_done, k - 1)
                    for i in range(2):
                        last = pe.matmul(ps[:, 2 * i + k % 2, :], w12[:, i, m * 128:(m + 1) * 128],
                                         X[:, c * CH:(c + 1) * CH], start=True, stop=True)
                    last.then_inc(up_ps, 1)

                def hidden(weights, src, src_ready, banks, emptied, ready):
                    for k, (c, m) in enumerate(tiles):
                        pe.wait_ge(src_ready, NM * (c + 1))
                        if k >= 2:
                            pe.wait_ge(emptied, k - 1)
                        for i in range(NM):
                            last = pe.matmul(ps[:, banks + k % 2, :], weights[:, i, m * 128:(m + 1) * 128],
                                             src[:, i, c * CH:(c + 1) * CH], start=(i == 0), stop=(i == NM - 1))
                        last.then_inc(ready, 1)

                hidden(h1w, ha, ha_done, 4, hb_done, h1_ps)
                hidden(h2w, hb, hb_done, 6, hc_done, h2_ps)
                for c in range(NCH):
                    pe.wait_ge(hc_done, NM * (c + 1))
                    for i in range(NM):
                        last = pe.matmul(ps[:, c, :], w3[:, i, :], ha[:, i, c * CH:(c + 1) * CH],
                                         start=(i == 0), stop=(i == NM - 1))
                    last.then_inc(y_ps, 1)
                pe_ln(0)
                pe_ln(1)
                pe_ln2(0)
                pe_ln2(1)

            @block.scalar
            def _(act):
                for k, (c, m) in enumerate(tiles):
                    act.wait_ge(up_ps, k + 1)
                    if k >= 2:
                        act.wait_ge(ha_done, k - 1)
                    act.activation(sg[:, k % 2, :], ps[:, k % 2, :], ACT.Silu, scale=col[f"s1_{m}"]).then_inc(sg_done, 1)
                for k, (c, m) in enumerate(tiles):
                    act.wait_ge(h1_ps, k + 1)
                    act.activation(hb[:, m, c * CH:(c + 1) * CH], ps[:, 4 + k % 2, :], ACT.Gelu,
                                   scale=col[f"sh1_{m}"]).then_inc(hb_done, 1)
                for k, (c, m) in enumerate(tiles):
                    act.wait_ge(h2_ps, k + 1)
                    act.wait_ge(h1_ps, NM * (c + 1))
                    act.activation(ha[:, m, c * CH:(c + 1) * CH], ps[:, 6 + k % 2, :], ACT.Gelu,
                                   scale=col[f"sh2_{m}"]).then_inc(hc_done, 1)
                act_ln(0)
                act_ln(1)
                act_ln2(0)
                act_ln2(1)

            @block.vector
            def _(dve):
                for k, (c, m) in enumerate(tiles):
                    dve.wait_ge(sg_done, k + 1)
                    dve.scalar_tensor_tensor(out=ha[:, m, c * CH:(c + 1) * CH], in0=ps[:, 2 + k % 2, :],
                                             scalar=col[f"s2_{m}"], in1=sg[:, k % 2, :], op0=ALU.mult,
                                             op1=ALU.mult).then_inc(ha_done, 1)
                for c in range(NCH):
                    dve.wait_ge(y_ps, c + 1)
                    dve.scalar_tensor_tensor(out=R[:, c * CH:(c + 1) * CH], in0=ps[:, c, :], scalar=col["s3"],
                                             in1=X[:, c * CH:(c + 1) * CH], op0=ALU.mult, op1=ALU.add).then_inc(r_ready, 1)
                dve_ln(0)
                dve_ln(1)


BIAS_COLUMNS = ("bq0", "bk0", "bo0", "bks", "bqs", "bqc", "bp", "eps", "a_real", "one", "b_in0", "b_in1", "bgx", "bga",
                "half_pi", "a_imag", "b_out", "bq6", *[f"{n}_{m}" for n in ("s1", "s2", "sh1", "sh2") for m in range(4)], "s3")


def laid_out(i):
    f = {k: np.asarray(v) for k, v in i.items()}
    f4 = np.float32
    order = np.array([8 * (4 * g + 2 * e + j) + c for g in range(4) for e in range(2) for c in range(8) for j in range(2)])
    o = {}
    o["x_t"] = f["x"].reshape(T, C).T
    ctx = f["ctx_512"]
    ctx_t = np.ones((CC + 2, NB, TK), f4)
    ctx_t[:CC] = ctx.transpose(2, 0, 1)
    o["ctx_t"] = ctx_t
    ctx_k = np.zeros((128, NB, NKT, CC + 1), f4)
    for t in range(NKT):
        m = min(128, TK - 128 * t)
        ctx_k[:m, :, t, :CC] = ctx[:, 128 * t:128 * t + m].transpose(1, 0, 2)
        ctx_k[:m, :, t, CC] = 1.0
    o["ctx_k"] = ctx_k
    o["w_att"] = np.stack([f[f"L0_attn_W{n}"] for n in "qkvo"], 1)
    o["bv0"] = np.broadcast_to(f["L0_attn_bv"], (128, C))
    o["half_neg"] = np.full((C, C), -0.5, f4)
    o["ones"] = np.ones((C, C), f4)
    o["neg_col"] = np.full((C, 2), -1.0, f4)
    o["averager"] = np.full((C, C), 1.0 / C, f4)
    o["mean_out"] = np.eye(C, dtype=f4) - f4(1.0 / C)
    o["wx"] = np.stack([f["L0_xattn_Wk"][:, order], f["L0_xattn_Wq"][:, order], f["L0_xattn_Wcq"][:, order]], 1)

    def value_columns(w):
        p = np.zeros((w.shape[0], H, VW), f4)
        p[:, :, :HD] = w.reshape(-1, H, HD)
        return p

    o["wv_pad"] = value_columns(f["L0_xattn_Wv"]).reshape(C, -1)
    bv = value_columns(f["L0_xattn_bv"][None])
    bv[:, :, HD] = 1.0
    o["bv_pad"] = np.broadcast_to(bv.reshape(1, -1), (128, H * VW))
    bcv = value_columns(f["L0_xattn_bcv"][None])
    bcv[:, :, HD] = 1.0
    o["wcv"] = np.concatenate([value_columns(f["L0_xattn_Wcv"]).reshape(CC, -1), bcv.reshape(1, -1)])
    o["wck"] = np.concatenate([f["L0_xattn_Wck"][:, order], f["L0_xattn_bck"][None, order]])
    spread = np.zeros((128, 128), f4)
    wp = np.zeros((128, NG, C), f4)
    for hh in range(4):
        spread[32 * hh + HD, 32 * hh:32 * hh + 32] = 1.0
        for g in range(NG):
            wp[32 * hh:32 * hh + HD, g] = f["L0_xattn_Wp"][8 * (4 * g + hh):8 * (4 * g + hh) + 8]
    o["spread"], o["wp"] = spread, wp
    o["ident"] = np.eye(128, dtype=f4)
    key, query = np.arange(128)[:, None], np.arange(128)[None]
    mask = np.where(key > query, MASKED, 0.0).astype(f4)
    o["masks"] = np.stack([mask, mask.T], 1)
    o["wg"] = f["L0_ffn_Wg"].T
    o["iota"] = np.broadcast_to(np.tile(np.arange(E, dtype=f4), 8), (128, 8 * E))
    o["b3"] = f["L0_ffn_b3"]
    o["wexp"] = np.concatenate([
        f["L0_ffn_W1"].transpose(0, 2, 1), f["L0_ffn_W2"].transpose(0, 2, 1),
        f["L0_ffn_W3"].reshape(E, C, DFF // 128, 128).transpose(0, 3, 2, 1).reshape(E, 128, DFF),
        f["L0_ffn_b1"].reshape(E, DFF // 128, 128).transpose(0, 2, 1),
        f["L0_ffn_b2"].reshape(E, DFF // 128, 128).transpose(0, 2, 1)], 2)
    o["win"] = f["L1_attn_w_in"].reshape(C, 2, C)
    gates = np.zeros((2, 2 * C, C), f4)
    for i_, n in enumerate(("x", "a")):
        for blk in range(8):
            gates[i_, 32 * blk:32 * blk + 32, 16 * blk:16 * blk + 16] = f[f"L1_attn_w_g{n}"][blk]
    o["wgate"] = gates.reshape(2, 2, C, C).transpose(2, 0, 1, 3)
    o["wout"] = f["L1_attn_w_out"].reshape(2, C, C).transpose(1, 0, 2)
    carry = np.ones((C, T), f4)
    carry[:, ::TQ] = 0.0
    o["carry"] = carry
    o["wq6"] = f["L1_xattn_Wq"]
    o["wk6"] = np.concatenate([f["L1_xattn_Wk"].T, np.zeros((C, 1), f4), f["L1_xattn_bk"][:, None]], 1)
    o["wv6"] = np.concatenate([f["L1_xattn_Wv"], f["L1_xattn_bv"][None]])
    den_sel = np.zeros((CC + 1, C), f4)
    den_sel[CC] = 1.0
    o["den_sel"] = den_sel
    o["w12"] = np.stack([f["L1_ffn_w1_w"].T, f["L1_ffn_w2_w"].T], 1)
    for n in ("h1", "h2"):
        o[f"{n}w"] = f[f"L1_ffn_{n}_w"].T.reshape(HID // 128, 128, HID).transpose(1, 0, 2)
    o["w3"] = f["L1_ffn_w3_w"].T.reshape(HID // 128, 128, C).transpose(1, 0, 2)
    columns = {
        "bq0": f["L0_attn_bq"], "bk0": f["L0_attn_bk"], "bo0": f["L0_attn_bo"], "bks": f["L0_xattn_bk"][order],
        "bqs": f["L0_xattn_bq"][order], "bqc": f["L0_xattn_bcq"][order], "bp": f["L0_xattn_bp"],
        "eps": np.full(C, EPS, f4), "a_real": f["L1_attn_a_real_param"], "one": np.ones(C, f4),
        "b_in0": f["L1_attn_b_in"][:C], "b_in1": f["L1_attn_b_in"][C:], "bgx": f["L1_attn_b_gx"],
        "bga": f["L1_attn_b_ga"], "half_pi": np.full(C, PI / 2, f4), "a_imag": f["L1_attn_a_imag_param"],
        "b_out": f["L1_attn_b_out"], "bq6": f["L1_xattn_bq"], "s3": f["L1_ffn_w3_s"]}
    for n, src in (("s1", "w1_s"), ("s2", "w2_s"), ("sh1", "h1_s"), ("sh2", "h2_s")):
        for m in range(HID // 128):
            columns[f"{n}_{m}"] = f[f"L1_ffn_{src}"][m * 128:(m + 1) * 128]
    o["biases"] = np.stack([columns[n] for n in BIAS_COLUMNS], 1)
    return {k: np.ascontiguousarray(v) for k, v in o.items()}


def kernel(**inputs):
    import concourse.bacc as bacc
    from concourse.bass_utils import run_bass_kernel_spmd

    nc = bacc.Bacc("TRN2", target_bir_lowering=False, num_devices=1)
    arrays = laid_out(inputs)
    args = {n: nc.dram_tensor(f"in_{n}", v.shape, mybir.dt.from_np(v.dtype), kind="ExternalInput").ap()
            for n, v in arrays.items()}
    out = nc.dram_tensor("out_t", (C, T), F32, kind="ExternalOutput").ap()
    decoder_program(nc, args, out)
    r = run_bass_kernel_spmd(nc, [{f"in_{n}": v for n, v in arrays.items()}], core_ids=[0])
    return r.results[0]["out_t"].T.reshape(NB, TQ, C)
```

```python
from contextlib import ExitStack

import numpy as np

import concourse.bass as bass
from concourse import mybir

ALU = mybir.AluOpType
ACT = mybir.ActivationFunctionType
AX = mybir.AxisListType
F32 = mybir.dt.float32
BF16 = mybir.dt.bfloat16
U32 = mybir.dt.uint32

NB, TQ, C = 4, 256, 128
T = NB * TQ
H, HD = 16, 8
TK, CC = 1601, 64
NKT = (TK + 127) // 128
KLAST = TK - 128 * (NKT - 1)
NG = H // 4
NU = NB * NG
NST = NKT + 2
ROWS = 6 * HD
PROWS = 2 * ROWS
KROWS = PROWS + 4
VW = 16
E, DFF = 8, 256
HID = 512
CH = 512
NCH = T // CH
EPS = 1e-5
SCALE = float(np.float32(1.0 / np.sqrt(HD)))
KPART = (0, 0, 0, 1, 1, 2)
QPART = (0, 1, 2, 0, 1, 0)
SLOTS = 3
MASKED = -1e30
EXP_LN = "natural_log_exp_and_others"
ROUND = 12582912.0
ROUND12 = 3072.0
PI = float(np.pi)


def decoder_program(nc, a, out):
    persistent = ExitStack()
    with persistent:
        def keep(name, shape, dt=F32):
            return persistent.enter_context(nc.sbuf_tensor(name, shape, dt))

        first_sems = ExitStack()
        sem_owner = [first_sems]
        first_named = []

        def sems(stack, *names):
            made = [sem_owner[0].enter_context(nc.semaphore(n)) for n in names]
            if sem_owner[0] is first_sems:
                first_named.extend(made)
            return made

        X = keep("X", [C, T])
        R = keep("R", [C, T])
        mean_out = keep("mean_out", [C, C])
        averager = keep("averager", [C, C])
        ctx_t = keep("ctx_t", [128, NB, TK])
        biases = keep("biases", [C, a["biases"].shape[1]])
        col = {n: biases[:, i:i + 1] for i, n in enumerate(BIAS_COLUMNS)}

        kc_scr = nc.dram_tensor("kc_scr", [NB, 8, 6, 16, TK], BF16).ap()
        vc_scr = nc.dram_tensor("vc_scr", [NB, NG, 128, NKT * 64], F32).ap()
        xs_scr = {n: nc.dram_tensor(f"{n}_scr", [NB, 8, 6, 16, TQ], BF16).ap() for n in ("ks", "qs", "qc")}
        vs_scr = nc.dram_tensor("vs_scr", [NB, NG, 128, 128], F32).ap()
        comb_scr = nc.dram_tensor("comb_scr", [E, T], F32).ap()

        def ln_parts(stack, tag, psum_c, psum_v, r_ready):
            sq = stack.enter_context(nc.sbuf_tensor(f"{tag}_sq", [C, T], F32))
            lnv = stack.enter_context(nc.sbuf_tensor(f"{tag}_ln", [C, T], F32))
            rstd = stack.enter_context(nc.sbuf_tensor(f"{tag}_rstd", [C, T], F32))
            centred, squared, var_ready, lnv_ready, rstd_ready, x_ready = sems(
                stack, *[f"{tag}_{n}" for n in ("centred", "squared", "var", "lnv", "rstd", "x")])

            def pe(c):
                nc.tensor.wait_ge(r_ready, c + 1)
                nc.tensor.matmul(psum_c[:, c, :], mean_out[:], R[:, c * CH:(c + 1) * CH],
                                 start=True, stop=True).then_inc(centred, 1)

            def pe2(c):
                nc.tensor.wait_ge(squared, c + 1)
                nc.tensor.matmul(psum_v[:, c, :], averager[:], sq[:, c * CH:(c + 1) * CH],
                                 start=True, stop=True).then_inc(var_ready, 1)

            def act(c):
                nc.scalar.wait_ge(centred, c + 1)
                nc.scalar.activation(sq[:, c * CH:(c + 1) * CH], psum_c[:, c, :], ACT.Square).then_inc(squared, 1)

            def act2(c):
                s = slice(c * CH, (c + 1) * CH)
                nc.scalar.wait_ge(var_ready, c + 1)
                nc.scalar.activation(lnv[:, s], psum_v[:, c, :], ACT.Ln, bias=col["eps"]).then_inc(lnv_ready, 1)
                nc.scalar.wait_ge(lnv_ready, c + 1)
                nc.scalar.activation(rstd[:, s], lnv[:, s], ACT.Exp, scale=-0.5).then_inc(rstd_ready, 1)

            def dve(c):
                s = slice(c * CH, (c + 1) * CH)
                nc.vector.wait_ge(rstd_ready, c + 1)
                nc.vector.tensor_tensor(X[:, s], psum_c[:, c, :], rstd[:, s], ALU.mult).then_inc(x_ready, 1)

            return pe, pe2, act, act2, dve, x_ready

        with ExitStack() as st:
            def sb(name, shape, dt=F32):
                return st.enter_context(nc.sbuf_tensor(name, shape, dt))

            wqkv = sb("wqkv", [C, 4, C])
            wx = sb("wx", [C, 3, C])
            wv_pad = sb("wv_pad", [C, H * VW])
            bv_pad = sb("bv_pad", [128, H * VW])
            wck = sb("wck", [128, C])
            wcv = sb("wcv", [128, H * VW])
            bv0 = sb("bv0", [128, C])
            half_neg = sb("half_neg", [C, C])
            ones = sb("ones", [C, C])
            neg_col = sb("neg_col", [C, 2])
            qt = sb("qt", [C, T])
            kt = sb("kt", [C, T])
            qsq = sb("qsq", [C, T])
            ksq = sb("ksq", [C, T])
            ksum = sb("ksum", [128, 8])
            v0 = sb("v0", [128, 8, C])
            e1 = sb("e1", [128, 2, 2 * TQ])
            p0 = sb("p0", [128, 2, 2 * TQ])
            lden = sb("lden", [C, 2, TQ])
            rden = sb("rden", [C, 2, TQ])
            ot = sb("ot", [C, 2, TQ])
            hi = sb("hi", [C, 2, 512], BF16)
            mid = sb("mid", [C, 2, 512], BF16)
            low = sb("low", [C, 2, 512], BF16)
            rem = sb("rem", [C, 2, 512])
            rem2 = sb("rem2", [C, 2, 512])
            full = sb("full", [C, 2, 512])
            vst = sb("vst", [128, NG, NKT, 64])
            vss = sb("vss", [128, NB, NG, 2, 64])
            ps = st.enter_context(nc.psum_tensor("ps1", [128, 8, 512], F32))

            (ld_att, ld_ctx, ld_x, cleared, ones_set) = sems(st, "ld_att", "ld_ctx", "ld_x", "cleared", "ones_set")
            (g_qk, g_qk_sb, g_sq, g_ksum, g_ksum_sb, g_v, g_v_sb, g_s, g_e1, g_p, g_o, g_lden, g_rden, g_ot,
             g_wo, g_r) = sems(st, *[f"g_{n}" for n in (
                 "qk", "qk_sb", "sq", "ksum", "ksum_sb", "v", "v_sb", "s", "e1", "p", "o", "lden", "rden", "ot",
                 "wo", "r")])
            (j_ps, j_hi, j_rem, j_mid, j_rem2, j_low, j_full) = sems(st, *[f"j_{n}" for n in (
                "ps", "hi", "rem", "mid", "rem2", "low", "full")])
            j_out = sems(st, "j_out0", "j_out1")
            (v_ps, v_sb, v_out, w_ps, w_sb, w_out) = sems(st, "v_ps", "v_sb", "v_out", "w_ps", "w_sb", "w_out")

            pieces = [("kc", b, c0, min(512, TK - c0)) for b in range(NB) for c0 in range(0, TK, 512)]
            NPC = len(pieces)
            pieces += [(n, i, b * TQ, TQ) for i, n in enumerate(("ks", "qs", "qc")) for b in range(NB)]
            NPX = len(pieces)

            pe_ln, pe_ln2, act_ln, act_ln2, dve_ln, x_ready = ln_parts(st, "ln1", ps[:, 4:6, :], ps[:, 6:8, :], g_r)

            def piece_target(j):
                kind, i, c0, w = pieces[j]
                if kind == "kc":
                    return [kc_scr[i, :, r, :, c0:c0 + w] for r in range(6)], KPART
                return [xs_scr[kind][c0 // TQ, :, r, :, :] for r in range(6)], (KPART if kind == "ks" else QPART)

            with nc.Block() as block:
                @block.sync
                def _(sp):
                    sp.dma_start(X[:], a["x_t"]).then_inc(ld_x, 16)
                    for dst, src in ((wqkv, "w_att"), (bv0, "bv0"), (half_neg, "half_neg"), (ones, "ones"),
                                     (neg_col, "neg_col"), (biases, "biases"), (mean_out, "mean_out"),
                                     (averager, "averager")):
                        sp.dma_start(dst[:], a[src]).then_inc(ld_att, 16)
                    for j in range(NPX):
                        sp.wait_ge(j_low, j + 1)
                        sp.wait_ge(j_mid, j + 1)
                        sp.wait_ge(j_hi, j + 1)
                        w = pieces[j][3]
                        targets, part = piece_target(j)
                        for r in range(6):
                            src = (hi, mid, low)[part[r]][:, j % 2, 0:w]
                            sp.dma_start(targets[r], src).then_inc(j_out[j % 2], 16)
                    sp.wait_ge(j_out[0], 96 * ((NPX + 1) // 2))
                    sp.wait_ge(j_out[1], 96 * (NPX // 2))

                @block.gpsimd
                def _(pool):
                    pool.memset(vst[:], 0.0).then_inc(cleared, 1)
                    for dst, src in ((wck, "wck"), (wcv, "wcv")):
                        pool.dma_start(dst[:], a[src]).then_inc(ld_ctx, 16)
                    for b in range(NB):
                        pool.dma_start(ctx_t[0:CC, b, :], a["ctx_t"][:, b, :]).then_inc(ld_ctx, 16)
                    for dst, src in ((wx, "wx"), (wv_pad, "wv_pad"), (bv_pad, "bv_pad")):
                        pool.dma_start(dst[:], a[src]).then_inc(ld_ctx, 16)
                    for b in range(NB):
                        pool.wait_ge(v_sb, NKT * (b + 1))
                        pool.dma_start(vc_scr[b].rearrange("g p n -> p g n"),
                                       vst[:].rearrange("p g t n -> p g (t n)")).then_inc(v_out, 16)
                    pool.wait_ge(w_sb, 8)
                    for b in range(NB):
                        pool.dma_start(vs_scr[b].rearrange("g p n -> p g n"),
                                       vss[:, b].rearrange("p g t n -> p g (t n)")).then_inc(w_out, 16)
                    pool.wait_ge(v_out, 16 * NB)
                    pool.wait_ge(w_out, 16 * NB)

                @block.tensor
                def _(pe):
                    pe.wait_ge(ld_x, 16)
                    pe.wait_ge(ld_att, 16 * 8)
                    for i in range(2):
                        for c in range(NCH):
                            pe.matmul(ps[:, 4 + 2 * i + c, :], wqkv[:, i, :], X[:, c * CH:(c + 1) * CH],
                                      start=True, stop=True).then_inc(g_qk, 1)
                    for t in range(8):
                        last = pe.matmul(ps[:, 2 + t // 4, (t % 4) * C:(t % 4 + 1) * C],
                                         X[:, t * 128:(t + 1) * 128], wqkv[:, 2, :], start=True, stop=True)
                        if t % 4 == 3:
                            last.then_inc(g_v, 1)
                    pe.wait_ge(ld_ctx, 16 * (5 + NB))
                    pe.wait_ge(ones_set, 1)

                    def piece(j):
                        if j >= 2:
                            pe.wait_ge(j_rem if j < NPC + 2 else j_full, j - 1 if j < NPC + 2 else j - 1 - NPC)
                        kind, i, c0, w = pieces[j]
                        if kind == "kc":
                            pe.matmul(ps[:, j % 2, 0:w], wck[:], ctx_t[:, i, c0:c0 + w],
                                      start=True, stop=True).then_inc(j_ps, 1)
                        else:
                            pe.matmul(ps[:, j % 2, 0:w], wx[:, i, :], X[:, c0:c0 + w],
                                      start=True, stop=True).then_inc(j_ps, 1)

                    def values(n):
                        b, t = n // NKT, n % NKT
                        k = 128 if t < NKT - 1 else KLAST
                        if n < 2:
                            pe.wait_ge(g_v_sb, n + 1)
                        else:
                            pe.wait_ge(v_sb, n - 1)
                        pe.matmul(ps[0:k, 2 + n % 2, 0:H * VW], ctx_t[:, b, t * 128:t * 128 + k], wcv[:],
                                  start=True, stop=True).then_inc(v_ps, 1)

                    pe.wait_ge(g_sq, 4)
                    for t in range(8):
                        last = pe.matmul(ps[:, 4, t:t + 1], ksq[:, t * 128:(t + 1) * 128], neg_col[:, 0:1],
                                         start=True, stop=True)
                    last.then_inc(g_ksum, 1)
                    for b in range(NB):
                        q = slice(b * TQ, (b + 1) * TQ)
                        if b >= 2:
                            pe.wait_ge(g_e1, 2 * (b - 1))
                        for t in range(2):
                            o = ps[:, 5 + b % 2, t * TQ:(t + 1) * TQ]
                            pe.matmul(o, kt[:, b * TQ + t * 128:b * TQ + (t + 1) * 128], qt[:, q],
                                      start=True, stop=False)
                            last = pe.matmul(o, half_neg[:], qsq[:, q], start=False, stop=True)
                        last.then_inc(g_s, 1)
                        for n in range(b * NKT, (b + 1) * NKT):
                            values(n)
                        for j in range(4 * b, 4 * b + 4):
                            piece(j)
                        pe.wait_ge(g_p, b + 1)
                        if b == 0:
                            pe.wait_ge(g_v_sb, 2)
                        if b >= 1:
                            pe.wait_ge(g_ot, b)
                            pe.wait_ge(g_lden, b)
                        for t in range(2):
                            pe.matmul(ps[:, 7, 0:TQ], v0[:, 2 * b + t, :], p0[:, b % 2, t * TQ:(t + 1) * TQ],
                                      start=(t == 0), stop=(t == 1))
                        for t in range(2):
                            last = pe.matmul(ps[:, 7, TQ:2 * TQ], ones[:], p0[:, b % 2, t * TQ:(t + 1) * TQ],
                                             start=(t == 0), stop=(t == 1))
                        last.then_inc(g_o, 1)
                        pe.wait_ge(g_ot, b + 1)
                        if b == 0:
                            pe.wait_ge(g_ksum_sb, 1)
                        if b == 2:
                            pe.wait_ge(g_r, 1)
                        pe.matmul(ps[:, 4, (b % 2) * TQ:(b % 2 + 1) * TQ], wqkv[:, 3, :], ot[:, b % 2, :],
                                  start=True, stop=True).then_inc(g_wo, 1)
                    pe.wait_ge(g_r, 2)
                    pe_ln(0)
                    pe_ln(1)
                    pe_ln2(0)
                    pe_ln2(1)
                    for c in range(NCH):
                        pe.wait_ge(x_ready, c + 1)
                    for j in range(NPC, NPX):
                        piece(j)
                    for t in range(8):
                        if t < 2:
                            pe.wait_ge(v_sb, NB * NKT - 1 + t)
                        else:
                            pe.wait_ge(w_sb, t - 1)
                        pe.matmul(ps[:, 2 + t % 2, 0:H * VW], X[:, t * 128:(t + 1) * 128], wv_pad[:],
                                  start=True, stop=True).then_inc(w_ps, 1)

                @block.scalar
                def _(act):
                    act.preload_act_table_set(EXP_LN)
                    act.wait_ge(ld_att, 16 * 8)
                    for i in range(4):
                        act.wait_ge(g_qk, i + 1)
                        dst, c = (qt, kt)[i // 2], i % 2
                        act.activation(dst[:, c * CH:(c + 1) * CH], ps[:, 4 + i, :], ACT.Identity,
                                       bias=col[("bq0", "bk0")[i // 2]]).then_inc(g_qk_sb, 1)
                    for i in range(4):
                        act.wait_ge(g_qk_sb, i + 1)
                        src, dst, c = (qt, kt)[i // 2], (qsq, ksq)[i // 2], i % 2
                        act.activation(dst[:, c * CH:(c + 1) * CH], src[:, c * CH:(c + 1) * CH],
                                       ACT.Square).then_inc(g_sq, 1)

                    def hi_mid(j):
                        w = pieces[j][3]
                        act.wait_ge(j_ps, j + 1)
                        if j >= 2:
                            act.wait_ge(j_out[j % 2], 96 * (j // 2))
                        if pieces[j][0] == "kc":
                            act.activation(hi[:, j % 2, 0:w], ps[:, j % 2, 0:w], ACT.Copy).then_inc(j_hi, 1)
                        else:
                            act.activation(full[:, j % 2, 0:w], ps[:, j % 2, 0:w], ACT.Identity,
                                           bias=col[("bks", "bqs", "bqc")[pieces[j][1]]]).then_inc(j_full, 1)
                            act.wait_ge(j_full, j - NPC + 1)
                            act.activation(hi[:, j % 2, 0:w], full[:, j % 2, 0:w], ACT.Copy).then_inc(j_hi, 1)
                        act.wait_ge(j_rem, j + 1)
                        act.activation(mid[:, j % 2, 0:w], rem[:, j % 2, 0:w], ACT.Copy).then_inc(j_mid, 1)

                    def values(n):
                        b, t = n // NKT, n % NKT
                        k = 128 if t < NKT - 1 else KLAST
                        act.wait_ge(v_ps, n + 1)
                        if n == 0:
                            act.wait_ge(cleared, 1)
                        if t == 0 and b:
                            act.wait_ge(v_out, 16 * b)
                        act.activation(vst[0:k, :, t, :], ps[0:k, 2 + n % 2, 0:H * VW].rearrange(
                            "p (g n) -> p g n", g=NG), ACT.Copy).then_inc(v_sb, 1)

                    for b in range(NB):
                        act.wait_ge(g_s, b + 1)
                        if b == 0:
                            act.wait_ge(g_ksum_sb, 1)
                        for t in range(2):
                            act.activation(e1[:, b % 2, t * TQ:(t + 1) * TQ], ps[:, 5 + b % 2, t * TQ:(t + 1) * TQ],
                                           ACT.Exp, bias=ksum[:, 2 * b + t:2 * b + t + 1], scale=2.0).then_inc(g_e1, 1)
                        act.wait_ge(g_e1, 2 * (b + 1))
                        act.activation(p0[:, b % 2, :], e1[:, b % 2, :], ACT.Exp).then_inc(g_p, 1)
                        for n in range(b * NKT, (b + 1) * NKT):
                            values(n)
                        for j in range(4 * b, 4 * b + 4):
                            hi_mid(j)
                        act.wait_ge(g_o, b + 1)
                        act.activation(lden[:, b % 2, :], ps[:, 7, TQ:2 * TQ], ACT.Ln).then_inc(g_lden, 1)
                        act.wait_ge(g_lden, b + 1)
                        act.activation(rden[:, b % 2, :], lden[:, b % 2, :], ACT.Exp, scale=-1.0).then_inc(g_rden, 1)
                    act_ln(0)
                    act_ln(1)
                    act_ln2(0)
                    act_ln2(1)
                    for j in range(NPC, NPX):
                        hi_mid(j)

                @block.vector
                def _(dve):
                    dve.memset(ctx_t[CC:128], 1.0).then_inc(ones_set, 1)
                    dve.wait_ge(ld_att, 16 * 8)
                    for i in range(2):
                        dve.wait_ge(g_v, i + 1)
                        for t in range(4):
                            last = dve.tensor_tensor(v0[:, 4 * i + t, :], ps[:, 2 + i, t * C:(t + 1) * C], bv0[:],
                                                     ALU.add)
                        last.then_inc(g_v_sb, 1)
                    dve.wait_ge(g_ksum, 1)
                    dve.tensor_copy(ksum[:], ps[:, 4, 0:8]).then_inc(g_ksum_sb, 1)

                    def split(j):
                        w = pieces[j][3]
                        s = (slice(None), j % 2, slice(0, w))
                        whole = ps[s] if pieces[j][0] == "kc" else full[s]
                        dve.wait_ge(j_hi, j + 1)
                        if j >= 2:
                            dve.wait_ge(j_mid, j - 1)
                        dve.tensor_tensor(rem[s], whole, hi[s], ALU.subtract).then_inc(j_rem, 1)
                        dve.wait_ge(j_mid, j + 1)
                        dve.tensor_tensor(low[s], rem[s], mid[s], ALU.subtract).then_inc(j_low, 1)

                    for b in range(NB):
                        for j in range(4 * b, 4 * b + 4):
                            split(j)
                        dve.wait_ge(g_rden, b + 1)
                        if b >= 2:
                            dve.wait_ge(g_wo, b - 1)
                        dve.tensor_tensor(ot[:, b % 2, :], ps[:, 7, 0:TQ], rden[:, b % 2, :],
                                          ALU.mult).then_inc(g_ot, 1)
                        if b % 2 == 1:
                            c = b // 2
                            dve.wait_ge(g_wo, b + 1)
                            dve.scalar_tensor_tensor(out=R[:, c * CH:(c + 1) * CH], in0=ps[:, 4, :],
                                                     scalar=col["bo0"], in1=X[:, c * CH:(c + 1) * CH],
                                                     op0=ALU.add, op1=ALU.add).then_inc(g_r, 1)
                    dve_ln(0)
                    dve_ln(1)
                    for j in range(NPC, NPX):
                        split(j)
                    for t in range(8):
                        dve.wait_ge(w_ps, t + 1)
                        dve.tensor_tensor(vss[:, t // 2, :, t % 2, :],
                                          ps[:, 2 + t % 2, 0:H * VW].rearrange("p (g n) -> p g n", g=NG),
                                          bv_pad[:].rearrange("p (g n) -> p g n", g=NG), ALU.add).then_inc(w_sb, 1)

        sem_owner[0] = persistent
        later = {n: keep(f"w_{n}", a[n].shape) for n in LATER}
        wexp = [keep(f"wexp{s}", a["wexp"].shape[1:]) for s in range(2)]
        outputs_scope = ExitStack()
        o_all = outputs_scope.enter_context(
            nc.sbuf_tensor("o_all", [128, NU, 2 * TQ], F32))
        with ExitStack() as st:
            def sb(name, shape, dt=F32):
                return st.enter_context(nc.sbuf_tensor(name, shape, dt))

            kc = [sb(f"kc{s}", [128, 2, TK], BF16) for s in range(SLOTS)]
            ks = [sb(f"ks{s}", [128, 2, TQ], BF16) for s in range(SLOTS)]
            qq = [sb(f"qq{s}", [128, 2, 2, 2, TQ], BF16) for s in range(SLOTS)]
            vv = [sb(f"vv{s}", [128, NST, 64]) for s in range(SLOTS)]
            prob = sb("prob", [128, 3, 4, TQ])
            nm_a = sb("nm_a", [128, 8])
            nm_b = sb("nm_b", [128, 8])
            nm = sb("nm", [128, 2, 2, 4])
            mrow = [sb(f"mrow{s}", [16, 2, 128], BF16) for s in range(SLOTS)]
            ident = sb("ident", [128, 128])
            ident_b = sb("ident_b", [128, 128], BF16)
            mask_kq = sb("mask_kq", [128, 128], BF16)
            mask_qk = sb("mask_qk", [128, 128], BF16)
            masks_f = sb("masks_f", [128, 2, 128])
            s1 = st.enter_context(nc.psum_tensor("s1", [128, 4, 512], F32))
            s2 = st.enter_context(nc.psum_tensor("s2", [128, 3, 512], F32))
            o_ps = st.enter_context(nc.psum_tensor("o_ps", [128, 2 * TQ], F32))
            (consts, consts_b, later_in, filled, s1_ready, s1_read, nm_ready, nm_t, m1_done, mrow_ready, s2_ready, exp_done, av_done,
             o_copied) = sems(st, "consts", "consts_b", "later_in", "filled", "s1_ready", "s1_read", "nm_ready", "nm_t", "m1_done",
                              "mrow_ready", "s2_ready", "exp_done", "av_done", "o_copied")
            slot_in = sems(st, *[f"slot_in{s}" for s in range(SLOTS)])
            max_in = sems(st, *[f"max_in{s}" for s in range(SLOTS)])
            SLOT_INC = 16 * 8
            MAX_INC = 16 * 4
            HALVES = 2 * NST
            LOOPED = 4
            JOBS = 16
            S2_FREE, P_FREE, S1_FREE = 3, 3, 2

            with nc.Block() as block:
                @block.gpsimd
                def _(pool):
                    pool.wait_ge(consts, 16 * 2)
                    for dst, src in ((ident_b, ident[:]), (mask_kq, masks_f[:, 0, :]), (mask_qk, masks_f[:, 1, :])):
                        pool.tensor_copy(dst[:], src).then_inc(consts_b, 1)
                    for done in first_named:
                        pool.sem_clear(done)
                    for n in LATER:
                        pool.dma_start(later[n][:], a[n]).then_inc(later_in, 16)
                    for s in range(2):
                        pool.dma_start(wexp[s][:], a["wexp"][s]).then_inc(later_in, 16)
                    pool.wait_ge(later_in, 16 * (len(LATER) + 2))

                @block.sync
                def _(sp):
                    for dst, src in ((ident, "ident"), (masks_f, "masks")):
                        sp.dma_start(dst[:], a[src]).then_inc(consts, 16)
                    sp.wait_ge(filled, 1)

                    pairs = {n: scr.rearrange("b g r c t -> (b g) r c t") for n, scr in (("kc", kc_scr), *xs_scr.items())}
                    values_c, values_s = (v.rearrange("b g p n -> (b g) p n") for v in (vc_scr, vs_scr))

                    def rows(name, at, count):
                        return pairs[name][bass.ds(at, count)].rearrange("o r c t -> (o r c) t").rearrange(
                            "(q j) t -> q j t", j=2)

                    def load(n, s):
                        for dst, src in ((kc, "kc"), (ks, "ks")):
                            sp.dma_start(dst[s][0:PROWS], rows(src, n * 2, 2)).then_inc(slot_in[s], 16)
                        for kind, src in enumerate(("qc", "qs")):
                            for e in range(2):
                                sp.dma_start(qq[s][ROWS * e:ROWS * (e + 1), e, kind, :, :],
                                             rows(src, n * 2 + e, 1)).then_inc(slot_in[s], 16)
                        for t0, t1, src in ((0, NKT, values_c), (NKT, NST, values_s)):
                            sp.dma_start(vv[s][:, t0:t1, :].rearrange("p t n -> p (t n)"),
                                         src[bass.ds(n, 1)].rearrange("o p n -> (o p) n")).then_inc(slot_in[s], 16)

                    def max_rows(s):
                        for e in range(2):
                            for part in range(2):
                                at = PROWS + 2 * e + part
                                sp.dma_start(qq[s][at:at + 1, e, :, :, :].rearrange("o k j (t q) -> o (k j t) q", t=2),
                                             mrow[s][8 * e:8 * e + 8, part, :]).then_inc(max_in[s], 16)

                    def step(i, u):
                        sp.wait_ge(av_done, i * (3 * NST) + (P_FREE + NST * u))
                        load(i * 3 + (u + 2), (u + 2) % SLOTS)
                        sp.wait_ge(mrow_ready, i * 3 + (u + 2))
                        max_rows((u + 1) % SLOTS)

                    load(0, 0)
                    load(1, 1)
                    sp.wait_ge(mrow_ready, 1)
                    max_rows(0)
                    with sp.Fori(0, LOOPED) as i:
                        for u in range(SLOTS):
                            step(i, u)
                    for n in range(SLOTS * LOOPED, NU - 2):
                        step(n // SLOTS, n % SLOTS)
                    sp.wait_ge(mrow_ready, NU)
                    max_rows((NU - 1) % SLOTS)

                @block.tensor
                def _(pe):
                    pe.sem_inc(av_done, P_FREE)
                    pe.wait_ge(consts, 16 * 2)
                    pe.wait_ge(consts_b, 3)

                    def score_half(s, k, base):
                        j, e, t = k // 8, (k // 4) % 2, (k // 2) % 2
                        pe.wait_ge(s1_read, base[0] + (base[1] + k + 1))
                        q = qq[s][0:PROWS, e, 0, j, t * 128:(t + 1) * 128]
                        if k % 2 == 0:
                            for i in range(2):
                                last = pe.matmul(s1[:, i, :], q, kc[s][0:PROWS, j, i * 512:(i + 1) * 512],
                                                 start=True, stop=True)
                        else:
                            pe.matmul(s1[:, 2, :], q, kc[s][0:PROWS, j, 1024:1536], start=True, stop=True)
                            pe.matmul(s1[:, 3, 0:TK - 1536], q, kc[s][0:PROWS, j, 1536:TK], start=True, stop=True)
                            qs_ = qq[s][0:PROWS, e, 1, j, t * 128:(t + 1) * 128]
                            w = 128 * (t + 1)
                            pe.matmul(s1[:, 3, 128:128 + w], qs_, ks[s][0:PROWS, j, 0:w], start=True, stop=False)
                            last = pe.matmul(s1[:, 3, w:w + 128], ident_b[:], mask_qk[:], start=False, stop=True)
                        last.then_inc(s1_ready, 1)

                    def scores_t(s, t, j, base):
                        k = 2 * t + j
                        pe.wait_ge(exp_done, base[0] + (base[1] + k + 1))
                        bank = k % 3
                        if t < NKT:
                            m = 128 if t < NKT - 1 else KLAST
                            last = pe.matmul(s2[0:m, bank, :].rearrange("p (e q) -> p e q", e=2), kc[s][0:KROWS, j, t * 128:t * 128 + m],
                                             qq[s][0:KROWS, :, 0, j, :],
                                             start=True, stop=True)
                        else:
                            q0 = 128 * (t - NKT)
                            w = TQ - q0
                            pe.matmul(s2[:, bank, 0:2 * w].rearrange("p (e q) -> p e q", e=2),
                                      ks[s][0:KROWS, j, q0:q0 + 128], qq[s][0:KROWS, :, 1, j, q0:TQ],
                                      start=True, stop=False)
                            for e in range(2):
                                last = pe.matmul(s2[:, bank, e * w:e * w + 128], ident_b[:], mask_kq[:],
                                                 start=False, stop=(e == 1))
                        last.then_inc(s2_ready, 1)

                    def outputs(s, t, base):
                        pe.wait_ge(exp_done, base[0] + (base[1] + S2_FREE + 2 * t + 2))
                        k = KLAST if t == NKT - 1 else 128
                        kind, q0 = (0, 0) if t < NKT else (1, 128 * (t - NKT))
                        for hh in range(4):
                            last = pe.matmul(o_ps[32 * hh:32 * hh + VW, kind * TQ + q0:(kind + 1) * TQ],
                                             vv[s][0:k, t, hh * VW:(hh + 1) * VW],
                                             prob[0:k, t % 3, 2 * (hh % 2) + hh // 2, q0:TQ],
                                             start=t in (0, NKT), stop=t in (NKT - 1, NST - 1))
                        last.then_inc(av_done, 1)

                    def unit(i, u, n=None):
                        nxt, after = (u + 1) % SLOTS, (u + 2) % SLOTS
                        has_next, has_after = n is None or n + 1 < NU, n is None or n + 2 < NU
                        pe.wait_ge(max_in[u], i * MAX_INC + MAX_INC)
                        s2_base = (i * (3 * HALVES), u * HALVES)
                        next_base = (i * (3 * JOBS), (u + 1) * JOBS)
                        after_base = (i * (3 * JOBS), (u + 2) * JOBS)
                        scores_t(u, 0, 0, s2_base)
                        scores_t(u, 0, 1, s2_base)
                        if has_next:
                            score_half(nxt, 8, next_base)
                        for t in range(NST):
                            if t + 1 < NST:
                                scores_t(u, t + 1, 0, s2_base)
                            if t < 7 and has_next:
                                score_half(nxt, 9 + t, next_base)
                            if t == 7 and has_after:
                                pe.wait_ge(slot_in[after], i * SLOT_INC + SLOT_INC * (1 if u == 0 else 2))
                                score_half(after, 0, after_base)
                            if t + 1 < NST:
                                scores_t(u, t + 1, 1, s2_base)
                            if t == 0:
                                pe.wait_ge(o_copied, i * 3 + (u + 1))
                            outputs(u, t, s2_base)
                            if t == 7 and has_next:
                                turn_maxima(i * 3 + (u + 2))
                            if t == 8 and has_next:
                                pe.wait_ge(mrow_ready, i * 3 + (u + 2))
                            if t >= 8 and has_after:
                                score_half(after, t - 7, after_base)

                    def turn_maxima(count):
                        pe.wait_ge(nm_ready, count)
                        pe.transpose(s1[0:16, 3, 384:512], nm[:].rearrange("p e k i -> p (e k i)"),
                                     ident[:]).then_inc(nm_t, 1)

                    pe.wait_ge(slot_in[0], SLOT_INC)
                    for k in range(JOBS):
                        score_half(0, k, (0, 0))
                    pe.wait_ge(slot_in[1], SLOT_INC)
                    score_half(1, 0, (0, JOBS))
                    turn_maxima(1)
                    pe.wait_ge(mrow_ready, 1)
                    for k in range(1, 8):
                        score_half(1, k, (0, JOBS))
                    with pe.Fori(0, LOOPED) as i:
                        for u in range(SLOTS):
                            unit(i, u)
                    for n in range(SLOTS * LOOPED, NU):
                        unit(n // SLOTS, n % SLOTS, n)

                @block.scalar
                def _(act):
                    act.preload_act_table_set(EXP_LN)
                    act.sem_inc(exp_done, S2_FREE)

                    def unit(i, u):
                        for k in range(HALVES):
                            t, half = k // 2, k % 2
                            if half == 0:
                                act.wait_ge(av_done, i * (3 * NST) + (u * NST + t + 1))
                            act.wait_ge(s2_ready, i * (3 * HALVES) + (u * HALVES + k + 1))
                            p = KLAST if t == NKT - 1 else 128
                            q0 = 0 if t < NKT else 128 * (t - NKT)
                            w = TQ - q0
                            act.activation(prob[0:p, t % 3, 2 * half:2 * half + 2, q0:TQ],
                                           s2[0:p, k % 3, 0:2 * w].rearrange("p (i q) -> p i q", i=2),
                                           ACT.Exp, scale=SCALE).then_inc(exp_done, 1)
                        act.wait_ge(av_done, i * (3 * NST) + (P_FREE + (u + 1) * NST))
                        act.activation(o_all[:, bass.ds(i * 3 + u, 1), :].rearrange("p o q -> p (o q)"), o_ps[:],
                                       ACT.Copy).then_inc(o_copied, 1)

                    with act.Fori(0, NU // SLOTS) as i:
                        for u in range(SLOTS):
                            unit(i, u)
                    unit(NU // SLOTS, 0)

                @block.vector
                def _(dve):
                    for s in range(SLOTS):
                        dve.memset(qq[s][:], 0.0)
                        dve.memset(kc[s][PROWS:128], 1.0)
                        last = dve.memset(ks[s][PROWS:128], 1.0)
                    last.then_inc(filled, 1)
                    dve.memset(o_ps[:], 0.0).then_inc(o_copied, 1)
                    dve.sem_inc(s1_read, S1_FREE)

                    def reduce_half(i3, u, k):
                        j, e, t = k // 8, (k // 4) % 2, (k // 2) % 2
                        i = 4 * e + 2 * j + t
                        dve.wait_ge(s1_ready, i3 * (3 * JOBS) + (u * JOBS + k + 1))
                        if k % 2 == 0:
                            dve.tensor_reduce(nm_a[:, i:i + 1], s1[:, 0:2, :], AX.XY, ALU.max,
                                              negate=True).then_inc(s1_read, 1)
                        else:
                            dve.tensor_reduce(nm_b[:, i:i + 1], s1[:, 2:4, :].rearrange("p b n -> p (b n)")[:, 0:TK - 1024],
                                              AX.X, ALU.max, negate=True)
                            dve.tensor_reduce(nm[:, e, 1, 2 * j + t:2 * j + t + 1], s1[:, 3, 128:128 + 128 * (t + 1)],
                                              AX.X, ALU.max, negate=True).then_inc(s1_read, 1)

                    def unit(i3, u, last_unit=False):
                        for k in range(1, JOBS):
                            reduce_half(i3, u, k)
                        dve.wait_ge(s1_read, i3 * (3 * JOBS) + (S1_FREE + (u + 1) * JOBS))
                        dve.tensor_tensor(nm[:, :, 0, :], nm_a[:].rearrange("p (e i) -> p e i", e=2),
                                          nm_b[:].rearrange("p (e i) -> p e i", e=2), ALU.min).then_inc(nm_ready, 1)
                        if not last_unit:
                            dve.wait_ge(nm_ready, i3 * 3 + (u + 1))
                            reduce_half(i3, u + 1, 0)
                        dve.wait_ge(nm_t, i3 * 3 + (u + 1))
                        dve.tensor_copy(mrow[u][:, 0, :], s1[0:16, 3, 384:512]).then_inc(m1_done, 1)
                        dve.wait_ge(m1_done, i3 * 3 + (u + 1))
                        dve.tensor_tensor(mrow[u][:, 1, :], s1[0:16, 3, 384:512], mrow[u][:, 0, :],
                                          ALU.subtract).then_inc(mrow_ready, 1)

                    reduce_half(0, 0, 0)
                    with dve.Fori(0, NU // SLOTS) as i3:
                        for u in range(SLOTS):
                            unit(i3, u)
                    unit(NU // SLOTS, 0, last_unit=True)

        first_sems.close()
        emit_rest(nc, a, out, sems, ln_parts, X, R, ctx_t, col, o_all, outputs_scope, later, wexp, comb_scr)


def emit_rest(nc, a, out, sems, ln_parts, X, R, ctx_t, col, o_all, outputs_scope, later, wexp, comb_scr):
    with ExitStack() as st:
        def sb(name, shape, dt=F32):
            return st.enter_context(nc.sbuf_tensor(name, shape, dt))

        spread = later["spread"]
        wp, wg, ident, iota = (later[n] for n in ("wp", "wg", "ident", "iota"))
        lden = sb("lden3", [128, 2, 512])
        rden = sb("rden3", [128, 2, 512])
        y2 = sb("y2", [128, 2, 512])
        y = sb("y", [128, 4, TQ])
        gout = sb("gout", [128, 8, E])
        top = sb("top", [128, 8, 8])
        idx = sb("idx", [128, 8, 8], U32)
        idxf = sb("idxf", [128, 8, 8])
        w12 = sb("w12", [128, 8, 4])
        w2 = sb("w2", [128, 8, 1])
        c1 = sb("c1", [128, 8, E])
        c2 = sb("c2", [128, 8, E])
        comb = sb("comb", [128, 8, E])
        comb_t = sb("comb_t", [E, T])
        ps = st.enter_context(nc.psum_tensor("ps3", [128, 8, 512], F32))
        (den, dlog, drec, y2s, ys, proj, r_ready, gates, chain, expd, combs, comb_ps, comb_sb, stored) = sems(
            st, "den", "dlog", "drec", "y2s", "ys", "proj", "b3_r", "gates", "b3_chain", "expd", "combs",
            "comb_ps", "comb_sb", "stored")
        pe_ln, pe_ln2, act_ln, act_ln2, dve_ln, x_ready = ln_parts(st, "ln2", ps[:, 4:6, :], ps[:, 6:8, :], r_ready)

        with nc.Block() as block:
            @block.sync
            def _(sp):
                sp.wait_ge(comb_sb, 2)
                sp.dma_start(comb_scr, comb_t[:]).then_inc(stored, 16)
                sp.wait_ge(stored, 16)

            @block.tensor
            def _(pe):
                def denominators(n):
                    if n >= 2:
                        pe.wait_ge(dlog, n - 1)
                    pe.matmul(ps[:, n % 2, :], spread[:], o_all[:, n, :], start=True, stop=True).then_inc(den, 1)

                denominators(0)
                denominators(1)
                for n in range(NU):
                    b, g = n // NG, n % NG
                    if n + 2 < NU:
                        denominators(n + 2)
                    pe.wait_ge(ys, n + 1)
                    last = pe.matmul(ps[:, 2 + b // 2, (b % 2) * TQ:(b % 2 + 1) * TQ], wp[:, g, :], y[:, n % 4, :],
                                     start=(g == 0), stop=(g == NG - 1))
                    last.then_inc(proj, 1)
                pe_ln(0)
                pe_ln(1)
                pe_ln2(0)
                pe_ln2(1)
                for t in range(8):
                    if t % 4 == 0:
                        pe.wait_ge(x_ready, t // 4 + 1)
                    last = pe.matmul(ps[:, 0, t * E:(t + 1) * E], X[:, t * 128:(t + 1) * 128], wg[:],
                                     start=True, stop=True)
                last.then_inc(gates, 1)
                pe.wait_ge(combs, 1)
                for t in range(8):
                    last = pe.transpose(ps[0:E, 2 + t // 4, (t % 4) * 128:(t % 4 + 1) * 128], comb[:, t, :], ident[:])
                    if t % 4 == 3:
                        last.then_inc(comb_ps, 1)

            @block.scalar
            def _(act):
                act.preload_act_table_set(EXP_LN)
                for n in range(NU):
                    act.wait_ge(den, n + 1)
                    act.activation(lden[:, n % 2, :], ps[:, n % 2, :], ACT.Ln).then_inc(dlog, 1)
                    act.wait_ge(dlog, n + 1)
                    if n >= 2:
                        act.wait_ge(y2s, n - 1)
                    act.activation(rden[:, n % 2, :], lden[:, n % 2, :], ACT.Exp, scale=-1.0).then_inc(drec, 1)
                act_ln(0)
                act_ln(1)
                act_ln2(0)
                act_ln2(1)
                act.wait_ge(chain, 18)
                act.activation(w12[:, :, 1:2], w12[:, :, 0:1], ACT.Exp).then_inc(expd, 1)

            @block.vector
            def _(dve):
                for n in range(NU):
                    dve.wait_ge(drec, n + 1)
                    dve.tensor_tensor(y2[:, n % 2, :], o_all[:, n, :], rden[:, n % 2, :], ALU.mult).then_inc(y2s, 1)
                    dve.wait_ge(y2s, n + 1)
                    if n >= 4:
                        dve.wait_ge(proj, n - 3)
                    dve.tensor_tensor(y[:, n % 4, :], y2[:, n % 2, 0:TQ], y2[:, n % 2, TQ:2 * TQ],
                                      ALU.add).then_inc(ys, 1)
                    if n % 8 == 7:
                        c = n // 8
                        dve.wait_ge(proj, n + 1)
                        dve.scalar_tensor_tensor(out=R[:, c * CH:(c + 1) * CH], in0=ps[:, 2 + c, :], scalar=col["bp"],
                                                 in1=X[:, c * CH:(c + 1) * CH], op0=ALU.add,
                                                 op1=ALU.add).then_inc(r_ready, 1)
                dve_ln(0)
                dve_ln(1)
                count = [0]

                def link(ins):
                    count[0] += 1
                    ins.then_inc(chain, 1)
                    dve.wait_ge(chain, count[0])

                dve.wait_ge(gates, 1)
                link(dve.tensor_copy(gout[:].rearrange("p t e -> p (t e)"), ps[:, 0, 0:8 * E]))
                for t in range(8):
                    link(dve.max(top[:, t, :], gout[:, t, :]))
                for t in range(8):
                    link(dve.max_index(idx[:, t, :], top[:, t, :], gout[:, t, :]))
                link(dve.tensor_tensor(w12[:, :, 0:1], top[:, :, 1:2], top[:, :, 0:1], ALU.subtract))
                link(dve.tensor_copy(idxf[:], idx[:]))
                link(dve.tensor_tensor(c1[:], iota[:].rearrange("p (t e) -> p t e", t=8),
                                       idxf[:, :, 0:1].to_broadcast([128, 8, E]), ALU.is_equal))
                link(dve.tensor_tensor(c2[:], iota[:].rearrange("p (t e) -> p t e", t=8),
                                       idxf[:, :, 1:2].to_broadcast([128, 8, E]), ALU.is_equal))
                dve.wait_ge(expd, 1)
                link(dve.tensor_scalar(w12[:, :, 2:3], w12[:, :, 1:2], 1.0, None, ALU.add))
                link(dve.reciprocal(w12[:, :, 3:4], w12[:, :, 2:3]))
                link(dve.tensor_tensor(w2[:], w12[:, :, 1:2], w12[:, :, 3:4], ALU.mult))
                link(dve.tensor_tensor(c1[:], c1[:], w12[:, :, 3:4].to_broadcast([128, 8, E]), ALU.mult))
                link(dve.tensor_tensor(c2[:], c2[:], w2[:].to_broadcast([128, 8, E]), ALU.mult))
                dve.tensor_tensor(comb[:], c1[:], c2[:], ALU.add).then_inc(combs, 1)
                for c in range(NCH):
                    dve.wait_ge(comb_ps, c + 1)
                    dve.tensor_copy(comb_t[:, c * CH:(c + 1) * CH], ps[0:E, 2 + c, :]).then_inc(comb_sb, 1)

    outputs_scope.close()

    with ExitStack() as st:
        def sb(name, shape, dt=F32):
            return st.enter_context(nc.sbuf_tensor(name, shape, dt))

        NF = DFF // 128
        comb_bc = [sb(f"comb_bc{s}", [128, T]) for s in range(2)]
        b3 = later["b3"]
        comb_r = sb("comb_r", [E, T])
        sg = sb("sg", [128, 2, CH])
        hv = sb("hv", [128, 2, CH])
        hh = sb("hh", [128, 4, CH])
        ps = st.enter_context(nc.psum_tensor("ps4", [128, 8, 512], F32))
        exp_in = sems(st, "exp_in0", "exp_in1")
        (ld, gv_ready, sg_done, hv_done, h_done, w3_done, out_done, r_ready) = sems(
            st, "b4_ld", "gv_ready", "sg_done", "hv_done", "h_done", "w3_done", "moe_out", "b4_r")
        pe_ln, pe_ln2, act_ln, act_ln2, dve_ln, x_ready = ln_parts(st, "ln3", ps[:, 0:2, :], ps[:, 2:4, :], r_ready)
        GV_FREE, H_FREE = 2, 4
        tiles = [(f, c) for f in range(NF) for c in range(NCH)]
        NT = len(tiles)

        with nc.Block() as block:
            @block.sync
            def _(sp):
                sp.dma_start(comb_r[:], comb_scr).then_inc(ld, 16)

                def load_weights(e, s):
                    sp.dma_start(wexp[s][:], a["wexp"][bass.ds(e, 1)].rearrange("o p n -> (o p) n")).then_inc(exp_in[s], 16)

                def load_comb(e, s):
                    sp.dma_start(comb_bc[s][:], comb_scr[bass.ds(e, 1), :].to_broadcast([128, T])).then_inc(exp_in[s], 16)

                load_comb(0, 0)
                load_comb(1, 1)
                with sp.Fori(1, E // 2) as i:
                    for s in range(2):
                        sp.wait_ge(w3_done, i * (2 * NT) + (H_FREE + (s - 1) * NT))
                        load_weights(i * 2 + s, s)
                        load_comb(i * 2 + s, s)

            @block.tensor
            def _(pe):
                pe.sem_inc(w3_done, H_FREE)
                pe.wait_ge(ld, 16)
                for c in range(NCH):
                    pe.matmul(ps[:, 4 + c, :], b3[:], comb_r[:, c * CH:(c + 1) * CH], start=True, stop=False,
                              skip_group_check=True)

                def up(i, s, k):
                    f, c = tiles[k]
                    done = i * (2 * NT) + (s * NT + k + 1)
                    pe.wait_ge(sg_done, done)
                    pe.wait_ge(hv_done, done)
                    for m in range(2):
                        last = pe.matmul(ps[:, 2 * m + k % 2, :], wexp[s][:, m * DFF + f * 128:m * DFF + (f + 1) * 128],
                                         X[:, c * CH:(c + 1) * CH], start=True, stop=True)
                    last.then_inc(gv_ready, 1)

                def down(i, s, k):
                    f, c = tiles[k]
                    pe.wait_ge(h_done, i * (2 * NT) + (s * NT + k + 1))
                    pe.matmul(ps[:, 4 + c, :], wexp[s][:, 2 * DFF + f * 128:2 * DFF + (f + 1) * 128], hh[:, k, :],
                              start=False, stop=False, skip_group_check=True).then_inc(w3_done, 1)

                def expert(i, s, before):
                    up(i, s, 0)
                    before()
                    up(i, s, 1)
                    up(i, s, 2)
                    down(i, s, 0)
                    up(i, s, 3)
                    down(i, s, 1)
                    down(i, s, 2)

                pe.wait_ge(exp_in[0], 16)
                expert(0, 0, lambda: None)
                pe.wait_ge(exp_in[1], 16)
                expert(0, 1, lambda: down(0, 0, 3))
                with pe.Fori(1, E // 2) as i:
                    pe.wait_ge(exp_in[0], i * 32 + 16)
                    expert(i, 0, lambda: down(i - 1, 1, 3))
                    pe.wait_ge(exp_in[1], i * 32 + 16)
                    expert(i, 1, lambda: down(i, 0, 3))
                down(E // 2 - 1, 1, 3)
                pe.wait_ge(r_ready, 2)
                pe_ln(0)
                pe_ln(1)
                pe_ln2(0)
                pe_ln2(1)

            @block.scalar
            def _(act):
                act.sem_inc(sg_done, GV_FREE)
                act.preload_act_table(ACT.Silu)
                with act.Fori(0, E // 2) as i:
                    for s in range(2):
                        act.wait_ge(exp_in[s], i * 32 + 16)
                        for k, (f, c) in enumerate(tiles):
                            act.wait_ge(gv_ready, i * (2 * NT) + (s * NT + k + 1))
                            act.wait_ge(hv_done, i * (2 * NT) + (s * NT + k + 1))
                            act.activation(sg[:, k % 2, :], ps[:, k % 2, :], ACT.Silu,
                                           bias=wexp[s][:, 3 * DFF + f:3 * DFF + f + 1]).then_inc(sg_done, 1)
                act.preload_act_table_set(EXP_LN)
                act_ln(0)
                act_ln(1)
                act_ln2(0)
                act_ln2(1)

            @block.vector
            def _(dve):
                dve.sem_inc(hv_done, GV_FREE)
                with dve.Fori(0, E // 2) as i:
                    for s in range(2):
                        dve.wait_ge(exp_in[s], i * 32 + 16)
                        for k, (f, c) in enumerate(tiles):
                            n = i * (2 * NT)
                            dve.wait_ge(sg_done, n + (GV_FREE + s * NT + k + 1))
                            dve.scalar_tensor_tensor(out=hv[:, k % 2, :], in0=ps[:, 2 + k % 2, :],
                                                     scalar=wexp[s][:, 3 * DFF + NF + f:3 * DFF + NF + f + 1],
                                                     in1=sg[:, k % 2, :], op0=ALU.add, op1=ALU.mult).then_inc(hv_done, 1)
                            dve.wait_ge(hv_done, n + (GV_FREE + s * NT + k + 1))
                            dve.wait_ge(w3_done, n + (s * NT + k + 1))
                            dve.tensor_tensor(hh[:, k, :], hv[:, k % 2, :], comb_bc[s][:, c * CH:(c + 1) * CH],
                                              ALU.mult).then_inc(h_done, 1)
                dve.wait_ge(w3_done, H_FREE + E * NT)
                for c in range(NCH):
                    dve.tensor_tensor(R[:, c * CH:(c + 1) * CH], ps[:, 4 + c, :], X[:, c * CH:(c + 1) * CH],
                                      ALU.add).then_inc(r_ready, 1)
                dve_ln(0)
                dve_ln(1)

    with ExitStack() as st:
        def sb(name, shape, dt=F32):
            return st.enter_context(nc.sbuf_tensor(name, shape, dt))

        win, wgate, wout, carry = (later[n] for n in ("win", "wgate", "wout", "carry"))
        names = ("xre", "xim", "gx", "ga", "mag", "nrm", "tau", "tk", "thi", "tlo", "chi", "clo", "s", "c", "sn", "cs",
                 "t1", "t2", "t3", "t4")
        v = {n: sb(f"r_{n}", [C, T]) for n in names}
        sp_ = sb("sp_", [C, 8])
        ps = st.enter_context(nc.psum_tensor("ps5", [128, 8, 512], F32))
        (xh, xh_sb, gate_ps, gate_sb, spc, spd, mags, nrm_in, nrm_out, th_ready, trig, h_ready, y_ps, r_ready,
         chain, act_chain) = sems(st, "xh", "xh_sb", "gate_ps", "gate_sb", "spc", "spd", "mags", "nrm_in",
                                  "nrm_out", "th_ready", "trig", "h_ready", "y_ps", "b5_r", "b5_chain", "b5_act")
        pe_ln, pe_ln2, act_ln, act_ln2, dve_ln, x_ready = ln_parts(st, "ln4", ps[:, 0:2, :], ps[:, 2:4, :], r_ready)

        with nc.Block() as block:
            @block.tensor
            def _(pe):
                for c in range(NCH):
                    for i in range(2):
                        pe.matmul(ps[:, 2 * c + i, :], win[:, i, :], X[:, c * CH:(c + 1) * CH],
                                  start=True, stop=True).then_inc(xh, 1)
                for c in range(NCH):
                    pe.wait_ge(xh_sb, 2 * c + 2)
                    for i in range(2):
                        pe.matmul(ps[:, 4 + 2 * c + i, :], wgate[:, i, 0, :], v["xre"][:, c * CH:(c + 1) * CH],
                                  start=True, stop=False)
                        pe.matmul(ps[:, 4 + 2 * c + i, :], wgate[:, i, 1, :], v["xim"][:, c * CH:(c + 1) * CH],
                                  start=False, stop=True).then_inc(gate_ps, 1)
                for c in range(NCH):
                    pe.wait_ge(h_ready, c + 1)
                    pe.matmul(ps[:, 4 + c, :], wout[:, 0, :], v["t3"][:, c * CH:(c + 1) * CH], start=True, stop=False)
                    pe.matmul(ps[:, 4 + c, :], wout[:, 1, :], v["t4"][:, c * CH:(c + 1) * CH],
                              start=False, stop=True).then_inc(y_ps, 1)
                pe_ln(0)
                pe_ln(1)
                pe_ln2(0)
                pe_ln2(1)

            @block.scalar
            def _(act):
                act.preload_act_table_set(EXP_LN)
                act.activation(sp_[:, 0:1], col["a_real"], ACT.Abs).then_inc(act_chain, 1)
                act.wait_ge(act_chain, 1)
                act.activation(sp_[:, 1:2], sp_[:, 0:1], ACT.Exp, scale=-1.0).then_inc(act_chain, 1)
                act.wait_ge(act_chain, 2)
                act.activation(sp_[:, 2:3], sp_[:, 1:2], ACT.Ln, bias=col["one"]).then_inc(spc, 1)
                for c in range(NCH):
                    for i, (dst, b) in enumerate((("xre", "b_in0"), ("xim", "b_in1"))):
                        act.wait_ge(xh, 2 * c + i + 1)
                        act.activation(v[dst][:, c * CH:(c + 1) * CH], ps[:, 2 * c + i, :], ACT.Identity,
                                       bias=col[b]).then_inc(xh_sb, 1)
                for c in range(NCH):
                    for i, (dst, b) in enumerate((("gx", "bgx"), ("ga", "bga"))):
                        act.wait_ge(gate_ps, 2 * c + i + 1)
                        act.activation(v[dst][:, c * CH:(c + 1) * CH], ps[:, 4 + 2 * c + i, :], ACT.Sigmoid,
                                       bias=col[b]).then_inc(gate_sb, 1)
                act.preload_act_table_set(EXP_LN)
                act.wait_ge(spd, 1)
                for c in range(NCH):
                    s = slice(c * CH, (c + 1) * CH)
                    act.wait_ge(gate_sb, 2 * c + 2)
                    act.activation(v["nrm"][:, s], v["ga"][:, s], ACT.Exp, scale=sp_[:, 6:7]).then_inc(mags, 1)
                    act.activation(v["mag"][:, s], v["ga"][:, s], ACT.Exp, scale=sp_[:, 5:6]).then_inc(mags, 1)
                for c in range(NCH):
                    s = slice(c * CH, (c + 1) * CH)
                    act.wait_ge(nrm_in, c + 1)
                    act.activation(v["nrm"][:, s], v["nrm"][:, s], ACT.Sqrt).then_inc(nrm_out, 1)
                act.preload_act_table(ACT.Sin)
                for c in range(NCH):
                    s = slice(c * CH, (c + 1) * CH)
                    act.wait_ge(th_ready, c + 1)
                    act.activation(v["tk"][:, s], v["tau"][:, s], ACT.Abs).then_inc(act_chain, 1)
                    act.activation(v["s"][:, s], v["tau"][:, s], ACT.Sin, scale=PI).then_inc(trig, 1)
                    act.wait_ge(act_chain, 3 + c)
                    act.activation(v["c"][:, s], v["tk"][:, s], ACT.Sin, scale=-PI, bias=col["half_pi"]).then_inc(trig, 1)
                act.preload_act_table_set(EXP_LN)
                act_ln(0)
                act_ln(1)
                act_ln2(0)
                act_ln2(1)

            @block.vector
            def _(dve):
                count = [0]

                def link(ins):
                    count[0] += 1
                    ins.then_inc(chain, 1)
                    dve.wait_ge(chain, count[0])

                dve.wait_ge(spc, 1)
                link(dve.tensor_scalar(sp_[:, 3:4], col["a_real"], 0.0, None, ALU.max))
                link(dve.tensor_tensor(sp_[:, 4:5], sp_[:, 3:4], sp_[:, 2:3], ALU.add))
                link(dve.tensor_scalar(sp_[:, 5:6], sp_[:, 4:5], -8.0, None, ALU.mult))
                dve.tensor_scalar(sp_[:, 6:7], sp_[:, 4:5], -16.0, None, ALU.mult).then_inc(spd, 1)
                for c in range(NCH):
                    w = {n: t[:, c * CH:(c + 1) * CH] for n, t in v.items()}
                    dve.wait_ge(gate_sb, 2 * c + 2)
                    link(dve.tensor_scalar(w["tau"], w["ga"], col["a_imag"], 1.0 / (2.0 * PI), ALU.mult, ALU.mult))
                    link(dve.tensor_scalar(w["tk"], w["tau"], ROUND, ROUND, ALU.add, ALU.subtract))
                    link(dve.tensor_tensor(w["t1"], w["tau"], w["tk"], ALU.subtract))
                    link(dve.tensor_scalar(w["thi"], w["t1"], ROUND12, ROUND12, ALU.add, ALU.subtract))
                    link(dve.tensor_tensor(w["tlo"], w["t1"], w["thi"], ALU.subtract))
                    keep_ = carry[:, c * CH:(c + 1) * CH]
                    link(dve.tensor_tensor_scan(w["chi"], keep_, w["thi"], 0.0, ALU.mult, ALU.add))
                    link(dve.tensor_tensor_scan(w["clo"], keep_, w["tlo"], 0.0, ALU.mult, ALU.add))
                    link(dve.tensor_scalar(w["tk"], w["chi"], ROUND, ROUND, ALU.add, ALU.subtract))
                    link(dve.tensor_tensor(w["t1"], w["chi"], w["tk"], ALU.subtract))
                    dve.tensor_tensor(w["tau"], w["t1"], w["clo"], ALU.add).then_inc(th_ready, 1)
                    dve.wait_ge(mags, 2 * c + 2)
                    link(dve.tensor_scalar(w["t2"], w["nrm"], -1.0, 1.0, ALU.mult, ALU.add))
                    dve.tensor_scalar(w["nrm"], w["t2"], 1e-6, None, ALU.max).then_inc(nrm_in, 1)
                for c in range(NCH):
                    w = {n: t[:, c * CH:(c + 1) * CH] for n, t in v.items()}

                    def times(o, x, y, op=ALU.mult):
                        return dve.tensor_tensor(w[o], w[x], w[y], op)

                    link(dve.tensor_tensor(w["mag"], w["mag"], carry[:, c * CH:(c + 1) * CH], ALU.mult))
                    dve.wait_ge(nrm_out, c + 1)
                    link(times("t1", "nrm", "gx"))
                    link(times("xre", "xre", "t1"))
                    link(times("xim", "xim", "t1"))
                    dve.wait_ge(trig, 2 * c + 2)
                    link(dve.scalar_tensor_tensor(out=w["sn"], in0=w["s"], scalar=2.0, in1=w["c"], op0=ALU.mult,
                                                  op1=ALU.mult))
                    link(dve.scalar_tensor_tensor(out=w["t1"], in0=w["s"], scalar=-2.0, in1=w["s"], op0=ALU.mult,
                                                  op1=ALU.mult))
                    link(dve.tensor_scalar(w["cs"], w["t1"], 1.0, None, ALU.add))
                    link(times("t1", "xre", "cs"))
                    link(times("t2", "xim", "sn"))
                    link(times("t1", "t1", "t2", ALU.add))
                    link(times("t3", "xim", "cs"))
                    link(times("t2", "xre", "sn"))
                    link(times("t3", "t3", "t2", ALU.subtract))
                    link(dve.tensor_tensor_scan(w["xre"], w["mag"], w["t1"], 0.0, ALU.mult, ALU.add))
                    link(dve.tensor_tensor_scan(w["xim"], w["mag"], w["t3"], 0.0, ALU.mult, ALU.add))
                    link(times("t1", "xre", "cs"))
                    link(times("t2", "xim", "sn"))
                    link(times("t3", "t1", "t2", ALU.subtract))
                    link(times("t1", "xre", "sn"))
                    link(times("t2", "xim", "cs"))
                    times("t4", "t1", "t2", ALU.add).then_inc(h_ready, 1)
                for c in range(NCH):
                    dve.wait_ge(y_ps, c + 1)
                    dve.scalar_tensor_tensor(out=R[:, c * CH:(c + 1) * CH], in0=ps[:, 4 + c, :], scalar=col["b_out"],
                                             in1=X[:, c * CH:(c + 1) * CH], op0=ALU.add, op1=ALU.add).then_inc(r_ready, 1)
                dve_ln(0)
                dve_ln(1)

    with ExitStack() as st:
        def sb(name, shape, dt=F32):
            return st.enter_context(nc.sbuf_tensor(name, shape, dt))

        wq = later["wq6"]
        wk = later["wk6"]
        den_sel = later["den_sel"]
        ctx_k = later["ctx_k"]
        wv, ident = later["wv6"], later["ident"]
        q = sb("q6", [C, T])
        qk = sb("qk6", [128, T])
        prob = sb("prob6", [128, 3, 2, TQ])
        nm = sb("nm6", [128, 2 * NB])
        osb = sb("osb6", [128, 2, TQ])
        lden = sb("lden6", [C, 2, TQ])
        rden = sb("rden6", [C, 2, TQ])
        att = sb("att6", [C, 2, TQ])
        s1 = st.enter_context(nc.psum_tensor("s1_6", [128, 4, 512], F32))
        s2 = st.enter_context(nc.psum_tensor("s2_6", [128, 2, 512], F32))
        o_ps = st.enter_context(nc.psum_tensor("o6", [128, 512], F32))
        fin = st.enter_context(nc.psum_tensor("fin6", [128, 512], F32))
        (q_ps, q_sb, qk_ps, qk_sb, s1_ready, s1_red, row_ps, row_sb, s2_ready, exp_done, av_done, o_sb, fin_ps, dlog,
         drec, att_done, r_ready) = sems(st, *[f"b6_{n}" for n in (
             "q_ps", "q_sb", "qk_ps", "qk_sb", "s1_ready", "s1_red", "row_ps", "row_sb", "s2_ready", "exp_done",
             "av_done", "o_sb", "fin_ps", "dlog", "drec", "att_done", "r")])
        pe_ln, pe_ln2, act_ln, act_ln2, dve_ln, x_ready = ln_parts(st, "ln5", s1[:, 0:2, :], s1[:, 2:4, :], r_ready)
        PAIRS = (NKT + 1) // 2

        with nc.Block() as block:
            @block.tensor
            def _(pe):
                for c in range(NCH):
                    pe.matmul(s1[:, c, :], wq[:], X[:, c * CH:(c + 1) * CH], start=True, stop=True).then_inc(q_ps, 1)
                for c in range(NCH):
                    pe.wait_ge(q_sb, c + 1)
                    pe.matmul(s1[:, 2 + c, :], wk[:], q[:, c * CH:(c + 1) * CH],
                              start=True, stop=True).then_inc(qk_ps, 1)
                pe.wait_ge(qk_sb, 2)

                def query_major(b, t):
                    n = 2 * b + t
                    if n:
                        pe.wait_ge(s1_red, n)
                    for i in range(4):
                        w = min(512, TK - 512 * i)
                        last = pe.matmul(s1[:, i, 0:w], qk[:, n * 128:(n + 1) * 128], ctx_t[:, b, i * 512:i * 512 + w],
                                         start=True, stop=True)
                    last.then_inc(s1_ready, 1)

                def max_row(b):
                    pe.wait_ge(s1_red, 2 * b + 2)
                    if b:
                        pe.wait_ge(att_done, b)
                    for t in range(2):
                        last = pe.matmul(fin[CC:CC + 1, t * 128:(t + 1) * 128], nm[:, 2 * b + t:2 * b + t + 1], ident[:],
                                         start=True, stop=True)
                    last.then_inc(row_ps, 1)

                def scores_t(b, p):
                    k = b * PAIRS + p
                    if k >= 2:
                        pe.wait_ge(exp_done, k - 1)
                    for t in range(2 * p, min(2 * p + 2, NKT)):
                        m = 128 if t < NKT - 1 else KLAST
                        last = pe.matmul(s2[0:m, k % 2, (t % 2) * TQ:(t % 2 + 1) * TQ],
                                         ctx_t[:, b, t * 128:t * 128 + m], qk[:, b * TQ:(b + 1) * TQ],
                                         start=True, stop=True)
                    last.then_inc(s2_ready, 1)

                def outputs(b, p):
                    k = b * PAIRS + p
                    pe.wait_ge(exp_done, k + 1)
                    for t in range(2 * p, min(2 * p + 2, NKT)):
                        m = 128 if t < NKT - 1 else KLAST
                        last = pe.matmul(o_ps[0:CC + 1, 0:TQ], ctx_k[0:m, b, t, :], prob[0:m, k % 3, t % 2, :],
                                         start=(t == 0), stop=(t == NKT - 1))
                    last.then_inc(av_done, 1)

                query_major(0, 0)
                query_major(0, 1)
                max_row(0)
                for b in range(NB):
                    pe.wait_ge(row_sb, b + 1)
                    scores_t(b, 0)
                    for p in range(PAIRS):
                        if p + 1 < PAIRS:
                            scores_t(b, p + 1)
                        if p == 0 and b:
                            pe.wait_ge(o_sb, b)
                        if b + 1 < NB and p in (0, 2):
                            query_major(b + 1, p // 2)
                        outputs(b, p)
                    pe.wait_ge(o_sb, b + 1)
                    if b:
                        pe.wait_ge(att_done, b)
                    pe.matmul(fin[:, 0:TQ], wv[:], osb[:, b % 2, :], start=True, stop=True)
                    pe.matmul(fin[:, TQ:2 * TQ], den_sel[:], osb[:, b % 2, :], start=True, stop=True).then_inc(fin_ps, 1)
                    if b + 1 < NB:
                        max_row(b + 1)
                pe_ln(0)
                pe_ln(1)
                pe_ln2(0)
                pe_ln2(1)

            @block.scalar
            def _(act):
                for c in range(NCH):
                    act.wait_ge(q_ps, c + 1)
                    act.activation(q[:, c * CH:(c + 1) * CH], s1[:, c, :], ACT.Identity, bias=col["bq6"]).then_inc(q_sb, 1)

                for b in range(NB):
                    for p in range(PAIRS):
                        k = b * PAIRS + p
                        act.wait_ge(s2_ready, k + 1)
                        if k >= 3:
                            act.wait_ge(av_done, k - 2)
                        m, w = (128, 2 * TQ) if p < PAIRS - 1 or NKT % 2 == 0 else (KLAST, TQ)
                        act.activation(prob[0:m, k % 3].rearrange("p i q -> p (i q)")[:, 0:w], s2[0:m, k % 2, 0:w],
                                       ACT.Exp).then_inc(exp_done, 1)
                    act.wait_ge(fin_ps, b + 1)
                    act.activation(lden[:, b % 2, :], fin[:, TQ:2 * TQ], ACT.Ln).then_inc(dlog, 1)
                    act.wait_ge(dlog, b + 1)
                    act.activation(rden[:, b % 2, :], lden[:, b % 2, :], ACT.Exp, scale=-1.0).then_inc(drec, 1)
                act.preload_act_table_set(EXP_LN)
                act_ln(0)
                act_ln(1)
                act_ln2(0)
                act_ln2(1)

            @block.vector
            def _(dve):
                dve.memset(osb[:], 0.0)
                for c in range(NCH):
                    dve.wait_ge(qk_ps, c + 1)
                    dve.tensor_copy(qk[:, c * CH:(c + 1) * CH], s1[:, 2 + c, :]).then_inc(qk_sb, 1)

                def maxima(b):
                    for t in range(2):
                        n = 2 * b + t
                        dve.wait_ge(s1_ready, n + 1)
                        dve.tensor_reduce(nm[:, n:n + 1], s1[:].rearrange("p b n -> p (b n)")[:, 0:TK], AX.X, ALU.max,
                                          negate=True).then_inc(s1_red, 1)

                def row(b):
                    dve.wait_ge(row_ps, b + 1)
                    dve.tensor_copy(qk[CC:CC + 1, b * TQ:(b + 1) * TQ], fin[CC:CC + 1, 0:TQ]).then_inc(row_sb, 1)

                maxima(0)
                row(0)
                for b in range(NB):
                    if b + 1 < NB:
                        maxima(b + 1)
                    dve.wait_ge(av_done, PAIRS * (b + 1))
                    dve.tensor_copy(osb[0:CC + 1, b % 2, :], o_ps[0:CC + 1, 0:TQ]).then_inc(o_sb, 1)
                    dve.wait_ge(drec, b + 1)
                    dve.tensor_tensor(att[:, b % 2, :], fin[:, 0:TQ], rden[:, b % 2, :], ALU.mult).then_inc(att_done, 1)
                    dve.wait_ge(att_done, b + 1)
                    s = slice(b * TQ, (b + 1) * TQ)
                    last = dve.tensor_tensor(R[:, s], att[:, b % 2, :], X[:, s], ALU.add)
                    if b % 2:
                        last.then_inc(r_ready, 1)
                    if b + 1 < NB:
                        row(b + 1)
                dve_ln(0)
                dve_ln(1)

    with ExitStack() as st:
        def sb(name, shape, dt=F32):
            return st.enter_context(nc.sbuf_tensor(name, shape, dt))

        NM = HID // 128
        w12, h1w, h2w, w3 = (later[n] for n in ("w12", "h1w", "h2w", "w3"))
        ha = sb("ha", [128, NM, T])
        hb = sb("hb", [128, NM, T])
        sg = sb("sg7", [128, 2, CH])
        ps = st.enter_context(nc.psum_tensor("ps7", [128, 8, 512], F32))
        (up_ps, sg_done, ha_done, h1_ps, hb_done, h2_ps, hc_done, y_ps, r_ready, stored) = sems(
            st, *[f"b7_{n}" for n in ("up_ps", "sg_done", "ha_done", "h1_ps", "hb_done", "h2_ps", "hc_done", "y_ps",
                                      "r", "stored")])
        pe_ln, pe_ln2, act_ln, act_ln2, dve_ln, x_ready = ln_parts(st, "ln6", ps[:, 2:4, :], ps[:, 4:6, :], r_ready)
        tiles = [(c, m) for c in range(NCH) for m in range(NM)]

        with nc.Block() as block:
            @block.sync
            def _(sp):
                for c in range(NCH):
                    sp.wait_ge(x_ready, c + 1)
                    sp.dma_start(out[:, c * CH:(c + 1) * CH], X[:, c * CH:(c + 1) * CH]).then_inc(stored, 16)
                sp.wait_ge(stored, 16 * NCH)

            @block.tensor
            def _(pe):
                for k, (c, m) in enumerate(tiles):
                    if k >= 2:
                        pe.wait_ge(ha_done, k - 1)
                    for i in range(2):
                        last = pe.matmul(ps[:, 2 * i + k % 2, :], w12[:, i, m * 128:(m + 1) * 128],
                                         X[:, c * CH:(c + 1) * CH], start=True, stop=True)
                    last.then_inc(up_ps, 1)

                def hidden(weights, src, src_ready, banks, emptied, ready):
                    for k, (c, m) in enumerate(tiles):
                        pe.wait_ge(src_ready, NM * (c + 1))
                        if k >= 2:
                            pe.wait_ge(emptied, k - 1)
                        for i in range(NM):
                            last = pe.matmul(ps[:, banks + k % 2, :], weights[:, i, m * 128:(m + 1) * 128],
                                             src[:, i, c * CH:(c + 1) * CH], start=(i == 0), stop=(i == NM - 1))
                        last.then_inc(ready, 1)

                hidden(h1w, ha, ha_done, 4, hb_done, h1_ps)
                hidden(h2w, hb, hb_done, 6, hc_done, h2_ps)
                for c in range(NCH):
                    pe.wait_ge(hc_done, NM * (c + 1))
                    for i in range(NM):
                        last = pe.matmul(ps[:, c, :], w3[:, i, :], ha[:, i, c * CH:(c + 1) * CH],
                                         start=(i == 0), stop=(i == NM - 1))
                    last.then_inc(y_ps, 1)
                pe_ln(0)
                pe_ln(1)
                pe_ln2(0)
                pe_ln2(1)

            @block.scalar
            def _(act):
                for k, (c, m) in enumerate(tiles):
                    act.wait_ge(up_ps, k + 1)
                    if k >= 2:
                        act.wait_ge(ha_done, k - 1)
                    act.activation(sg[:, k % 2, :], ps[:, k % 2, :], ACT.Silu, scale=col[f"s1_{m}"]).then_inc(sg_done, 1)
                for k, (c, m) in enumerate(tiles):
                    act.wait_ge(h1_ps, k + 1)
                    act.activation(hb[:, m, c * CH:(c + 1) * CH], ps[:, 4 + k % 2, :], ACT.Gelu,
                                   scale=col[f"sh1_{m}"]).then_inc(hb_done, 1)
                for k, (c, m) in enumerate(tiles):
                    act.wait_ge(h2_ps, k + 1)
                    act.wait_ge(h1_ps, NM * (c + 1))
                    act.activation(ha[:, m, c * CH:(c + 1) * CH], ps[:, 6 + k % 2, :], ACT.Gelu,
                                   scale=col[f"sh2_{m}"]).then_inc(hc_done, 1)
                act.preload_act_table_set(EXP_LN)
                act_ln(0)
                act_ln(1)
                act_ln2(0)
                act_ln2(1)

            @block.vector
            def _(dve):
                for k, (c, m) in enumerate(tiles):
                    dve.wait_ge(sg_done, k + 1)
                    dve.scalar_tensor_tensor(out=ha[:, m, c * CH:(c + 1) * CH], in0=ps[:, 2 + k % 2, :],
                                             scalar=col[f"s2_{m}"], in1=sg[:, k % 2, :], op0=ALU.mult,
                                             op1=ALU.mult).then_inc(ha_done, 1)
                for c in range(NCH):
                    dve.wait_ge(y_ps, c + 1)
                    dve.scalar_tensor_tensor(out=R[:, c * CH:(c + 1) * CH], in0=ps[:, c, :], scalar=col["s3"],
                                             in1=X[:, c * CH:(c + 1) * CH], op0=ALU.mult, op1=ALU.add).then_inc(r_ready, 1)
                dve_ln(0)
                dve_ln(1)


LATER = ("spread", "wp", "wg", "ident", "iota", "b3", "win", "wgate", "wout", "carry", "wq6", "wk6", "wv6", "den_sel",
         "ctx_k", "w12", "h1w", "h2w", "w3")
BIAS_COLUMNS = ("bq0", "bk0", "bo0", "bks", "bqs", "bqc", "bp", "eps", "a_real", "one", "b_in0", "b_in1", "bgx", "bga",
                "half_pi", "a_imag", "b_out", "bq6", *[f"{n}_{m}" for n in ("s1", "s2", "sh1", "sh2") for m in range(4)], "s3")


def laid_out(i):
    f = {k: np.asarray(v) for k, v in i.items()}
    f4 = np.float32
    order = np.array([8 * (4 * g + 2 * e + j) + c for g in range(4) for e in range(2) for c in range(8) for j in range(2)])
    o = {}
    o["x_t"] = f["x"].reshape(T, C).T
    ctx = f["ctx_512"]
    o["ctx_t"] = ctx.transpose(2, 0, 1)
    ctx_k = np.zeros((128, NB, NKT, CC + 1), f4)
    for t in range(NKT):
        m = min(128, TK - 128 * t)
        ctx_k[:m, :, t, :CC] = ctx[:, 128 * t:128 * t + m].transpose(1, 0, 2)
        ctx_k[:m, :, t, CC] = 1.0
    o["ctx_k"] = ctx_k
    o["w_att"] = np.stack([f[f"L0_attn_W{n}"] for n in "qkvo"], 1)
    o["bv0"] = np.broadcast_to(f["L0_attn_bv"], (128, C))
    o["half_neg"] = np.full((C, C), -0.5, f4)
    o["ones"] = np.ones((C, C), f4)
    o["neg_col"] = np.full((C, 2), -1.0, f4)
    o["averager"] = np.full((C, C), 1.0 / C, f4)
    o["mean_out"] = np.eye(C, dtype=f4) - f4(1.0 / C)
    o["wx"] = np.stack([f["L0_xattn_Wk"][:, order], f["L0_xattn_Wq"][:, order], f["L0_xattn_Wcq"][:, order]], 1)

    def rows_below(*parts):
        height = sum(p.shape[0] for p in parts)
        return np.concatenate([*parts, np.zeros((128 - height, parts[0].shape[1]), f4)])

    def value_columns(w):
        p = np.zeros((w.shape[0], H, VW), f4)
        p[:, :, :HD] = w.reshape(-1, H, HD)
        return p

    o["wv_pad"] = value_columns(f["L0_xattn_Wv"]).reshape(C, -1)
    bv = value_columns(f["L0_xattn_bv"][None])
    bv[:, :, HD] = 1.0
    o["bv_pad"] = np.broadcast_to(bv.reshape(1, -1), (128, H * VW))
    bcv = value_columns(f["L0_xattn_bcv"][None])
    bcv[:, :, HD] = 1.0
    o["wcv"] = rows_below(value_columns(f["L0_xattn_Wcv"]).reshape(CC, -1), bcv.reshape(1, -1))
    o["wck"] = rows_below(f["L0_xattn_Wck"][:, order], f["L0_xattn_bck"][None, order])
    spread = np.zeros((128, 128), f4)
    wp = np.zeros((128, NG, C), f4)
    for hh in range(4):
        spread[32 * hh + HD, 32 * hh:32 * hh + 32] = 1.0
        for g in range(NG):
            wp[32 * hh:32 * hh + HD, g] = f["L0_xattn_Wp"][8 * (4 * g + hh):8 * (4 * g + hh) + 8]
    o["spread"], o["wp"] = spread, wp
    o["ident"] = np.eye(128, dtype=f4)
    key, query = np.arange(128)[:, None], np.arange(128)[None]
    mask = np.where(key > query, MASKED, 0.0).astype(f4)
    o["masks"] = np.stack([mask, mask.T], 1)
    o["wg"] = f["L0_ffn_Wg"].T
    o["iota"] = np.broadcast_to(np.tile(np.arange(E, dtype=f4), 8), (128, 8 * E))
    o["b3"] = f["L0_ffn_b3"]
    o["wexp"] = np.concatenate([
        f["L0_ffn_W1"].transpose(0, 2, 1), f["L0_ffn_W2"].transpose(0, 2, 1),
        f["L0_ffn_W3"].reshape(E, C, DFF // 128, 128).transpose(0, 3, 2, 1).reshape(E, 128, DFF),
        f["L0_ffn_b1"].reshape(E, DFF // 128, 128).transpose(0, 2, 1),
        f["L0_ffn_b2"].reshape(E, DFF // 128, 128).transpose(0, 2, 1)], 2)
    o["win"] = f["L1_attn_w_in"].reshape(C, 2, C)
    gates = np.zeros((2, 2 * C, C), f4)
    for i_, n in enumerate(("x", "a")):
        for blk in range(8):
            gates[i_, 32 * blk:32 * blk + 32, 16 * blk:16 * blk + 16] = f[f"L1_attn_w_g{n}"][blk]
    o["wgate"] = gates.reshape(2, 2, C, C).transpose(2, 0, 1, 3)
    o["wout"] = f["L1_attn_w_out"].reshape(2, C, C).transpose(1, 0, 2)
    carry = np.ones((C, T), f4)
    carry[:, ::TQ] = 0.0
    o["carry"] = carry
    o["wq6"] = f["L1_xattn_Wq"]
    o["wk6"] = rows_below(f["L1_xattn_Wk"], np.zeros((1, C), f4), f["L1_xattn_bk"][None]).T
    o["wv6"] = rows_below(f["L1_xattn_Wv"], f["L1_xattn_bv"][None])
    den_sel = np.zeros((C, C), f4)
    den_sel[CC] = 1.0
    o["den_sel"] = den_sel
    o["w12"] = np.stack([f["L1_ffn_w1_w"].T, f["L1_ffn_w2_w"].T], 1)
    for n in ("h1", "h2"):
        o[f"{n}w"] = f[f"L1_ffn_{n}_w"].T.reshape(HID // 128, 128, HID).transpose(1, 0, 2)
    o["w3"] = f["L1_ffn_w3_w"].T.reshape(HID // 128, 128, C).transpose(1, 0, 2)
    columns = {
        "bq0": f["L0_attn_bq"], "bk0": f["L0_attn_bk"], "bo0": f["L0_attn_bo"], "bks": f["L0_xattn_bk"][order],
        "bqs": f["L0_xattn_bq"][order], "bqc": f["L0_xattn_bcq"][order], "bp": f["L0_xattn_bp"],
        "eps": np.full(C, EPS, f4), "a_real": f["L1_attn_a_real_param"], "one": np.ones(C, f4),
        "b_in0": f["L1_attn_b_in"][:C], "b_in1": f["L1_attn_b_in"][C:], "bgx": f["L1_attn_b_gx"],
        "bga": f["L1_attn_b_ga"], "half_pi": np.full(C, PI / 2, f4), "a_imag": f["L1_attn_a_imag_param"],
        "b_out": f["L1_attn_b_out"], "bq6": f["L1_xattn_bq"], "s3": f["L1_ffn_w3_s"]}
    for n, src in (("s1", "w1_s"), ("s2", "w2_s"), ("sh1", "h1_s"), ("sh2", "h2_s")):
        for m in range(HID // 128):
            columns[f"{n}_{m}"] = f[f"L1_ffn_{src}"][m * 128:(m + 1) * 128]
    o["biases"] = np.stack([columns[n] for n in BIAS_COLUMNS], 1)
    return {k: np.ascontiguousarray(v) for k, v in o.items()}


def kernel(**inputs):
    import concourse.bacc as bacc
    from concourse.bass_utils import run_bass_kernel_spmd

    nc = bacc.Bacc("TRN2", target_bir_lowering=False, num_devices=1)
    arrays = laid_out(inputs)
    args = {n: nc.dram_tensor(f"in_{n}", v.shape, mybir.dt.from_np(v.dtype), kind="ExternalInput").ap()
            for n, v in arrays.items()}
    out = nc.dram_tensor("out_t", (C, T), F32, kind="ExternalOutput").ap()
    decoder_program(nc, args, out)
    r = run_bass_kernel_spmd(nc, [{f"in_{n}": v for n, v in arrays.items()}], core_ids=[0])
    return r.results[0]["out_t"].T.reshape(NB, TQ, C)
```

```python
from contextlib import ExitStack

import numpy as np

import concourse.bass as bass
from concourse import mybir

ALU = mybir.AluOpType
ACT = mybir.ActivationFunctionType
AX = mybir.AxisListType
F32 = mybir.dt.float32
BF16 = mybir.dt.bfloat16
F32R = mybir.dt.float32r
U32 = mybir.dt.uint32

NB, TQ, C = 4, 256, 128
T = NB * TQ
H, HD = 16, 8
TK, CC = 1601, 64
NKT = (TK + 127) // 128
KLAST = TK - 128 * (NKT - 1)
NG = H // 4
NU = NB * NG
NST = NKT + 2
ROWS = 6 * HD
PROWS = 2 * ROWS
KROWS = PROWS + 4
VW = HD + 1
E, DFF = 8, 256
HID = 512
CH = 512
NCH = T // CH
EPS = 1e-5
SCALE = float(np.float32(1.0 / np.sqrt(HD)))
KPART = (0, 0, 0, 1, 1, 2)
QPART = (0, 1, 2, 0, 1, 0)
SLOTS = 3
MASKED = -1e30
EXP_LN = "natural_log_exp_and_others"
ROUND = 12582912.0
ROUND12 = 3072.0
PI = float(np.pi)


def columns_of(tensor, widths):
    at, views = 0, []
    for w in widths:
        views.append(tensor[:, at:at + w])
        at += w
    return views


def reciprocals(dve, den, part, done):
    dve.reciprocal(den[:, 1, :], den[:, 0, :]).then_inc(done, 1)
    dve.wait_ge(done, 1)
    dve.tensor_copy(part[:, 0, :], den[:, 1, :]).then_inc(done, 1)
    dve.wait_ge(done, 2)
    dve.tensor_tensor(den[:, 2, :], den[:, 1, :], part[:, 0, :], ALU.subtract).then_inc(done, 1)
    dve.wait_ge(done, 3)
    dve.tensor_copy(part[:, 1, :], den[:, 2, :]).then_inc(done, 1)
    dve.wait_ge(done, 4)
    dve.tensor_tensor(part[:, 2, :], den[:, 2, :], part[:, 1, :], ALU.subtract).then_inc(done, 1)


def decoder_program(nc, a, out):
    persistent = ExitStack()
    with persistent:
        def keep(name, shape, dt=F32):
            return persistent.enter_context(nc.sbuf_tensor(name, shape, dt))

        first_sems = ExitStack()
        sem_owner = [first_sems]
        first_named = []

        def sems(stack, *names):
            made = [sem_owner[0].enter_context(nc.semaphore(n)) for n in names]
            if sem_owner[0] is first_sems:
                first_named.extend(made)
            return made

        X = keep("X", [C, T])
        R = keep("R", [C, T])
        base = keep("base", [128, a["base"].shape[1]])
        mean_out, averager, ident, biases = columns_of(base, [C, C, 128, len(BIAS_COLUMNS)])
        ctx_t = keep("ctx_t", [128, NB, TK])
        col = {n: biases[:, i:i + 1] for i, n in enumerate(BIAS_COLUMNS)}

        kc_scr = nc.dram_tensor("kc_scr", [3, NB, 128, TK], BF16).ap()
        xs_scr = {n: nc.dram_tensor(f"{n}_scr", [6, NB, 128, TQ], BF16).ap() for n in ("ks", "qs", "qc")}
        vc_scr = nc.dram_tensor("vc_scr", [NB, NG, 128, NKT * 4 * VW], F32).ap()
        vs_scr = nc.dram_tensor("vs_scr", [NB, NG, 128, 2 * 4 * VW], F32).ap()
        exp_scr = nc.dram_tensor("exp_scr", [E, 2, 128, 3 * DFF], F32).ap()
        comb_scr = nc.dram_tensor("comb_scr", [E, T], F32).ap()

        def ln_parts(stack, tag, psum_c, psum_v, r_ready, apart=False):
            sq = stack.enter_context(nc.sbuf_tensor(f"{tag}_sq", [C, T], F32))
            lnv = stack.enter_context(nc.sbuf_tensor(f"{tag}_ln", [C, T], F32))
            rstd = stack.enter_context(nc.sbuf_tensor(f"{tag}_rstd", [C, T], F32))
            centred, squared, var_ready, lnv_ready, rstd_ready, x_ready = sems(
                stack, *[f"{tag}_{n}" for n in ("centred", "squared", "var", "lnv", "rstd", "x")])

            def pe(c):
                nc.tensor.wait_ge(r_ready, c + 1)
                nc.tensor.matmul(psum_c[:, c, :], mean_out, R[:, c * CH:(c + 1) * CH],
                                 start=True, stop=True).then_inc(centred, 1)

            def pe2(c):
                nc.tensor.wait_ge(squared, c + 1)
                nc.tensor.matmul(psum_v[:, c, :], averager, sq[:, c * CH:(c + 1) * CH],
                                 start=True, stop=True).then_inc(var_ready, 1)

            def act(c):
                nc.scalar.wait_ge(centred, c + 1)
                nc.scalar.activation(sq[:, c * CH:(c + 1) * CH], psum_c[:, c, :], ACT.Square).then_inc(squared, 1)

            def act_log(c):
                s = slice(c * CH, (c + 1) * CH)
                nc.scalar.wait_ge(var_ready, c + 1)
                nc.scalar.activation(lnv[:, s], psum_v[:, c, :], ACT.Ln, bias=col["eps"]).then_inc(lnv_ready, 1)

            def act_exp(c):
                s = slice(c * CH, (c + 1) * CH)
                nc.scalar.wait_ge(lnv_ready, c + 1)
                nc.scalar.activation(rstd[:, s], lnv[:, s], ACT.Exp, scale=-0.5).then_inc(rstd_ready, 1)

            def dve(c):
                s = slice(c * CH, (c + 1) * CH)
                nc.vector.wait_ge(rstd_ready, c + 1)
                nc.vector.tensor_tensor(X[:, s], psum_c[:, c, :], rstd[:, s], ALU.mult).then_inc(x_ready, 1)

            def act2(c):
                act_log(c)
                act_exp(c)

            parts = pe, pe2, act, act2, dve, x_ready
            return (*parts, act_log, act_exp) if apart else parts

        up_w = [[keep(f"up_{part}{s}", [128, 2 * DFF], F32R) for part in ("high", "low")] for s in range(2)]
        down_w = [[keep(f"down_{part}{s}", [128, DFF], F32R) for part in ("high", "low")] for s in range(2)]
        exp_bias = [keep(f"exp_bias{s}", [128, 2 * (DFF // 128)]) for s in range(2)]
        up_in, down_in = ([persistent.enter_context(nc.semaphore(f"{n}_in{s}")) for s in range(2)] for n in ("up", "down"))
        b3 = keep("b3", [E, C])
        SLOT_INC = 16 * 14

        def load_unit(sp, n, s, of_context=True, of_x=True):
            keys = kc_scr.rearrange("q b (g m) t -> q (b g) m t", g=NG)
            for e in range(2):
                at = ROWS * e
                for part, r0, copies in ((0, 0, 3), (1, 3, 2), (2, 5, 1)) if of_context else ():
                    src = keys[part, bass.ds(n, 1), 16 * e:16 * e + 16, :].rearrange("o (c j) t -> (o c) (j t)", j=2)
                    sp.dma_start(kc[s][at + HD * r0:at + HD * (r0 + copies)],
                                 src.unsqueeze(0).to_broadcast([copies, HD, 2 * TK])).then_inc(slot_in[s], 16)
                for dst, name in ((ks[s][at:at + ROWS], "ks"), (qq[s][at:at + ROWS, e, 0], "qc"),
                                  (qq[s][at:at + ROWS, e, 1], "qs")) if of_x else ():
                    src = xs_scr[name].rearrange("r b (g m) t -> r (b g) m t", g=NG)[:, bass.ds(n, 1), 16 * e:16 * e + 16, :]
                    sp.dma_start(dst, src.rearrange("r o (c j) t -> r (o c) (j t)", j=2)).then_inc(slot_in[s], 16)
            for t0, t1, values in [(0, NKT, vc_scr)] * of_context + [(NKT, NST, vs_scr)] * of_x:
                src = values.rearrange("b g p n -> (b g) p n")[bass.ds(n, 1)].rearrange("o p n -> (o p) n")
                sp.dma_start(vv[s][:, t0:t1, :].rearrange("p t n -> p (t n)"), src).then_inc(slot_in[s], 16)

        slots_scope = ExitStack()
        persistent.enter_context(slots_scope)

        def slot(name, shape, dt):
            return slots_scope.enter_context(nc.sbuf_tensor(name, shape, dt))

        kc = [slot(f"kc{s}", [128, 2, TK], BF16) for s in range(SLOTS)]
        ks = [slot(f"ks{s}", [128, 2, TQ], BF16) for s in range(SLOTS)]
        qq = [slot(f"qq{s}", [128, 2, 2, 2, TQ], BF16) for s in range(SLOTS)]
        vv = [slot(f"vv{s}", [128, NST, 4 * VW], F32) for s in range(SLOTS)]
        ident_b = slot("ident_b", [128, 128], BF16)
        mask_kq = slot("mask_kq", [128, 128], BF16)
        mask_qk = slot("mask_qk", [128, 128], BF16)
        slot_in = [persistent.enter_context(nc.semaphore(f"slot_in{s}")) for s in range(SLOTS)]
        filled = persistent.enter_context(nc.semaphore("filled"))
        ld_masks, v_out, w_out = (persistent.enter_context(nc.semaphore(n)) for n in ("ld_masks", "v_out", "w_out"))
        j_out = [persistent.enter_context(nc.semaphore(f"j_out{n}")) for n in ("0", "1", "_x")]

        with ExitStack() as st:
            def sb(name, shape, dt=F32):
                return st.enter_context(nc.sbuf_tensor(name, shape, dt))

            att_w = sb("att_w", [128, a["att_w"].shape[1]])
            wq0, wk0, wv0, wo0, bv0, half_neg, neg_col = columns_of(att_w, [C] * 6 + [1])
            proj_w = sb("proj_w", [128, a["proj_w"].shape[1]])
            wck, wx_ks, wx_qs, wx_qc, wcv, wv_x, bv_x = columns_of(proj_w, [C] * 4 + [H * VW] * 3)
            masks_f = sb("masks_f", [128, 2, 128])
            qt = sb("qt", [C, T])
            kt = sb("kt", [C, T])
            qsq = sb("qsq", [C, T])
            ksq = sb("ksq", [C, T])
            ksum = sb("ksum", [128, 8])
            v0 = sb("v0", [128, 8, C + 1])
            e1 = sb("e1", [128, 2, 2 * TQ])
            p0 = sb("p0", [128, NB, 2 * TQ])
            rden = sb("rden", [128, 8])
            o_tok = qt[:].rearrange("p (t n) -> p t n", t=8)
            o_chan = kt
            hi = sb("hi", [C, 2, TK], BF16)
            mid = sb("mid", [C, 2, TK], BF16)
            low = sb("low", [C, 2, TK], BF16)
            x_parts = [sb(f"x_{n}", [C, 3, T], BF16) for n in ("hi", "mid", "low")]
            rem = sb("rem", [C, 2, 512])
            vst = sb("vst", [128, 2, NG, NKT, 4 * VW])
            vss = sb("vss", [128, NB, NG, 2, 4 * VW])
            ps = st.enter_context(nc.psum_tensor("ps1", [128, 8, 512], F32))

            (ld_att, ld_base, ld_proj, ld_x, cleared, ones_set, masks_b) = sems(
                st, "ld_att", "ld_base", "ld_proj", "ld_x", "cleared", "ones_set", "masks_b")
            ld_ctx = sems(st, *[f"ld_ctx{b}" for b in range(NB)])
            (g_qk, g_qk_sb, g_sq, g_ksum, g_ksum_sb, g_v, g_v_sb, g_s, g_e1, g_p, g_o, g_rden, g_otok, g_t, g_ochan,
             g_wo, g_r) = sems(st, *[f"g_{n}" for n in (
                 "qk", "qk_sb", "sq", "ksum", "ksum_sb", "v", "v_sb", "s", "e1", "p", "o", "rden", "otok", "t", "ochan",
                 "wo", "r")])
            (j_ps, j_hi, j_rem, j_mid, c_low, x_low, v_ps, v_sb) = sems(
                st, "j_ps", "j_hi", "j_rem", "j_mid", "c_low", "x_low", "v_ps", "v_sb")

            groups = [("kc", 0), ("kc", 1), ("ks", "bks"), ("qs", "bqs"), ("qc", "bqc"), ("kc", 2), ("kc", 3)]
            wx = {"ks": wx_ks, "qs": wx_qs, "qc": wx_qc}
            pieces = []
            for gi, (kind, _) in enumerate(groups):
                width = TK if kind == "kc" else T
                pieces += [(gi, c0, min(512, width - c0)) for c0 in range(0, width, 512)]
            last_piece = [max(j for j, p in enumerate(pieces) if p[0] == gi) for gi in range(len(groups))]
            is_ctx = [groups[p[0]][0] == "kc" for p in pieces]

            def parts_of(j):
                gi, c0, w = pieces[j]
                if is_ctx[j]:
                    return [buf[:, groups[gi][1] % 2, c0:c0 + w] for buf in (hi, mid, low)]
                return [buf[:, gi - 2, c0:c0 + w] for buf in x_parts]

            def wait_parts_left(engine, j):
                if is_ctx[j] and groups[pieces[j][0]][1] >= 2:
                    engine.wait_ge(j_out[groups[pieces[j][0]][1] % 2], 16 * 3)

            def lows(j):
                return (c_low if is_ctx[j] else x_low), sum(is_ctx[i] == is_ctx[j] for i in range(j + 1))

            ctx_values = {b: [(b, t0, min(3, NKT - t0)) for t0 in range(0, NKT, 3)] for b in range(NB)}
            values_order = [*ctx_values[0], *ctx_values[1], *[("x", b) for b in range(NB)], *ctx_values[2], *ctx_values[3]]

            def values_done(b):
                return 1 + max(n for n, v in enumerate(values_order) if v[0] == b)

            X_VALUES = 1 + max(n for n, v in enumerate(values_order) if v[0] == "x")
            by_chunk = ps[:, 4:8, :].rearrange("p (c k) n -> p c k n", k=2)
            pe_ln, pe_ln2, act_ln, act_ln2, dve_ln, x_ready = ln_parts(st, "ln1", by_chunk[:, :, 0], by_chunk[:, :, 1], g_r)

            with nc.Block() as block:
                def parts_out(sp, gi):
                    kind, j = groups[gi][0], last_piece[gi]
                    sp.wait_ge(j_hi, j + 1)
                    sp.wait_ge(j_mid, j + 1)
                    sp.wait_ge(*lows(j))
                    if kind == "kc":
                        b = groups[gi][1]
                        for part, src in enumerate((hi, mid, low)):
                            sp.dma_start(kc_scr[part, b], src[:, b % 2, :]).then_inc(j_out[b % 2], 16)
                    else:
                        for r in range(6):
                            src = x_parts[(KPART if kind == "ks" else QPART)[r]]
                            sp.dma_start(xs_scr[kind][r].rearrange("b p t -> p b t"),
                                         src[:, gi - 2, :].rearrange("p (b t) -> p b t", b=NB)).then_inc(j_out[2], 16)

                @block.sync
                def _(sp):
                    sp.dma_start(X[:], a["x_t"]).then_inc(ld_x, 16)
                    sp.dma_start(att_w[:], a["att_w"]).then_inc(ld_att, 16)
                    sp.dma_start(base[:], a["base"]).then_inc(ld_base, 16)
                    parts_out(sp, 0)
                    sp.wait_ge(filled, 3)
                    sp.wait_ge(v_out, 16)
                    sp.wait_ge(j_out[0], 16 * 3)
                    load_unit(sp, 0, 0, of_x=False)
                    for gi in range(1, 5):
                        parts_out(sp, gi)
                    sp.wait_ge(filled, 3 * SLOTS)
                    sp.wait_ge(v_out, 32)
                    sp.wait_ge(w_out, 16)
                    for s in range(2):
                        sp.wait_ge(j_out[s], 16 * 3)
                    sp.wait_ge(j_out[2], 16 * 18)
                    load_unit(sp, 0, 0, of_context=False)
                    parts_out(sp, 5)
                    parts_out(sp, 6)

                @block.gpsimd
                def _(pool):
                    pool.dma_start(masks_f[:], a["masks"]).then_inc(ld_masks, 16)
                    pool.memset(vst[:, :, :, NKT - 1, :], 0.0).then_inc(cleared, 1)
                    pool.wait_ge(cleared, 1)
                    for s in range(SLOTS):
                        pool.memset(qq[s][:], 0.0).then_inc(filled, 1)
                        pool.wait_ge(filled, 3 * s + 1)
                        pool.memset(kc[s][PROWS:128], 1.0).then_inc(filled, 1)
                        pool.wait_ge(filled, 3 * s + 2)
                        pool.memset(ks[s][PROWS:128], 1.0).then_inc(filled, 1)
                        pool.wait_ge(filled, 3 * s + 3)
                        if s == 0:
                            pool.wait_ge(ld_base, 16)
                            pool.wait_ge(ld_masks, 16)
                            for i, (dst, src) in enumerate(((ident_b, ident), (mask_kq, masks_f[:, 0, :]),
                                                            (mask_qk, masks_f[:, 1, :]))):
                                pool.tensor_copy(dst[:], src).then_inc(masks_b, 1)
                                pool.wait_ge(masks_b, i + 1)

                    def low_part(j):
                        wait_parts_left(pool, j)
                        pool.wait_ge(j_mid, j + 1)
                        pool.tensor_tensor(parts_of(j)[2], rem[:, j % 2, 0:pieces[j][2]], parts_of(j)[1],
                                           ALU.subtract).then_inc(c_low, 1)

                    def values_out(b):
                        pool.wait_ge(v_sb, values_done(b))
                        if b == 1:
                            pool.wait_ge(v_out, 16)
                        pool.dma_start(vc_scr[b].rearrange("g p n -> p g n"),
                                       vst[:, b % 2].rearrange("p g t n -> p g (t n)")).then_inc(v_out, 16)

                    for gi, (kind, b) in enumerate(groups):
                        if kind == "kc":
                            for j in range(last_piece[gi] - 3, last_piece[gi] + 1):
                                low_part(j)
                            values_out(b)
                        elif kind == "ks":
                            pool.wait_ge(v_sb, X_VALUES)
                            pool.dma_start(vs_scr.rearrange("b g p n -> p (b g) n"),
                                           vss[:].rearrange("p b g t n -> p (b g) (t n)")).then_inc(w_out, 16)
                    pool.wait_ge(v_out, 16 * NB)

                @block.tensor
                def _(pe):
                    def keys(j):
                        gi, c0, w = pieces[j]
                        kind, b = groups[gi]
                        if j >= 2:
                            pe.wait_ge(j_rem, j - 1)
                        if kind == "kc":
                            pe.wait_ge(ld_ctx[b], 16)
                            pe.matmul(ps[:, j % 2, 0:w], wck, ctx_t[:, b, c0:c0 + w], start=True, stop=True).then_inc(j_ps, 1)
                        else:
                            pe.wait_ge(x_ready, c0 // CH + 1)
                            pe.matmul(ps[:, j % 2, 0:w], wx[kind], X[:, c0:c0 + w], start=True, stop=True).then_inc(j_ps, 1)

                    def values(n):
                        if n >= 2:
                            pe.wait_ge(v_sb, n - 1)
                        b, t0, count = values_order[n] if values_order[n][0] != "x" else (values_order[n][1], None, 2)
                        w = H * VW
                        if t0 is not None:
                            pe.wait_ge(ld_ctx[b], 16)
                        for i in range(count):
                            if t0 is None:
                                last = pe.matmul(ps[:, 2 + n % 2, i * w:(i + 1) * w],
                                                 X[:, (2 * b + i) * 128:(2 * b + i + 1) * 128], wv_x, start=True, stop=True)
                            else:
                                t = t0 + i
                                k = 128 if t < NKT - 1 else KLAST
                                last = pe.matmul(ps[0:k, 2 + n % 2, i * w:(i + 1) * w],
                                                 ctx_t[:, b, t * 128:t * 128 + k], wcv, start=True, stop=True)
                        last.then_inc(v_ps, 1)

                    def scores(b):
                        q = slice(b * TQ, (b + 1) * TQ)
                        for t in range(2):
                            o = ps[:, 4 + b, t * TQ:(t + 1) * TQ]
                            pe.matmul(o, kt[:, b * TQ + t * 128:b * TQ + (t + 1) * 128], qt[:, q],
                                      start=True, stop=False)
                            last = pe.matmul(o, half_neg, qsq[:, q], start=False, stop=True)
                        last.then_inc(g_s, 1)

                    def attend(b):
                        pe.wait_ge(g_p, b + 1)
                        for i in range(2):
                            for t in range(2):
                                last = pe.matmul(ps[:, 4 + b, i * (C + 1):(i + 1) * (C + 1)],
                                                 p0[:, b, t * TQ + i * 128:t * TQ + (i + 1) * 128], v0[:, 2 * b + t, :],
                                                 start=(t == 0), stop=(t == 1))
                        last.then_inc(g_o, 1)

                    def turn(c):
                        pe.wait_ge(g_otok, 2 * c + 2)
                        for i in range(4):
                            last = pe.transpose(ps[:, 4 + 2 * c, i * 128:(i + 1) * 128], o_tok[:, 4 * c + i, :], ident)
                        last.then_inc(g_t, 1)

                    def project(c):
                        pe.wait_ge(g_ochan, c + 1)
                        pe.matmul(ps[:, 5 + 2 * c, :], wo0, o_chan[:, c * CH:(c + 1) * CH],
                                  start=True, stop=True).then_inc(g_wo, 1)

                    pe.wait_ge(ld_x, 16)
                    pe.wait_ge(ld_att, 16)
                    for i, w in enumerate((wq0, wk0)):
                        for c in range(NCH):
                            pe.matmul(ps[:, 4 + 2 * i + c, :], w, X[:, c * CH:(c + 1) * CH],
                                      start=True, stop=True).then_inc(g_qk, 1)
                    for t in range(8):
                        last = pe.matmul(ps[:, 2 + t // 4, (t % 4) * C:(t % 4 + 1) * C],
                                         X[:, t * 128:(t + 1) * 128], wv0, start=True, stop=True)
                        if t % 4 == 3:
                            last.then_inc(g_v, 1)
                    pe.wait_ge(ld_proj, 16)
                    pe.wait_ge(ones_set, 1)
                    keys(0)
                    keys(1)
                    pe.wait_ge(g_v_sb, 2)
                    pe.wait_ge(g_sq, 4)
                    for t in range(8):
                        last = pe.matmul(ps[:, 3, t:t + 1], ksq[:, t * 128:(t + 1) * 128], neg_col, start=True, stop=True)
                    last.then_inc(g_ksum, 1)
                    scores(0)
                    values(0)
                    pe.wait_ge(g_ksum_sb, 1)
                    for b in range(1, NB):
                        scores(b)
                        values(b)
                    keys(2)
                    attend(0)
                    keys(3)
                    attend(1)
                    values(4)
                    attend(2)
                    attend(3)
                    pe.wait_ge(ld_base, 16)
                    turn(0)
                    values(5)
                    turn(1)
                    keys(4)
                    project(0)
                    values(6)
                    project(1)
                    keys(5)
                    pe_ln(0)
                    values(7)
                    pe_ln(1)
                    keys(6)
                    pe_ln2(0)
                    values(8)
                    pe_ln2(1)
                    keys(7)
                    values(9)
                    for i in range(4):
                        keys(8 + i)
                        values(10 + i)
                    keys(12)
                    keys(13)
                    for i in range(4):
                        keys(14 + i)
                        values(14 + i)
                    values(18)
                    for i in range(4):
                        keys(18 + i)
                        values(19 + i)
                    values(23)

                @block.scalar
                def _(act):
                    act.dma_start(proj_w[:], a["proj_w"]).then_inc(ld_proj, 16)
                    for b in range(NB):
                        act.dma_start(ctx_t[0:CC, b, :], a["ctx_t"][:, b, :]).then_inc(ld_ctx[b], 16)
                    act.preload_act_table_set(EXP_LN)
                    act.wait_ge(ld_base, 16)
                    for i in range(4):
                        act.wait_ge(g_qk, i + 1)
                        dst, c = (qt, kt)[i // 2], i % 2
                        act.activation(dst[:, c * CH:(c + 1) * CH], ps[:, 4 + i, :], ACT.Identity,
                                       bias=col[("bq0", "bk0")[i // 2]]).then_inc(g_qk_sb, 1)
                    for i in (2, 3, 0, 1):
                        act.wait_ge(g_qk_sb, i + 1)
                        src, dst, c = (qt, kt)[i // 2], (qsq, ksq)[i // 2], i % 2
                        act.activation(dst[:, c * CH:(c + 1) * CH], src[:, c * CH:(c + 1) * CH],
                                       ACT.Square).then_inc(g_sq, 1)

                    def high(j):
                        gi, c0, w = pieces[j]
                        kind, b = groups[gi]
                        act.wait_ge(j_ps, j + 1)
                        wait_parts_left(act, j)
                        if kind == "kc":
                            act.activation(parts_of(j)[0], ps[:, j % 2, 0:w], ACT.Copy).then_inc(j_hi, 1)
                        else:
                            act.activation(parts_of(j)[0], ps[:, j % 2, 0:w], ACT.Identity,
                                           bias=col[b]).then_inc(j_hi, 1)

                    def middle(j):
                        act.wait_ge(j_rem, j + 1)
                        act.activation(parts_of(j)[1], rem[:, j % 2, 0:pieces[j][2]], ACT.Copy).then_inc(j_mid, 1)

                    def numerators(b):
                        act.wait_ge(g_s, b + 1)
                        for t in range(2):
                            act.activation(e1[:, b % 2, t * TQ:(t + 1) * TQ], ps[:, 4 + b, t * TQ:(t + 1) * TQ],
                                           ACT.Exp, bias=ksum[:, 2 * b + t:2 * b + t + 1], scale=2.0).then_inc(g_e1, 1)
                        act.wait_ge(g_e1, 2 * (b + 1))
                        act.activation(p0[:, b, :], e1[:, b % 2, :], ACT.Exp).then_inc(g_p, 1)

                    def turned(c):
                        act.wait_ge(g_t, c + 1)
                        act.activation(o_chan[:, c * CH:(c + 1) * CH], ps[:, 4 + 2 * c, :], ACT.Copy).then_inc(g_ochan, 1)

                    high(0)
                    high(1)
                    act.wait_ge(g_ksum_sb, 1)
                    numerators(0)
                    middle(0)
                    numerators(1)
                    middle(1)
                    numerators(2)
                    numerators(3)
                    high(2)
                    middle(2)
                    high(3)
                    middle(3)
                    turned(0)
                    turned(1)
                    high(4)
                    middle(4)
                    act_ln(0)
                    high(5)
                    act_ln(1)
                    middle(5)
                    act_ln2(0)
                    high(6)
                    act_ln2(1)
                    middle(6)
                    high(7)
                    for j in range(8, len(pieces)):
                        middle(j - 1)
                        high(j)
                    middle(len(pieces) - 1)

                @block.vector
                def _(dve):
                    dve.memset(ctx_t[CC:128], 1.0).then_inc(ones_set, 1)
                    dve.memset(v0[:, :, C:C + 1], 1.0)
                    dve.wait_ge(ld_att, 16)
                    for i in range(2):
                        dve.wait_ge(g_v, i + 1)
                        dve.tensor_tensor(v0[:, 4 * i:4 * i + 4, 0:C], ps[:, 2 + i, :].rearrange("p (t n) -> p t n", t=4),
                                          bv0.unsqueeze(1).to_broadcast([128, 4, C]), ALU.add).then_inc(g_v_sb, 1)

                    def rest(j):
                        gi, c0, w = pieces[j]
                        kind, b = groups[gi]
                        dve.wait_ge(j_hi, j + 1)
                        if j >= 2:
                            dve.wait_ge(j_mid, j - 1)
                            dve.wait_ge(*lows(j - 2))
                        high = parts_of(j)[0]
                        if kind == "kc":
                            dve.tensor_tensor(rem[:, j % 2, 0:w], ps[:, j % 2, 0:w], high, ALU.subtract).then_inc(j_rem, 1)
                        else:
                            dve.scalar_tensor_tensor(out=rem[:, j % 2, 0:w], in0=ps[:, j % 2, 0:w], scalar=col[b],
                                                     in1=high, op0=ALU.add, op1=ALU.subtract).then_inc(j_rem, 1)

                    def low_part(j):
                        dve.wait_ge(j_mid, j + 1)
                        dve.tensor_tensor(parts_of(j)[2], rem[:, j % 2, 0:pieces[j][2]], parts_of(j)[1],
                                          ALU.subtract).then_inc(x_low, 1)

                    def values(n):
                        dve.wait_ge(v_ps, n + 1)
                        if values_order[n][0] == "x":
                            b = values_order[n][1]
                            dve.tensor_tensor(vss[:, b], ps[:, 2 + n % 2, 0:2 * H * VW].rearrange(
                                "p (t g n) -> p g t n", t=2, g=NG), bv_x.rearrange("p (g n) -> p g n", g=NG).unsqueeze(
                                    2).to_broadcast([128, NG, 2, 4 * VW]), ALU.add).then_inc(v_sb, 1)
                            return
                        b, t0, count = values_order[n]
                        k = 128 if t0 + count < NKT else KLAST
                        if t0 == 0 and b >= 2:
                            dve.wait_ge(v_out, 32)
                        if n == 4:
                            dve.wait_ge(cleared, 1)
                        dve.tensor_copy(vst[0:k, b % 2, :, t0:t0 + count, :], ps[0:k, 2 + n % 2, 0:count * H * VW].rearrange(
                            "p (t g n) -> p g t n", t=count, g=NG)).then_inc(v_sb, 1)

                    def divide(b):
                        o = ps[:, 4 + b, 0:2 * (C + 1)].rearrange("p (i n) -> p i n", i=2)
                        dve.wait_ge(g_o, b + 1)
                        dve.reciprocal(rden[:, 2 * b:2 * b + 2].unsqueeze(2), o[:, :, C:C + 1]).then_inc(g_rden, 1)
                        dve.wait_ge(g_rden, b + 1)
                        dve.tensor_tensor(o_tok[:, 2 * b:2 * b + 2, :], o[:, :, 0:C],
                                          rden[:, 2 * b:2 * b + 2].unsqueeze(2).to_broadcast([128, 2, C]),
                                          ALU.mult).then_inc(g_otok, 1)

                    def residual(c):
                        dve.wait_ge(g_wo, c + 1)
                        dve.scalar_tensor_tensor(out=R[:, c * CH:(c + 1) * CH], in0=ps[:, 5 + 2 * c, :],
                                                 scalar=col["bo0"], in1=X[:, c * CH:(c + 1) * CH],
                                                 op0=ALU.add, op1=ALU.add).then_inc(g_r, 1)

                    rest(0)
                    rest(1)
                    dve.wait_ge(g_ksum, 1)
                    dve.tensor_copy(ksum[:], ps[:, 3, 0:8]).then_inc(g_ksum_sb, 1)
                    for n in range(4):
                        values(n)
                    divide(0)
                    rest(2)
                    divide(1)
                    rest(3)
                    values(4)
                    divide(2)
                    divide(3)
                    values(5)
                    residual(0)
                    rest(4)
                    values(6)
                    residual(1)
                    rest(5)
                    values(7)
                    rest(6)
                    dve_ln(0)
                    values(8)
                    dve_ln(1)
                    rest(7)
                    values(9)
                    for i in range(6):
                        rest(8 + i)
                        if i > 0:
                            low_part(7 + i)
                        if i < 4:
                            values(10 + i)
                    low_part(13)
                    for i in range(4):
                        rest(14 + i)
                        values(14 + i)
                    values(18)
                    for i in range(4):
                        rest(18 + i)
                        values(19 + i)
                    values(23)

        sem_owner[0] = persistent
        outputs_scope = ExitStack()
        persistent.enter_context(outputs_scope)
        later = {n: outputs_scope.enter_context(nc.sbuf_tensor(f"w_{n}", a[n].shape, F32)) for n in FOR_BLOCK_3}
        later["ident"] = ident
        rden_rows = outputs_scope.enter_context(nc.sbuf_tensor("rden_rows", [12, NU, 2 * TQ], BF16))
        rden_in = persistent.enter_context(nc.semaphore("rden_in"))
        o_all = outputs_scope.enter_context(
            nc.sbuf_tensor("o_all", [128, NU, 2 * TQ], F32))
        with ExitStack() as st:
            def sb(name, shape, dt=F32):
                return st.enter_context(nc.sbuf_tensor(name, shape, dt))

            prob = sb("prob", [128, 3, 4, TQ])
            raw, raw_high, raw_low = ([sb(f"{n}{r}", [128, 3 * DFF], dt) for r in range(2)]
                                      for n, dt in (("raw", F32), ("raw_high", F32R), ("raw_low", F32R)))
            DEN = 4 * (NU - 1) * 2 * TQ // 128
            den = sb("den", [128, 3, DEN])
            den_part = sb("den_part", [128, 3, DEN], BF16)
            nm_a = sb("nm_a", [128, 8])
            nm_b = sb("nm_b", [128, 8])
            nm = sb("nm", [128, 2, 2, 4])
            mrow = [sb(f"mrow{s}", [16, 2, 128], BF16) for s in range(SLOTS)]
            s1 = st.enter_context(nc.psum_tensor("s1", [128, 4, 512], F32))
            s2 = st.enter_context(nc.psum_tensor("s2", [128, 3, 512], F32))
            o_ps = st.enter_context(nc.psum_tensor("o_ps", [128, 2 * TQ], F32))
            (den_in, den_done, later_in, s1_ready, s1_read, nm_ready, nm_t, m1_done, mrow_ready, s2_ready, exp_done, av_done,
             o_copied) = sems(st, "den_in", "den_done", "later_in", "s1_ready", "s1_read", "nm_ready", "nm_t", "m1_done",
                              "mrow_ready", "s2_ready", "exp_done", "av_done", "o_copied")
            raw_in, raw_split, *parts_left = sems(st, "raw_in", "raw_split", "parts_left0", "parts_left1")
            max_in = sems(st, *[f"max_in{s}" for s in range(SLOTS)])
            MAX_INC = 16 * 4
            HALVES = 2 * NST
            LOOPED = 4
            JOBS = 16
            S2_FREE, P_FREE, S1_FREE = 3, 3, 2

            with nc.Block() as block:
                @block.gpsimd
                def _(pool):
                    for done in first_named:
                        pool.sem_clear(done)
                    pool.dma_start(b3[:], a["b3"]).then_inc(later_in, 16)
                    for n in FOR_BLOCK_3:
                        pool.dma_start(later[n][:], a[n]).then_inc(later_in, 16)
                    pool.wait_ge(later_in, 16 * (len(FOR_BLOCK_3) + 1))
                    for e in range(E):
                        r = e % 2
                        if e >= 2:
                            pool.wait_ge(parts_left[r], 32 * (e // 2))
                        pool.dma_start(raw[r][:], a["wexp"][e, :, 0:3 * DFF]).then_inc(raw_in, 16)
                        pool.wait_ge(raw_in, 16 * (e + 1))
                        pool.tensor_copy(raw_high[r][:], raw[r][:]).then_inc(raw_split, 1)
                        pool.wait_ge(raw_split, 2 * e + 1)
                        pool.tensor_tensor(raw_low[r][:], raw[r][:], raw_high[r][:], ALU.subtract).then_inc(raw_split, 1)
                        pool.wait_ge(raw_split, 2 * e + 2)
                        for part, src in enumerate((raw_high[r], raw_low[r])):
                            pool.dma_start(exp_scr[e, part], src[:].bitcast(F32)).then_inc(parts_left[r], 16)
                    for r in range(2):
                        pool.wait_ge(parts_left[r], 16 * E)

                @block.sync
                def _(sp):
                    def max_rows(s):
                        for e in range(2):
                            for part in range(2):
                                at = PROWS + 2 * e + part
                                sp.dma_start(qq[s][at:at + 1, e, :, :, :].rearrange("o k j (t q) -> o (k j t) q", t=2),
                                             mrow[s][8 * e:8 * e + 8, part, :]).then_inc(max_in[s], 16)

                    def step(i, u):
                        sp.wait_ge(av_done, i * (3 * NST) + (P_FREE + NST * u))
                        load_unit(sp, i * 3 + (u + 2), (u + 2) % SLOTS)
                        sp.wait_ge(mrow_ready, i * 3 + (u + 2))
                        max_rows((u + 1) % SLOTS)

                    load_unit(sp, 1, 1)
                    for s in range(2):
                        sp.wait_ge(j_out[s], 16 * 6)
                    sp.wait_ge(mrow_ready, 1)
                    max_rows(0)
                    with sp.Fori(0, LOOPED) as i:
                        for u in range(SLOTS):
                            step(i, u)
                    for n in range(SLOTS * LOOPED, NU - 2):
                        step(n // SLOTS, n % SLOTS)
                    sp.wait_ge(mrow_ready, NU)
                    max_rows((NU - 1) % SLOTS)
                    sp.wait_ge(o_copied, NU)
                    sp.dma_start(den[:, 0, :], o_all[HD:128:32, 0:NU - 1, :]).then_inc(den_in, 16)
                    sp.wait_ge(den_done, 5)
                    for part in range(3):
                        sp.dma_start(rden_rows[4 * part:4 * part + 4, 0:NU - 1, :], den_part[:, part, :]).then_inc(rden_in, 16)
                    sp.wait_ge(rden_in, 48)

                @block.tensor
                def _(pe):
                    pe.sem_inc(av_done, P_FREE)

                    def score_half(s, k, base):
                        j, e, t = k // 8, (k // 4) % 2, (k // 2) % 2
                        pe.wait_ge(s1_read, base[0] + (base[1] + k + 1))
                        q = qq[s][0:PROWS, e, 0, j, t * 128:(t + 1) * 128]
                        if k % 2 == 0:
                            for i in range(2):
                                last = pe.matmul(s1[:, i, :], q, kc[s][0:PROWS, j, i * 512:(i + 1) * 512],
                                                 start=True, stop=True)
                        else:
                            pe.matmul(s1[:, 2, :], q, kc[s][0:PROWS, j, 1024:1536], start=True, stop=True)
                            pe.matmul(s1[:, 3, 0:TK - 1536], q, kc[s][0:PROWS, j, 1536:TK], start=True, stop=True)
                            qs_ = qq[s][0:PROWS, e, 1, j, t * 128:(t + 1) * 128]
                            w = 128 * (t + 1)
                            pe.matmul(s1[:, 3, 128:128 + w], qs_, ks[s][0:PROWS, j, 0:w], start=True, stop=False)
                            last = pe.matmul(s1[:, 3, w:w + 128], ident_b[:], mask_qk[:], start=False, stop=True)
                        last.then_inc(s1_ready, 1)

                    def scores_t(s, t, j, base):
                        k = 2 * t + j
                        pe.wait_ge(exp_done, base[0] + (base[1] + k + 1))
                        bank = k % 3
                        if t < NKT:
                            m = 128 if t < NKT - 1 else KLAST
                            last = pe.matmul(s2[0:m, bank, :].rearrange("p (e q) -> p e q", e=2), kc[s][0:KROWS, j, t * 128:t * 128 + m],
                                             qq[s][0:KROWS, :, 0, j, :],
                                             start=True, stop=True)
                        else:
                            q0 = 128 * (t - NKT)
                            w = TQ - q0
                            pe.matmul(s2[:, bank, 0:2 * w].rearrange("p (e q) -> p e q", e=2),
                                      ks[s][0:KROWS, j, q0:q0 + 128], qq[s][0:KROWS, :, 1, j, q0:TQ],
                                      start=True, stop=False)
                            for e in range(2):
                                last = pe.matmul(s2[:, bank, e * w:e * w + 128], ident_b[:], mask_kq[:],
                                                 start=False, stop=(e == 1))
                        last.then_inc(s2_ready, 1)

                    def outputs(s, t, base):
                        pe.wait_ge(exp_done, base[0] + (base[1] + S2_FREE + 2 * t + 2))
                        k = KLAST if t == NKT - 1 else 128
                        kind, q0 = (0, 0) if t < NKT else (1, 128 * (t - NKT))
                        for hh in range(4):
                            last = pe.matmul(o_ps[32 * hh:32 * hh + VW, kind * TQ + q0:(kind + 1) * TQ],
                                             vv[s][0:k, t, hh * VW:(hh + 1) * VW],
                                             prob[0:k, t % 3, 2 * (hh % 2) + hh // 2, q0:TQ],
                                             start=t in (0, NKT), stop=t in (NKT - 1, NST - 1))
                        last.then_inc(av_done, 1)

                    def unit(i, u, n=None):
                        nxt, after = (u + 1) % SLOTS, (u + 2) % SLOTS
                        has_next, has_after = n is None or n + 1 < NU, n is None or n + 2 < NU
                        pe.wait_ge(max_in[u], i * MAX_INC + MAX_INC)
                        s2_base = (i * (3 * HALVES), u * HALVES)
                        next_base = (i * (3 * JOBS), (u + 1) * JOBS)
                        after_base = (i * (3 * JOBS), (u + 2) * JOBS)
                        scores_t(u, 0, 0, s2_base)
                        scores_t(u, 0, 1, s2_base)
                        if has_next:
                            score_half(nxt, 8, next_base)
                        for t in range(NST):
                            if t + 1 < NST:
                                scores_t(u, t + 1, 0, s2_base)
                            if t < 7 and has_next:
                                score_half(nxt, 9 + t, next_base)
                            if t == 7 and has_after:
                                pe.wait_ge(slot_in[after], i * SLOT_INC + SLOT_INC * (1 if u == 0 else 2))
                                score_half(after, 0, after_base)
                            if t + 1 < NST:
                                scores_t(u, t + 1, 1, s2_base)
                            if t == 0:
                                pe.wait_ge(o_copied, i * 3 + (u + 1))
                            outputs(u, t, s2_base)
                            if t == 7 and has_next:
                                turn_maxima(i * 3 + (u + 2))
                            if t == 8 and has_next:
                                pe.wait_ge(mrow_ready, i * 3 + (u + 2))
                            if t >= 8 and has_after:
                                score_half(after, t - 7, after_base)

                    def turn_maxima(count):
                        pe.wait_ge(nm_ready, count)
                        pe.transpose(s1[0:16, 3, 384:512], nm[:].rearrange("p e k i -> p (e k i)"),
                                     ident).then_inc(nm_t, 1)

                    pe.wait_ge(slot_in[0], SLOT_INC)
                    for k in range(JOBS):
                        score_half(0, k, (0, 0))
                    pe.wait_ge(slot_in[1], SLOT_INC)
                    score_half(1, 0, (0, JOBS))
                    turn_maxima(1)
                    pe.wait_ge(mrow_ready, 1)
                    for k in range(1, 8):
                        score_half(1, k, (0, JOBS))
                    with pe.Fori(0, LOOPED) as i:
                        for u in range(SLOTS):
                            unit(i, u)
                    for n in range(SLOTS * LOOPED, NU):
                        unit(n // SLOTS, n % SLOTS, n)

                @block.scalar
                def _(act):
                    act.preload_act_table_set(EXP_LN)
                    act.sem_inc(exp_done, S2_FREE)

                    def unit(i, u):
                        for k in range(HALVES):
                            t, half = k // 2, k % 2
                            if half == 0:
                                act.wait_ge(av_done, i * (3 * NST) + (u * NST + t + 1))
                            act.wait_ge(s2_ready, i * (3 * HALVES) + (u * HALVES + k + 1))
                            p = KLAST if t == NKT - 1 else 128
                            q0 = 0 if t < NKT else 128 * (t - NKT)
                            w = TQ - q0
                            act.activation(prob[0:p, t % 3, 2 * half:2 * half + 2, q0:TQ],
                                           s2[0:p, k % 3, 0:2 * w].rearrange("p (i q) -> p i q", i=2),
                                           ACT.Exp, scale=SCALE).then_inc(exp_done, 1)
                        act.wait_ge(av_done, i * (3 * NST) + (P_FREE + (u + 1) * NST))
                        act.activation(o_all[:, bass.ds(i * 3 + u, 1), :].rearrange("p o q -> p (o q)"), o_ps[:],
                                       ACT.Copy).then_inc(o_copied, 1)

                    with act.Fori(0, NU // SLOTS) as i:
                        for u in range(SLOTS):
                            unit(i, u)
                    unit(NU // SLOTS, 0)

                @block.vector
                def _(dve):
                    dve.memset(o_ps[:], 0.0).then_inc(o_copied, 1)
                    dve.sem_inc(s1_read, S1_FREE)

                    def reduce_half(i3, u, k):
                        j, e, t = k // 8, (k // 4) % 2, (k // 2) % 2
                        i = 4 * e + 2 * j + t
                        dve.wait_ge(s1_ready, i3 * (3 * JOBS) + (u * JOBS + k + 1))
                        if k % 2 == 0:
                            dve.tensor_reduce(nm_a[:, i:i + 1], s1[:, 0:2, :], AX.XY, ALU.max,
                                              negate=True).then_inc(s1_read, 1)
                        else:
                            dve.tensor_reduce(nm_b[:, i:i + 1], s1[:, 2:4, :].rearrange("p b n -> p (b n)")[:, 0:TK - 1024],
                                              AX.X, ALU.max, negate=True)
                            dve.tensor_reduce(nm[:, e, 1, 2 * j + t:2 * j + t + 1], s1[:, 3, 128:128 + 128 * (t + 1)],
                                              AX.X, ALU.max, negate=True).then_inc(s1_read, 1)

                    def unit(i3, u, last_unit=False):
                        for k in range(1, JOBS):
                            reduce_half(i3, u, k)
                        dve.wait_ge(s1_read, i3 * (3 * JOBS) + (S1_FREE + (u + 1) * JOBS))
                        dve.tensor_tensor(nm[:, :, 0, :], nm_a[:].rearrange("p (e i) -> p e i", e=2),
                                          nm_b[:].rearrange("p (e i) -> p e i", e=2), ALU.min).then_inc(nm_ready, 1)
                        if not last_unit:
                            dve.wait_ge(nm_ready, i3 * 3 + (u + 1))
                            reduce_half(i3, u + 1, 0)
                        dve.wait_ge(nm_t, i3 * 3 + (u + 1))
                        dve.tensor_copy(mrow[u][:, 0, :], s1[0:16, 3, 384:512]).then_inc(m1_done, 1)
                        dve.wait_ge(m1_done, i3 * 3 + (u + 1))
                        dve.tensor_tensor(mrow[u][:, 1, :], s1[0:16, 3, 384:512], mrow[u][:, 0, :],
                                          ALU.subtract).then_inc(mrow_ready, 1)

                    reduce_half(0, 0, 0)
                    with dve.Fori(0, NU // SLOTS) as i3:
                        for u in range(SLOTS):
                            unit(i3, u)
                    unit(NU // SLOTS, 0, last_unit=True)
                    dve.wait_ge(den_in, 16)
                    reciprocals(dve, den, den_part, den_done)

        first_sems.close()
        emit_rest(nc, a, out, keep, sems, ln_parts, X, R, ctx_t, col, o_all, (outputs_scope, slots_scope), later, rden_rows, rden_in,
                  (up_w, down_w, exp_bias, up_in, down_in, exp_scr), b3, comb_scr)


def emit_rest(nc, a, out, keep, sems, ln_parts, X, R, ctx_t, col, o_all, scopes, later, rden_rows, rden_in, experts, b3,
              comb_scr):
    up_w, down_w, exp_bias, up_in, down_in, exp_scr = experts
    parts_of_all = exp_scr.rearrange("e part p n -> part e p n")

    def load_up(sp, e, s):
        for part in range(2):
            src = parts_of_all[part, bass.ds(e, 1), :, 0:2 * DFF].rearrange("o p n -> (o p) n")
            sp.dma_start(up_w[s][part][:].bitcast(F32), src).then_inc(up_in[s], 16)
        sp.dma_start(exp_bias[s][:], a["wexp"][bass.ds(e, 1), :, 3 * DFF:].rearrange("o p n -> (o p) n")).then_inc(up_in[s], 16)

    def load_down(sp, e, s):
        for part in range(2):
            src = parts_of_all[part, bass.ds(e, 1), :, 2 * DFF:].rearrange("o p n -> (o p) n")
            sp.dma_start(down_w[s][part][:].bitcast(F32), src).then_inc(down_in[s], 16)

    with ExitStack() as st:
        def sb(name, shape, dt=F32):
            return st.enter_context(nc.sbuf_tensor(name, shape, dt))

        spread = sb("spread", [12, 128], BF16)
        den = sb("den3", [128, 3, 16])
        den_part = sb("den_part3", [128, 3, 16], BF16)
        wp, wg, ident, iota = (later[n] for n in ("wp", "wg", "ident", "iota"))
        y2 = sb("y2", [128, 4, 512])
        y = sb("y", [128, 4, TQ])
        gout = sb("gout", [128, 8, E])
        top = sb("top", [128, 8, 8])
        idx = sb("idx", [128, 8, 8], U32)
        idxf = sb("idxf", [128, 8, 8])
        w12 = sb("w12", [128, 8, 4])
        w2 = sb("w2", [128, 8, 1])
        c1 = sb("c1", [128, 8, E])
        c2 = sb("c2", [128, 8, E])
        comb = sb("comb", [128, 8, E])
        comb_t = sb("comb_t", [E, T])
        ps = st.enter_context(nc.psum_tensor("ps3", [128, 8, 512], F32))
        (den_in, den_done, spread_b, spreads, y2s, ys, proj, r_ready, gates, chain, expd, combs, comb_ps, comb_sb, stored) = sems(
            st, "den_in3", "den_done3", "spread_b", "spreads", "y2s", "ys", "proj", "b3_r", "gates", "b3_chain", "expd", "combs",
            "comb_ps", "comb_sb", "stored")
        pe_ln, pe_ln2, act_ln, act_ln2, dve_ln, x_ready = ln_parts(st, "ln2", ps[:, 4:6, :], ps[:, 6:8, :], r_ready)

        with nc.Block() as block:
            @block.sync
            def _(sp):
                sp.dma_start(den[:, 0, :], o_all[HD:128:32, NU - 1, :]).then_inc(den_in, 16)
                for s in range(2):
                    load_up(sp, s, s)
                    load_down(sp, s, s)
                sp.wait_ge(den_done, 5)
                for part in range(3):
                    sp.dma_start(rden_rows[4 * part:4 * part + 4, NU - 1, :], den_part[:, part, :]).then_inc(rden_in, 16)
                sp.wait_ge(comb_sb, 2)
                sp.dma_start(comb_scr, comb_t[:]).then_inc(stored, 16)
                sp.wait_ge(stored, 16)

            @block.gpsimd
            def _(pool):
                for n in range(NU):
                    pool.wait_ge(y2s, n + 1)
                    if n >= 4:
                        pool.wait_ge(proj, n - 3)
                    pool.tensor_tensor(y[:, n % 4, :], y2[:, n % 4, 0:TQ], y2[:, n % 4, TQ:2 * TQ],
                                       ALU.add).then_inc(ys, 1)

            @block.tensor
            def _(pe):
                def denominators(n):
                    if n >= 2:
                        pe.wait_ge(y2s, n - 1)
                    if n == NU - 1:
                        pe.wait_ge(rden_in, 96)
                    pe.matmul(ps[:, n % 2, :], spread[:], rden_rows[:, n, :], start=True, stop=True).then_inc(spreads, 1)

                pe.wait_ge(spread_b, 1)
                denominators(0)
                denominators(1)
                for n in range(NU):
                    b, g = n // NG, n % NG
                    if n + 2 < NU:
                        denominators(n + 2)
                    pe.wait_ge(ys, n + 1)
                    last = pe.matmul(ps[:, 2 + b // 2, (b % 2) * TQ:(b % 2 + 1) * TQ], wp[:, g, :], y[:, n % 4, :],
                                     start=(g == 0), stop=(g == NG - 1))
                    last.then_inc(proj, 1)
                pe_ln(0)
                pe_ln(1)
                pe_ln2(0)
                pe_ln2(1)
                for t in range(8):
                    if t % 4 == 0:
                        pe.wait_ge(x_ready, t // 4 + 1)
                    last = pe.matmul(ps[:, 0, t * E:(t + 1) * E], X[:, t * 128:(t + 1) * 128], wg[:],
                                     start=True, stop=True)
                last.then_inc(gates, 1)
                pe.wait_ge(combs, 1)
                for t in range(8):
                    last = pe.transpose(ps[0:E, 2 + t // 4, (t % 4) * 128:(t % 4 + 1) * 128], comb[:, t, :], ident)
                    if t % 4 == 3:
                        last.then_inc(comb_ps, 1)

            @block.scalar
            def _(act):
                act.preload_act_table_set(EXP_LN)
                act_ln(0)
                act_ln(1)
                act_ln2(0)
                act_ln2(1)
                act.wait_ge(chain, 18)
                act.activation(w12[:, :, 1:2], w12[:, :, 0:1], ACT.Exp).then_inc(expd, 1)

            @block.vector
            def _(dve):
                dve.tensor_copy(spread[:], later["spread"][0:12, :]).then_inc(spread_b, 1)
                for n in range(NU):
                    if n == 2:
                        dve.wait_ge(den_in, 16)
                        reciprocals(dve, den, den_part, den_done)
                    dve.wait_ge(spreads, n + 1)
                    if n >= 4:
                        dve.wait_ge(ys, n - 3)
                    dve.tensor_tensor(y2[:, n % 4, :], o_all[:, n, :], ps[:, n % 2, :], ALU.mult).then_inc(y2s, 1)
                    if n % 8 == 7:
                        c = n // 8
                        dve.wait_ge(proj, n + 1)
                        dve.scalar_tensor_tensor(out=R[:, c * CH:(c + 1) * CH], in0=ps[:, 2 + c, :], scalar=col["bp"],
                                                 in1=X[:, c * CH:(c + 1) * CH], op0=ALU.add,
                                                 op1=ALU.add).then_inc(r_ready, 1)
                dve_ln(0)
                dve_ln(1)
                count = [0]

                def link(ins):
                    count[0] += 1
                    ins.then_inc(chain, 1)
                    dve.wait_ge(chain, count[0])

                dve.wait_ge(gates, 1)
                link(dve.tensor_copy(gout[:].rearrange("p t e -> p (t e)"), ps[:, 0, 0:8 * E]))
                for t in range(8):
                    link(dve.max(top[:, t, :], gout[:, t, :]))
                for t in range(8):
                    link(dve.max_index(idx[:, t, :], top[:, t, :], gout[:, t, :]))
                link(dve.tensor_tensor(w12[:, :, 0:1], top[:, :, 1:2], top[:, :, 0:1], ALU.subtract))
                link(dve.tensor_copy(idxf[:], idx[:]))
                link(dve.tensor_tensor(c1[:], iota[:].rearrange("p (t e) -> p t e", t=8),
                                       idxf[:, :, 0:1].to_broadcast([128, 8, E]), ALU.is_equal))
                link(dve.tensor_tensor(c2[:], iota[:].rearrange("p (t e) -> p t e", t=8),
                                       idxf[:, :, 1:2].to_broadcast([128, 8, E]), ALU.is_equal))
                dve.wait_ge(expd, 1)
                link(dve.tensor_scalar(w12[:, :, 2:3], w12[:, :, 1:2], 1.0, None, ALU.add))
                link(dve.reciprocal(w12[:, :, 3:4], w12[:, :, 2:3]))
                link(dve.tensor_tensor(w2[:], w12[:, :, 1:2], w12[:, :, 3:4], ALU.mult))
                link(dve.tensor_tensor(c1[:], c1[:], w12[:, :, 3:4].to_broadcast([128, 8, E]), ALU.mult))
                link(dve.tensor_tensor(c2[:], c2[:], w2[:].to_broadcast([128, 8, E]), ALU.mult))
                dve.tensor_tensor(comb[:], c1[:], c2[:], ALU.add).then_inc(combs, 1)
                for c in range(NCH):
                    dve.wait_ge(comb_ps, c + 1)
                    dve.tensor_copy(comb_t[:, c * CH:(c + 1) * CH], ps[0:E, 2 + c, :]).then_inc(comb_sb, 1)

    for scope in scopes:
        scope.close()
    later.update({n: keep(f"w_{n}", a[n].shape) for n in LATER})
    TKE = TK + TK % 2
    ctx_2 = keep("ctx_2", [2 * CC, NB, TKE], F32R)

    with ExitStack() as st:
        def sb(name, shape, dt=F32):
            return st.enter_context(nc.sbuf_tensor(name, shape, dt))

        NF = DFF // 128
        comb_bc = [sb(f"comb_bc{s}", [128, T]) for s in range(2)]
        comb_r = sb("comb_r", [E, T])
        ctx_low = sb("ctx_low", [CC, NB, TKE], F32R)
        sg = sb("sg", [128, 2, CH])
        hv = sb("hv", [128, 2, CH])
        whole = sb("whole4", [128, 4, CH])
        hh = [sb(f"hh_{part}", [128, 4, CH], F32R) for part in ("high", "low")]
        xa = [sb(f"x4_{part}", [C, T], F32R) for part in ("high", "low")]
        ps = st.enter_context(nc.psum_tensor("ps4", [128, 8, 512], F32))
        comb_in = sems(st, "comb_in0", "comb_in1")
        (ctx_split, x_split, full_done, high_done, ld, later_in, gv_ready, sg_done, hv_done, h_done, w3_done, out_done, r_ready) = sems(
            st, "ctx_split", "b4_x_split", "b4_full", "b4_high", "b4_ld", "b4_later", "gv_ready", "sg_done", "hv_done", "h_done", "w3_done", "moe_out", "b4_r")
        pe_ln, pe_ln2, act_ln, act_ln2, dve_ln, x_ready = ln_parts(st, "ln3", ps[:, 0:2, :], ps[:, 2:4, :], r_ready)
        GV_FREE, H_FREE = 2, 4
        tiles = [(f, c) for f in range(NF) for c in range(NCH)]
        NT = len(tiles)

        with nc.Block() as block:
            @block.sync
            def _(sp):
                sp.dma_start(comb_r[:], comb_scr).then_inc(ld, 16)

                def load_comb(e, s):
                    sp.dma_start(comb_bc[s][:], comb_scr[bass.ds(e, 1), :].to_broadcast([128, T])).then_inc(comb_in[s], 16)

                load_comb(0, 0)
                load_comb(1, 1)
                with sp.Fori(1, E // 2) as i:
                    for s in range(2):
                        sp.wait_ge(gv_ready, i * (2 * NT) + (s - 1) * NT)
                        sp.wait_ge(full_done, i * (2 * NT) + (s - 1) * NT)
                        load_up(sp, i * 2 + s, s)
                        load_comb(i * 2 + s, s)
                        sp.wait_ge(w3_done, i * (2 * NT) + (H_FREE + (s - 1) * NT))
                        load_down(sp, i * 2 + s, s)

            @block.gpsimd
            def _(pool):
                for n in LATER:
                    pool.dma_start(later[n][:], a[n]).then_inc(later_in, 16)
                for b in range(NB):
                    if TKE > TK:
                        pool.tensor_copy(ctx_2[0:CC, b, TK:], ctx_t[0:CC, b, TK - 1:])
                    pool.tensor_copy(ctx_2[0:CC, b, 0:TK], ctx_t[0:CC, b, :]).then_inc(ctx_split, 1)
                    pool.wait_ge(ctx_split, 2 * b + 1)
                    if TKE > TK:
                        pool.tensor_tensor(ctx_low[:, b, TK:], ctx_t[0:CC, b, TK - 1:], ctx_2[0:CC, b, TK:], ALU.subtract)
                    pool.tensor_tensor(ctx_low[:, b, 0:TK], ctx_t[0:CC, b, :], ctx_2[0:CC, b, 0:TK], ALU.subtract).then_inc(ctx_split, 1)
                    pool.wait_ge(ctx_split, 2 * b + 2)
                pool.dma_start(ctx_2[CC:, :, :].bitcast(F32), ctx_low[:].bitcast(F32)).then_inc(later_in, 16)
                pool.wait_ge(later_in, 16 * (len(LATER) + 1))

            @block.tensor
            def _(pe):
                pe.sem_inc(w3_done, H_FREE)

                def biases():
                    pe.wait_ge(ld, 16)
                    for c in range(NCH):
                        pe.matmul(ps[:, 4 + c, :], b3[:], comb_r[:, c * CH:(c + 1) * CH], start=True, stop=False,
                                  skip_group_check=True)

                def passes(o, weight, x, start):
                    pe.matmul(o, weight[0], x[0], start=start, stop=False, skip_group_check=True)
                    pe.matmul(o, weight[0], x[1], start=False, stop=False, skip_group_check=True)
                    return pe.matmul(o, weight[1], x[0], start=False, stop=True, skip_group_check=True)

                def up(i, s, k):
                    f, c = tiles[k]
                    done = i * (2 * NT) + (s * NT + k + 1)
                    pe.wait_ge(sg_done, done)
                    pe.wait_ge(hv_done, done)
                    for m in range(2):
                        at = m * DFF + f * 128
                        last = passes(ps[:, 2 * m + k % 2, :], [w[:, at:at + 128] for w in up_w[s]],
                                      [x[:, c * CH:(c + 1) * CH] for x in xa], True)
                    last.then_inc(gv_ready, 1)

                def down(i, s, k):
                    f, c = tiles[k]
                    pe.wait_ge(h_done, i * (2 * NT) + (s * NT + k + 1))
                    if k == 0:
                        pe.wait_ge(down_in[s], i * 32 + 32)
                    passes(ps[:, 4 + c, :], [w[:, f * 128:(f + 1) * 128] for w in down_w[s]], [h[:, k, :] for h in hh],
                           False).then_inc(w3_done, 1)

                def expert(i, s, before):
                    pe.wait_ge(up_in[s], i * 48 + 48)
                    for k in range(NT):
                        if before is None and k < NCH:
                            pe.wait_ge(x_split, 2 * k + 2)
                        up(i, s, k)
                        if before is None and k == NCH - 1:
                            biases()
                        if k == NT - 1:
                            down(i, s, 0)
                        elif before:
                            down(*before, k + 1)

                expert(0, 0, None)
                expert(0, 1, (0, 0))
                with pe.Fori(1, E // 2) as i:
                    expert(i, 0, (i - 1, 1))
                    expert(i, 1, (i, 0))
                for k in range(1, NT):
                    down(E // 2 - 1, 1, k)
                pe.wait_ge(r_ready, 2)
                pe_ln(0)
                pe_ln(1)
                pe_ln2(0)
                pe_ln2(1)

            @block.scalar
            def _(act):
                act.sem_inc(sg_done, GV_FREE)
                act.preload_act_table(ACT.Silu)
                with act.Fori(0, E // 2) as i:
                    for s in range(2):
                        act.wait_ge(up_in[s], i * 48 + 48)

                        def gate(k):
                            f = tiles[k][0]
                            act.wait_ge(gv_ready, i * (2 * NT) + (s * NT + k + 1))
                            act.wait_ge(hv_done, i * (2 * NT) + (s * NT + k + 1))
                            act.activation(sg[:, k % 2, :], ps[:, k % 2, :], ACT.Silu,
                                           bias=exp_bias[s][:, f:f + 1]).then_inc(sg_done, 1)

                        def high_part(k):
                            act.wait_ge(full_done, i * (2 * NT) + (s * NT + k + 1))
                            act.activation(hh[0][:, k, :], whole[:, k, :], ACT.Copy).then_inc(high_done, 1)

                        gate(0)
                        for k in range(1, NT):
                            gate(k)
                            high_part(k - 1)
                        high_part(NT - 1)
                act.preload_act_table_set(EXP_LN)
                act_ln(0)
                act_ln(1)
                act_ln2(0)
                act_ln2(1)

            @block.vector
            def _(dve):
                dve.sem_inc(hv_done, GV_FREE)
                for c in range(NCH):
                    at = slice(c * CH, (c + 1) * CH)
                    dve.tensor_copy(xa[0][:, at], X[:, at]).then_inc(x_split, 1)
                    dve.wait_ge(x_split, 2 * c + 1)
                    dve.tensor_tensor(xa[1][:, at], X[:, at], xa[0][:, at], ALU.subtract).then_inc(x_split, 1)
                with dve.Fori(0, E // 2) as i:
                    for s in range(2):
                        dve.wait_ge(comb_in[s], i * 16 + 16)
                        dve.wait_ge(up_in[s], i * 48 + 48)
                        n = i * (2 * NT)

                        def weighted(k):
                            f, c = tiles[k]
                            dve.wait_ge(sg_done, n + (GV_FREE + s * NT + k + 1))
                            dve.scalar_tensor_tensor(out=hv[:, k % 2, :], in0=ps[:, 2 + k % 2, :],
                                                     scalar=exp_bias[s][:, NF + f:NF + f + 1],
                                                     in1=sg[:, k % 2, :], op0=ALU.add, op1=ALU.mult).then_inc(hv_done, 1)
                            dve.wait_ge(hv_done, n + (GV_FREE + s * NT + k + 1))
                            dve.wait_ge(w3_done, n + (s * NT + k + 1))
                            dve.tensor_tensor(whole[:, k, :], hv[:, k % 2, :], comb_bc[s][:, c * CH:(c + 1) * CH],
                                              ALU.mult).then_inc(full_done, 1)

                        def low_part(k):
                            dve.wait_ge(high_done, n + (s * NT + k + 1))
                            dve.tensor_tensor(hh[1][:, k, :], whole[:, k, :], hh[0][:, k, :],
                                              ALU.subtract).then_inc(h_done, 1)

                        weighted(0)
                        for k in range(1, NT):
                            weighted(k)
                            low_part(k - 1)
                        low_part(NT - 1)
                dve.wait_ge(w3_done, H_FREE + E * NT)
                for c in range(NCH):
                    dve.tensor_tensor(R[:, c * CH:(c + 1) * CH], ps[:, 4 + c, :], X[:, c * CH:(c + 1) * CH],
                                      ALU.add).then_inc(r_ready, 1)
                dve_ln(0)
                dve_ln(1)

    with ExitStack() as st:
        def sb(name, shape, dt=F32):
            return st.enter_context(nc.sbuf_tensor(name, shape, dt))

        win, wgate, wout, carry = (later[n] for n in ("win", "wgate", "wout", "carry"))
        names = ("xre", "xim", "gx", "ga", "mag", "nrm", "tau", "tk", "thi", "tlo", "chi", "clo", "s", "c", "sn", "cs",
                 "t1", "t2", "t3", "t4")
        v = {n: sb(f"r_{n}", [C, T]) for n in names}
        v.update(t5=v["thi"], t6=v["tlo"], sq=v["ga"], carry=carry)
        by_chunk = [{n: t[:, c * CH:(c + 1) * CH] for n, t in v.items()} for c in range(NCH)]
        NRM_STEPS, THETA_STEPS, H_STEPS = NCH * 6, NCH * 12, 15
        sp_ = sb("sp_", [C, 8])
        ps = st.enter_context(nc.psum_tensor("ps5", [128, 8, 512], F32))
        (xh, xh_sb, gate_ps, gate_sb, spc, spe, spd, mags, nrm_out, u_ready, trig, y_ps, r_ready,
         chain, act_chain) = sems(st, "xh", "xh_sb", "gate_ps", "gate_sb", "spc", "spe", "spd", "mags",
                                  "nrm_out", "u_ready", "trig", "y_ps", "b5_r", "b5_chain", "b5_act")
        pe_ln, pe_ln2, act_ln, act_ln2, dve_ln, x_ready = ln_parts(st, "ln4", ps[:, 0:2, :], ps[:, 2:4, :], r_ready)

        with nc.Block() as block:
            @block.gpsimd
            def _(pool):
                for c, w in enumerate(by_chunk):
                    pool.wait_ge(nrm_out, c + 1)
                    pool.tensor_tensor(w["gx"], w["nrm"], w["gx"], ALU.mult).then_inc(u_ready, 1)
                    pool.wait_ge(u_ready, 4 * c + 1)
                    pool.tensor_tensor(w["xre"], w["xre"], w["gx"], ALU.mult).then_inc(u_ready, 1)
                    pool.tensor_tensor(w["xim"], w["xim"], w["gx"], ALU.mult).then_inc(u_ready, 1)
                    pool.tensor_tensor(w["mag"], w["mag"], w["carry"], ALU.mult).then_inc(u_ready, 1)

            @block.tensor
            def _(pe):
                for c in range(NCH):
                    for i in range(2):
                        pe.matmul(ps[:, 2 * c + i, :], win[:, i, :], X[:, c * CH:(c + 1) * CH],
                                  start=True, stop=True).then_inc(xh, 1)
                for c in range(NCH):
                    pe.wait_ge(xh_sb, 2 * c + 2)
                    for i in range(2):
                        pe.matmul(ps[:, 4 + 2 * c + i, :], wgate[:, i, 0, :], v["xre"][:, c * CH:(c + 1) * CH],
                                  start=True, stop=False)
                        pe.matmul(ps[:, 4 + 2 * c + i, :], wgate[:, i, 1, :], v["xim"][:, c * CH:(c + 1) * CH],
                                  start=False, stop=True).then_inc(gate_ps, 1)
                for c in range(NCH):
                    pe.wait_ge(chain, THETA_STEPS + H_STEPS * (c + 1))
                    pe.matmul(ps[:, 4 + c, :], wout[:, 0, :], v["t3"][:, c * CH:(c + 1) * CH], start=True, stop=False)
                    pe.matmul(ps[:, 4 + c, :], wout[:, 1, :], v["t4"][:, c * CH:(c + 1) * CH],
                              start=False, stop=True).then_inc(y_ps, 1)
                    pe_ln(c)
                pe_ln2(0)
                pe_ln2(1)

            @block.scalar
            def _(act):
                act.preload_act_table_set(EXP_LN)
                act.activation(sp_[:, 0:1], col["a_real"], ACT.Abs).then_inc(act_chain, 1)
                act.wait_ge(act_chain, 1)
                act.activation(sp_[:, 1:2], sp_[:, 0:1], ACT.Exp, scale=-1.0).then_inc(act_chain, 1)
                act.wait_ge(act_chain, 2)
                act.activation(sp_[:, 2:3], sp_[:, 1:2], ACT.Ln, bias=col["one"]).then_inc(spc, 1)
                for c in range(NCH):
                    for i, (dst, b) in enumerate((("xre", "b_in0"), ("xim", "b_in1"))):
                        act.wait_ge(xh, 2 * c + i + 1)
                        act.activation(v[dst][:, c * CH:(c + 1) * CH], ps[:, 2 * c + i, :], ACT.Identity,
                                       bias=col[b]).then_inc(xh_sb, 1)
                for c in range(NCH):
                    for i, (dst, b) in enumerate((("gx", "bgx"), ("ga", "bga"))):
                        act.wait_ge(gate_ps, 2 * c + i + 1)
                        act.activation(v[dst][:, c * CH:(c + 1) * CH], ps[:, 4 + 2 * c + i, :], ACT.Sigmoid,
                                       bias=col[b]).then_inc(gate_sb, 1)
                act.preload_act_table_set(EXP_LN)
                act.wait_ge(spd, 1)
                for c in range(NCH):
                    s = slice(c * CH, (c + 1) * CH)
                    act.wait_ge(gate_sb, 2 * c + 2)
                    act.activation(v["nrm"][:, s], v["ga"][:, s], ACT.Exp, scale=sp_[:, 6:7]).then_inc(mags, 1)
                    act.activation(v["mag"][:, s], v["ga"][:, s], ACT.Exp, scale=sp_[:, 5:6]).then_inc(mags, 1)
                for c in range(NCH):
                    s = slice(c * CH, (c + 1) * CH)
                    act.wait_ge(chain, NRM_STEPS - NCH + c + 1)
                    act.activation(v["nrm"][:, s], v["nrm"][:, s], ACT.Sqrt).then_inc(nrm_out, 1)
                act.preload_act_table(ACT.Sin)
                for c in range(NCH):
                    s = slice(c * CH, (c + 1) * CH)
                    act.wait_ge(chain, THETA_STEPS - NCH + c + 1)
                    act.activation(v["tk"][:, s], v["tau"][:, s], ACT.Abs).then_inc(act_chain, 1)
                    act.activation(v["s"][:, s], v["tau"][:, s], ACT.Sin, scale=PI).then_inc(trig, 1)
                    act.wait_ge(act_chain, 2 * c + 3)
                    act.activation(v["c"][:, s], v["tk"][:, s], ACT.Sin, scale=-PI, bias=col["half_pi"]).then_inc(trig, 1)
                    act.wait_ge(trig, 3 * c + 1)
                    act.activation(v["sq"][:, s], v["s"][:, s], ACT.Square).then_inc(act_chain, 1)
                    act.wait_ge(act_chain, 2 * c + 4)
                    act.activation(v["cs"][:, s], v["sq"][:, s], ACT.Identity, scale=-2.0, bias=col["one"]).then_inc(trig, 1)
                act.preload_act_table_set(EXP_LN)
                act_ln(0)
                act_ln(1)
                act_ln2(0)
                act_ln2(1)

            @block.vector
            def _(dve):
                dve.wait_ge(spc, 1)
                dve.tensor_scalar(sp_[:, 3:4], col["a_real"], 0.0, None, ALU.max).then_inc(spe, 1)
                dve.wait_ge(spe, 1)
                dve.tensor_tensor(sp_[:, 4:5], sp_[:, 3:4], sp_[:, 2:3], ALU.add).then_inc(spe, 1)
                dve.wait_ge(spe, 2)
                dve.tensor_scalar(sp_[:, 5:6], sp_[:, 4:5], -8.0, None, ALU.mult)
                dve.tensor_scalar(sp_[:, 6:7], sp_[:, 4:5], -16.0, None, ALU.mult).then_inc(spd, 1)

                count = [0]

                def step(emit, also=None):
                    for c in range(NCH):
                        if count[0] >= NCH:
                            dve.wait_ge(chain, count[0] - 1)
                        if also:
                            also(c)
                        emit(by_chunk[c]).then_inc(chain, 1)
                        count[0] += 1

                def times(o, x, y, op=ALU.mult):
                    step(lambda w: dve.tensor_tensor(w[o], w[x], w[y], op))

                step(lambda w: dve.tensor_scalar(w["tau"], w["ga"], col["a_imag"], 1.0 / (2.0 * PI), ALU.mult, ALU.mult),
                     also=lambda c: dve.wait_ge(gate_sb, 2 * c + 2))
                step(lambda w: dve.tensor_scalar(w["tk"], w["tau"], ROUND, ROUND, ALU.add, ALU.subtract))
                times("t1", "tau", "tk", ALU.subtract)
                step(lambda w: dve.tensor_scalar(w["thi"], w["t1"], ROUND12, ROUND12, ALU.add, ALU.subtract))
                step(lambda w: dve.tensor_scalar(w["t2"], w["nrm"], -1.0, 1.0, ALU.mult, ALU.add),
                     also=lambda c: dve.wait_ge(mags, 2 * c + 2))
                step(lambda w: dve.tensor_scalar(w["nrm"], w["t2"], 1e-6, None, ALU.max))
                NRM_IN = count[0]
                assert NRM_IN == NRM_STEPS
                times("tlo", "t1", "thi", ALU.subtract)
                step(lambda w: dve.tensor_tensor_scan(w["chi"], w["carry"], w["thi"], 0.0, ALU.mult, ALU.add))
                step(lambda w: dve.tensor_tensor_scan(w["clo"], w["carry"], w["tlo"], 0.0, ALU.mult, ALU.add))
                step(lambda w: dve.tensor_scalar(w["tk"], w["chi"], ROUND, ROUND, ALU.add, ALU.subtract))
                times("t1", "chi", "tk", ALU.subtract)
                times("tau", "t1", "clo", ALU.add)
                assert count[0] == THETA_STEPS

                def output(c):
                    dve.wait_ge(y_ps, c + 1)
                    dve.scalar_tensor_tensor(out=R[:, c * CH:(c + 1) * CH], in0=ps[:, 4 + c, :], scalar=col["b_out"],
                                             in1=X[:, c * CH:(c + 1) * CH], op0=ALU.add, op1=ALU.add).then_inc(r_ready, 1)

                for c, w in enumerate(by_chunk):
                    def product(o, x, y, op=ALU.mult):
                        dve.wait_ge(chain, count[0] - 1)
                        dve.tensor_tensor(w[o], w[x], w[y], op).then_inc(chain, 1)
                        count[0] += 1

                    def scan(o, x):
                        dve.wait_ge(chain, count[0] - 1)
                        dve.tensor_tensor_scan(w[o], w["mag"], w[x], 0.0, ALU.mult, ALU.add).then_inc(chain, 1)
                        count[0] += 1

                    dve.wait_ge(trig, 3 * c + 3)
                    dve.scalar_tensor_tensor(out=w["sn"], in0=w["s"], scalar=2.0, in1=w["c"], op0=ALU.mult,
                                             op1=ALU.mult).then_inc(chain, 1)
                    count[0] += 1
                    dve.wait_ge(u_ready, 4 * c + 4)
                    product("t1", "xre", "cs")
                    product("t2", "xim", "sn")
                    product("t3", "xim", "cs")
                    product("t4", "xre", "sn")
                    product("t1", "t1", "t2", ALU.add)
                    product("t3", "t3", "t4", ALU.subtract)
                    scan("xre", "t1")
                    scan("xim", "t3")
                    product("t1", "xre", "cs")
                    product("t2", "xim", "sn")
                    product("t5", "xre", "sn")
                    product("t6", "xim", "cs")
                    if c:
                        output(c - 1)
                    product("t3", "t1", "t2", ALU.subtract)
                    product("t4", "t5", "t6", ALU.add)
                    assert count[0] == THETA_STEPS + H_STEPS * (c + 1)
                output(NCH - 1)
                dve_ln(0)
                dve_ln(1)

    high_w, low_w = ({n: keep(f"{part}_{n}", a[n].shape, F32R) for n in FFN_WEIGHTS} for part in ("high", "low"))

    with ExitStack() as st:
        def sb(name, shape, dt=F32):
            return st.enter_context(nc.sbuf_tensor(name, shape, dt))

        ffn_w = {n: sb(f"w_{n}", a[n].shape) for n in FFN_WEIGHTS}
        wq = later["wq6"]
        wk = later["wk6"]
        den_sel = later["den_sel"]
        ctx_k = later["ctx_k"]
        wv, ident = later["wv6"], later["ident"]
        q = sb("q6", [C, T])
        qk_high, qk_low = (sb(f"qk_{part}", [2 * CC, T], F32R) for part in ("high", "low"))
        shift = sb("shift6", [128, T], F32R)
        pick = sb("pick6", [128, 128], F32R)
        bkq = sb("bkq6", [128, 2 * NB])
        prob = sb("prob6", [128, 3, 2, TQ])
        nm = sb("nm6", [128, 2 * NB])
        nm_b = sb("nm_b6", [128, 2 * NB])
        osb = sb("osb6", [128, 2, TQ])
        rden = sb("rden6", [C, 2, TQ])
        att = sb("att6", [C, 2, TQ])
        s1 = st.enter_context(nc.psum_tensor("s1_6", [128, 4, 512], F32))
        s2 = st.enter_context(nc.psum_tensor("s2_6", [128, 2, 512], F32))
        o_ps = st.enter_context(nc.psum_tensor("o6", [128, 512], F32))
        fin = st.enter_context(nc.psum_tensor("fin6", [128, 512], F32))
        (q_ps, q_sb, qk_ps, qk_sb, s1_ready, s1_red, row_ps, row_sb, s2_ready, exp_done, av_done, o_sb, fin_ps,
         drec, att_done, r_ready, split, ffn_in, set_up, bkq_ps, bkq_sb, nm_done, row_high, qk_part) = sems(
             st, *[f"b6_{n}" for n in (
                 "q_ps", "q_sb", "qk_ps", "qk_sb", "s1_ready", "s1_red", "row_ps", "row_sb", "s2_ready", "exp_done",
                 "av_done", "o_sb", "fin_ps", "drec", "att_done", "r", "split", "ffn_in", "set_up", "bkq_ps", "bkq_sb",
                 "nm_done", "row_high", "qk_part")])
        pe_ln, pe_ln2, act_ln, act_ln2, dve_ln, x_ready = ln_parts(st, "ln5", s1[:, 0:2, :], s1[:, 2:4, :], r_ready)
        PAIRS = (NKT + 1) // 2

        with nc.Block() as block:
            @block.gpsimd
            def _(pool):
                pool.memset(pick[:].bitcast(F32), 0.0).then_inc(set_up, 1)
                pool.wait_ge(set_up, 1)
                pool.memset(pick[0:1, :].bitcast(F32), 1.0)
                pool.memset(pick[32:33, :].bitcast(F32), 1.0).then_inc(set_up, 1)
                pool.wait_ge(set_up, 2)
                pool.memset(shift[:].bitcast(F32), 0.0).then_inc(set_up, 1)
                for n in FFN_WEIGHTS:
                    pool.dma_start(ffn_w[n][:], a[n]).then_inc(ffn_in, 16)
                pool.wait_ge(ffn_in, 16 * len(FFN_WEIGHTS))
                for i, n in enumerate(FFN_WEIGHTS):
                    pool.tensor_copy(high_w[n][:], ffn_w[n][:]).then_inc(split, 1)
                    pool.wait_ge(split, 2 * i + 1)
                    pool.tensor_tensor(low_w[n][:], ffn_w[n][:], high_w[n][:], ALU.subtract).then_inc(split, 1)
                    pool.wait_ge(split, 2 * i + 2)

            @block.tensor
            def _(pe):
                for c in range(NCH):
                    pe.matmul(s1[:, c, :], wq[:], X[:, c * CH:(c + 1) * CH], start=True, stop=True).then_inc(q_ps, 1)
                for c in range(NCH):
                    pe.wait_ge(q_sb, c + 1)
                    pe.matmul(s2[:, c, :], wk[:], q[:, c * CH:(c + 1) * CH],
                              start=True, stop=True).then_inc(qk_ps, 1)

                def query_major(b, t):
                    n = 2 * b + t
                    if t == 0:
                        pe.wait_ge(qk_sb, 1 + b // (NB // NCH))
                    if n:
                        pe.wait_ge(s1_red, n)
                    for i in range(4):
                        w = min(512, TKE - 512 * i)
                        for part in (qk_high, qk_low):
                            last = pe.matmul(s1[:, i, 0:w], part[:, n * 128:(n + 1) * 128], ctx_2[:, b, i * 512:i * 512 + w],
                                             start=(part is qk_high), stop=(part is qk_low))
                    last.then_inc(s1_ready, 1)

                def max_row(b):
                    pe.wait_ge(nm_done, 2 * b + 2)
                    if b >= 2:
                        pe.wait_ge(att_done, b - 1)
                    for t in range(2):
                        n = 2 * b + t
                        o = fin[0:33, t * 128:(t + 1) * 128]
                        pe.matmul(o, nm_b[:, n:n + 1].to_broadcast([128, 33]), ident, start=True, stop=False)
                        last = pe.matmul(o, col["bk6"].to_broadcast([128, 33]), q[:, n * 128:(n + 1) * 128],
                                         start=False, stop=True)
                    last.then_inc(row_ps, 1)

                def scores_t(b, p):
                    k = b * PAIRS + p
                    if k >= 2:
                        pe.wait_ge(exp_done, k - 1)
                    at = slice(b * TQ, (b + 1) * TQ)
                    if 2 * p + 1 < NKT:
                        pe.matmul(s2[:, k % 2, :].rearrange("p (i q) -> p i q", i=2), pick[:],
                                  shift[:, at].unsqueeze(1).to_broadcast([128, 2, TQ]), start=True, stop=False,
                                  skip_group_check=True)
                    else:
                        pe.matmul(s2[0:KLAST, k % 2, 0:TQ], pick[:, 0:KLAST], shift[:, at], start=True, stop=False,
                                  skip_group_check=True)
                    for t in range(2 * p, min(2 * p + 2, NKT)):
                        m = 128 if t < NKT - 1 else KLAST
                        for part in (qk_high, qk_low):
                            last = pe.matmul(s2[0:m, k % 2, (t % 2) * TQ:(t % 2 + 1) * TQ],
                                             ctx_2[:, b, t * 128:t * 128 + m], part[:, at], start=False,
                                             stop=(part is qk_low), skip_group_check=True)
                    last.then_inc(s2_ready, 1)

                def outputs(b, p):
                    k = b * PAIRS + p
                    pe.wait_ge(exp_done, k + 1)
                    for t in range(2 * p, min(2 * p + 2, NKT)):
                        m = 128 if t < NKT - 1 else KLAST
                        last = pe.matmul(o_ps[0:CC + 1, 0:TQ], ctx_k[0:m, b, t, :], prob[0:m, k % 3, t % 2, :],
                                         start=(t == 0), stop=(t == NKT - 1))
                    last.then_inc(av_done, 1)

                query_major(0, 0)
                for n in range(2 * NB):
                    last = pe.matmul(o_ps[:, n:n + 1], q[:, n * 128:(n + 1) * 128], col["bk6"], start=True, stop=True)
                last.then_inc(bkq_ps, 1)
                query_major(0, 1)
                max_row(0)
                pe.wait_ge(set_up, 3)
                pe.wait_ge(bkq_sb, 1)
                pe.wait_ge(row_sb, 1)
                scores_t(0, 0)
                for b in range(NB):
                    for p in range(PAIRS):
                        if p + 1 < PAIRS:
                            scores_t(b, p + 1)
                        if p == 0 and b:
                            pe.wait_ge(o_sb, b)
                        if b + 1 < NB and p in (0, 2):
                            query_major(b + 1, p // 2)
                        outputs(b, p)
                        if b + 1 < NB and p == PAIRS - 2:
                            max_row(b + 1)
                    if b + 1 < NB:
                        pe.wait_ge(row_sb, b + 2)
                        scores_t(b + 1, 0)
                    pe.wait_ge(o_sb, b + 1)
                    if b:
                        pe.wait_ge(att_done, b)
                    pe.matmul(fin[:, 0:TQ], wv[:], osb[:, b % 2, :], start=True, stop=True)
                    pe.matmul(fin[:, TQ:2 * TQ], den_sel[:], osb[:, b % 2, :], start=True, stop=True).then_inc(fin_ps, 1)
                pe_ln(0)
                pe_ln(1)
                pe_ln2(0)
                pe_ln2(1)

            @block.scalar
            def _(act):
                for c in range(NCH):
                    act.wait_ge(q_ps, c + 1)
                    act.activation(q[:, c * CH:(c + 1) * CH], s1[:, c, :], ACT.Identity, bias=col["bq6"]).then_inc(q_sb, 1)

                for b in range(NB):
                    for p in range(PAIRS):
                        k = b * PAIRS + p
                        act.wait_ge(s2_ready, k + 1)
                        if k >= 3:
                            act.wait_ge(av_done, k - 2)
                        m, w = (128, 2 * TQ) if p < PAIRS - 1 or NKT % 2 == 0 else (KLAST, TQ)
                        act.activation(prob[0:m, k % 3].rearrange("p i q -> p (i q)")[:, 0:w], s2[0:m, k % 2, 0:w],
                                       ACT.Exp).then_inc(exp_done, 1)
                    act.wait_ge(fin_ps, b + 1)
                    act.activation(rden[:, b % 2, :], fin[:, TQ:2 * TQ], ACT.Copy).then_inc(drec, 1)
                act.preload_act_table_set(EXP_LN)
                act_ln(0)
                act_ln(1)
                act_ln2(0)
                act_ln2(1)

            @block.vector
            def _(dve):
                dve.memset(osb[:], 0.0)

                def split_qk(c):
                    at = slice(c * CH, (c + 1) * CH)
                    dve.wait_ge(qk_ps, c + 1)
                    dve.tensor_copy(qk_high[:, at], s2[:, c, :]).then_inc(qk_part, 1)
                    dve.wait_ge(qk_part, c + 1)
                    dve.tensor_tensor(qk_low[:, at], s2[:, c, :], qk_high[:, at], ALU.subtract).then_inc(qk_sb, 1)

                def maxima(b):
                    for t in range(2):
                        n = 2 * b + t
                        dve.wait_ge(s1_ready, n + 1)
                        dve.tensor_reduce(nm[:, n:n + 1], s1[:].rearrange("p b n -> p (b n)")[:, 0:TK], AX.X, ALU.max,
                                          negate=True).then_inc(s1_red, 1)
                        if n == 0:
                            dve.wait_ge(bkq_ps, 1)
                            dve.tensor_copy(bkq[:], o_ps[:, 0:2 * NB]).then_inc(bkq_sb, 1)
                            dve.wait_ge(bkq_sb, 1)
                        dve.wait_ge(s1_red, n + 1)
                        dve.tensor_tensor(nm_b[:, n:n + 1], nm[:, n:n + 1], bkq[:, n:n + 1],
                                          ALU.subtract).then_inc(nm_done, 1)

                def row(b):
                    at = slice(b * TQ, (b + 1) * TQ)
                    dve.wait_ge(row_ps, b + 1)
                    if b == 0:
                        dve.wait_ge(set_up, 3)
                    dve.tensor_copy(shift[0:33, at], fin[0:33, 0:TQ]).then_inc(row_high, 1)
                    dve.wait_ge(row_high, b + 1)
                    dve.tensor_tensor(shift[32:33, at], fin[32:33, 0:TQ], shift[32:33, at], ALU.subtract).then_inc(row_sb, 1)

                split_qk(0)
                split_qk(1)
                maxima(0)
                row(0)
                for b in range(NB):
                    if b + 1 < NB:
                        maxima(b + 1)
                        row(b + 1)
                    dve.wait_ge(av_done, PAIRS * (b + 1))
                    dve.tensor_copy(osb[0:CC, b % 2, :], o_ps[0:CC, 0:TQ])
                    dve.reciprocal(osb[CC:CC + 1, b % 2, :], o_ps[CC:CC + 1, 0:TQ]).then_inc(o_sb, 1)
                    dve.wait_ge(drec, b + 1)
                    dve.tensor_tensor(att[:, b % 2, :], fin[:, 0:TQ], rden[:, b % 2, :], ALU.mult).then_inc(att_done, 1)
                    dve.wait_ge(att_done, b + 1)
                    s = slice(b * TQ, (b + 1) * TQ)
                    last = dve.scalar_tensor_tensor(out=R[:, s], in0=att[:, b % 2, :], scalar=col["bv6"], in1=X[:, s],
                                                    op0=ALU.add, op1=ALU.add)
                    if b % 2:
                        last.then_inc(r_ready, 1)
                dve_ln(0)
                dve_ln(1)

    with ExitStack() as st:
        def sb(name, shape, dt=F32):
            return st.enter_context(nc.sbuf_tensor(name, shape, dt))

        NM = HID // 128
        xa = [sb(f"x7_{n}", [C, T], F32R) for n in ("high", "low")]
        def over_context(tensor, n, dt):
            return tensor[:].bitcast(dt).rearrange("p b k -> p (b k)")[:, n * NM * CH:(n + 1) * NM * CH].rearrange(
                "p (m n) -> p m n", m=NM)

        place = [[over_context(ctx_2, n, F32R) for n in range(2)]]
        place += [[sb(f"h_{part}{n}", [128, NM, CH], F32R) for part in ("high", "low")] for n in (1, 2)]
        ha, hb, hc = (place[0], place[1]), (place[2], place[0]), (place[1], place[2])
        whole = over_context(ctx_t, 0, F32)
        sg = sb("sg7", [128, 2, CH])
        ps = st.enter_context(nc.psum_tensor("ps7", [128, 8, 512], F32))
        (x_split, full_done, high_done, g1_done, g2_done, up_ps, sg_done, ha_done, h1_ps, hb_done, h2_ps, hc_done, y_ps, r_ready, stored) = sems(
            st, *[f"b7_{n}" for n in ("x_split", "full_done", "high_done", "g1_done", "g2_done", "up_ps", "sg_done", "ha_done", "h1_ps", "hb_done", "h2_ps", "hc_done", "y_ps",
                                      "r", "stored")])
        pe_ln, pe_ln2, act_ln, _, dve_ln, x_ready, act_log, act_exp = ln_parts(
            st, "ln6", ps[:, 2:4, :], ps[:, 4:6, :], r_ready, apart=True)
        tiles = [(c, m) for c in range(NCH) for m in range(NM)]

        with nc.Block() as block:
            @block.sync
            def _(sp):
                for c in range(NCH):
                    sp.wait_ge(x_ready, c + 1)
                    sp.dma_start(out[:, c * CH:(c + 1) * CH], X[:, c * CH:(c + 1) * CH]).then_inc(stored, 16)
                sp.wait_ge(stored, 16 * NCH)

            @block.gpsimd
            def _(pool):
                for k, (c, m) in enumerate(tiles):
                    pool.wait_ge(high_done, k + 1)
                    pool.tensor_tensor(ha[c][1][:, m, :], whole[:, k % 4, :], ha[c][0][:, m, :],
                                       ALU.subtract).then_inc(ha_done, 1)

            @block.tensor
            def _(pe):
                def passes(o, weight, m, x, first, last):
                    high, low = (w[:, m * 128:(m + 1) * 128] for w in weight)
                    pe.matmul(o, high, x[0], start=first, stop=False)
                    pe.matmul(o, high, x[1], start=False, stop=False)
                    return pe.matmul(o, low, x[0], start=False, stop=last)

                for k, (c, m) in enumerate(tiles):
                    pe.wait_ge(x_split, 2 * c + 2)
                    if k >= 2:
                        pe.wait_ge(full_done, k - 1)
                    for i in range(2):
                        done = passes(ps[:, 2 * i + k % 2, :], (high_w["w12"][:, i, :], low_w["w12"][:, i, :]), m,
                                      [part[:, c * CH:(c + 1) * CH] for part in xa], True, True)
                    done.then_inc(up_ps, 1)

                def hidden(name, src, src_ready, banks, emptied, ready):
                    for k, (c, m) in enumerate(tiles):
                        pe.wait_ge(src_ready, NM * (c + 1))
                        if k >= 2:
                            pe.wait_ge(emptied, k - 1)
                        for i in range(NM):
                            done = passes(ps[:, banks + k % 2, :], (high_w[name][:, i, :], low_w[name][:, i, :]), m,
                                          [part[:, i, :] for part in src[c]], i == 0, i == NM - 1)
                        done.then_inc(ready, 1)

                hidden("h1w", ha, ha_done, 4, g1_done, h1_ps)
                hidden("h2w", hb, hb_done, 6, g2_done, h2_ps)
                for c in range(NCH):
                    pe.wait_ge(hc_done, NM * (c + 1))
                    for i in range(NM):
                        done = passes(ps[:, c, :], (high_w["w3"][:, i, :], low_w["w3"][:, i, :]), 0,
                                      [part[:, i, :] for part in hc[c]], i == 0, i == NM - 1)
                    done.then_inc(y_ps, 1)
                pe_ln(0)
                pe_ln(1)
                pe_ln2(0)
                pe_ln2(1)

            @block.scalar
            def _(act):
                act.preload_act_table(ACT.Silu)
                for k, (c, m) in enumerate(tiles):
                    act.wait_ge(up_ps, k + 1)
                    if k >= 2:
                        act.wait_ge(full_done, k - 1)
                    act.activation(sg[:, k % 2, :], ps[:, k % 2, :], ACT.Silu, scale=col[f"s1_{m}"]).then_inc(sg_done, 1)
                act.preload_act_table(ACT.Gelu)

                def gelus(scale, banks, ready, done, read, read_before):
                    for k, (c, m) in enumerate(tiles):
                        act.wait_ge(ready, k + 1)
                        if k >= 4:
                            act.wait_ge(read, k - 3)
                        else:
                            act.wait_ge(*read_before[k])
                        act.activation(whole[:, k % 4, :], ps[:, banks + k % 2, :], ACT.Gelu,
                                       scale=col[f"{scale}_{m}"]).then_inc(done, 1)

                gelus("sh1", 4, h1_ps, g1_done, hb_done, [(ha_done, 5 + k) for k in range(4)])
                gelus("sh2", 6, h2_ps, g2_done, hc_done, [(hb_done, 5 + k) for k in range(4)])
                act.preload_act_table_set("natural_log")
                act_ln(0)
                act_ln(1)
                act_log(0)
                act_log(1)
                act.preload_act_table_set(EXP_LN)
                act_exp(0)
                act_exp(1)

            @block.vector
            def _(dve):
                for c in range(NCH):
                    at = slice(c * CH, (c + 1) * CH)
                    dve.tensor_copy(xa[0][:, at], X[:, at]).then_inc(x_split, 1)
                    dve.wait_ge(x_split, 2 * c + 1)
                    dve.tensor_tensor(xa[1][:, at], X[:, at], xa[0][:, at], ALU.subtract).then_inc(x_split, 1)
                for k, (c, m) in enumerate(tiles):
                    dve.wait_ge(sg_done, k + 1)
                    if k >= 4:
                        dve.wait_ge(ha_done, k - 3)
                    dve.scalar_tensor_tensor(out=whole[:, k % 4, :], in0=ps[:, 2 + k % 2, :],
                                             scalar=col[f"s2_{m}"], in1=sg[:, k % 2, :], op0=ALU.mult,
                                             op1=ALU.mult).then_inc(full_done, 1)
                    dve.wait_ge(full_done, k + 1)
                    dve.tensor_copy(ha[c][0][:, m, :], whole[:, k % 4, :]).then_inc(high_done, 1)

                def split_layer(dst, done, ready, base_count, place_read):
                    for k, (c, m) in enumerate(tiles):
                        dve.wait_ge(ready, k + 1)
                        if m == 0 and place_read[c]:
                            dve.wait_ge(*place_read[c])
                        high, low = (part[:, m, :] for part in dst[c])
                        dve.tensor_copy(high, whole[:, k % 4, :]).then_inc(high_done, 1)
                        dve.wait_ge(high_done, base_count + k + 1)
                        dve.tensor_tensor(low, whole[:, k % 4, :], high, ALU.subtract).then_inc(done, 1)

                split_layer(hb, hb_done, g1_done, len(tiles), [None, (h1_ps, NM)])
                split_layer(hc, hc_done, g2_done, 2 * len(tiles), [(h1_ps, 2 * NM), (h2_ps, NM)])
                for c in range(NCH):
                    dve.wait_ge(y_ps, c + 1)
                    dve.scalar_tensor_tensor(out=R[:, c * CH:(c + 1) * CH], in0=ps[:, c, :], scalar=col["s3"],
                                             in1=X[:, c * CH:(c + 1) * CH], op0=ALU.mult, op1=ALU.add).then_inc(r_ready, 1)
                dve_ln(0)
                dve_ln(1)


FOR_BLOCK_3 = ("spread", "wp", "wg", "iota")
LATER = ("win", "wgate", "wout", "carry", "wq6", "wk6", "wv6", "den_sel", "ctx_k")
FFN_WEIGHTS = ("w12", "h1w", "h2w", "w3")
BIAS_COLUMNS = ("bq0", "bk0", "bo0", "bks", "bqs", "bqc", "bp", "eps", "a_real", "one", "b_in0", "b_in1", "bgx", "bga",
                "half_pi", "a_imag", "b_out", "bq6", "bk6", "bv6", *[f"{n}_{m}" for n in ("s1", "s2", "sh1", "sh2") for m in range(4)], "s3")


def laid_out(i):
    f = {k: np.asarray(v) for k, v in i.items()}
    f4 = np.float32
    order = np.array([8 * (4 * g + 2 * e + j) + c for g in range(4) for e in range(2) for c in range(8) for j in range(2)])
    o = {}
    o["x_t"] = f["x"].reshape(T, C).T
    ctx = f["ctx_512"]
    o["ctx_t"] = ctx.transpose(2, 0, 1)
    ctx_k = np.zeros((128, NB, NKT, CC + 1), f4)
    for t in range(NKT):
        m = min(128, TK - 128 * t)
        ctx_k[:m, :, t, :CC] = ctx[:, 128 * t:128 * t + m].transpose(1, 0, 2)
        ctx_k[:m, :, t, CC] = 1.0
    o["ctx_k"] = ctx_k
    def rows_below(*parts):
        height = sum(p.shape[0] for p in parts)
        return np.concatenate([*parts, np.zeros((128 - height, parts[0].shape[1]), f4)])

    def value_columns(w):
        p = np.zeros((w.shape[0], H, VW), f4)
        p[:, :, :HD] = w.reshape(-1, H, HD)
        return p

    def value_bias(name):
        bias = value_columns(f[name][None])
        bias[:, :, HD] = 1.0
        return bias.reshape(1, -1)

    o["att_w"] = np.concatenate([*[f[f"L0_attn_W{n}"] for n in "qkvo"], np.broadcast_to(f["L0_attn_bv"], (128, C)),
                                 np.full((C, C), -0.5, f4), np.full((C, 1), -1.0, f4)], 1)
    o["proj_w"] = np.concatenate([
        rows_below(f["L0_xattn_Wck"][:, order], f["L0_xattn_bck"][None, order]),
        f["L0_xattn_Wk"][:, order], f["L0_xattn_Wq"][:, order], f["L0_xattn_Wcq"][:, order],
        rows_below(value_columns(f["L0_xattn_Wcv"]).reshape(CC, -1), value_bias("L0_xattn_bcv")),
        value_columns(f["L0_xattn_Wv"]).reshape(C, -1),
        np.broadcast_to(value_bias("L0_xattn_bv"), (128, H * VW))], 1)
    spread = np.zeros((128, 128), f4)
    wp = np.zeros((128, NG, C), f4)
    for hh in range(4):
        spread[hh:12:4, 32 * hh:32 * hh + 32] = 1.0
        for g in range(NG):
            wp[32 * hh:32 * hh + HD, g] = f["L0_xattn_Wp"][8 * (4 * g + hh):8 * (4 * g + hh) + 8]
    o["spread"], o["wp"] = spread, wp
    key, query = np.arange(128)[:, None], np.arange(128)[None]
    mask = np.where(key > query, MASKED, 0.0).astype(f4)
    o["masks"] = np.stack([mask, mask.T], 1)
    o["wg"] = f["L0_ffn_Wg"].T
    o["iota"] = np.broadcast_to(np.tile(np.arange(E, dtype=f4), 8), (128, 8 * E))
    o["b3"] = f["L0_ffn_b3"]
    o["wexp"] = np.concatenate([
        f["L0_ffn_W1"].transpose(0, 2, 1), f["L0_ffn_W2"].transpose(0, 2, 1),
        f["L0_ffn_W3"].reshape(E, C, DFF // 128, 128).transpose(0, 3, 2, 1).reshape(E, 128, DFF),
        f["L0_ffn_b1"].reshape(E, DFF // 128, 128).transpose(0, 2, 1),
        f["L0_ffn_b2"].reshape(E, DFF // 128, 128).transpose(0, 2, 1)], 2)
    o["win"] = f["L1_attn_w_in"].reshape(C, 2, C)
    gates = np.zeros((2, 2 * C, C), f4)
    for i_, n in enumerate(("x", "a")):
        for blk in range(8):
            gates[i_, 32 * blk:32 * blk + 32, 16 * blk:16 * blk + 16] = f[f"L1_attn_w_g{n}"][blk]
    o["wgate"] = gates.reshape(2, 2, C, C).transpose(2, 0, 1, 3)
    o["wout"] = f["L1_attn_w_out"].reshape(2, C, C).transpose(1, 0, 2)
    carry = np.ones((C, T), f4)
    carry[:, ::TQ] = 0.0
    o["carry"] = carry
    o["wq6"] = f["L1_xattn_Wq"]
    o["wk6"] = np.concatenate([f["L1_xattn_Wk"].T] * 2, 1)
    o["wv6"] = rows_below(f["L1_xattn_Wv"])
    den_sel = np.zeros((C, C), f4)
    den_sel[CC] = 1.0
    o["den_sel"] = den_sel
    o["w12"] = np.stack([f["L1_ffn_w1_w"].T, f["L1_ffn_w2_w"].T], 1)
    for n in ("h1", "h2"):
        o[f"{n}w"] = f[f"L1_ffn_{n}_w"].T.reshape(HID // 128, 128, HID).transpose(1, 0, 2)
    o["w3"] = f["L1_ffn_w3_w"].T.reshape(HID // 128, 128, C).transpose(1, 0, 2)
    columns = {
        "bq0": f["L0_attn_bq"], "bk0": f["L0_attn_bk"], "bo0": f["L0_attn_bo"], "bks": f["L0_xattn_bk"][order],
        "bqs": f["L0_xattn_bq"][order], "bqc": f["L0_xattn_bcq"][order], "bp": f["L0_xattn_bp"],
        "eps": np.full(C, EPS, f4), "a_real": f["L1_attn_a_real_param"], "one": np.ones(C, f4),
        "b_in0": f["L1_attn_b_in"][:C], "b_in1": f["L1_attn_b_in"][C:], "bgx": f["L1_attn_b_gx"],
        "bga": f["L1_attn_b_ga"], "half_pi": np.full(C, PI / 2, f4), "a_imag": f["L1_attn_a_imag_param"],
        "b_out": f["L1_attn_b_out"], "bq6": f["L1_xattn_bq"], "bk6": f["L1_xattn_bk"], "bv6": f["L1_xattn_bv"], "s3": f["L1_ffn_w3_s"]}
    for n, src in (("s1", "w1_s"), ("s2", "w2_s"), ("sh1", "h1_s"), ("sh2", "h2_s")):
        for m in range(HID // 128):
            columns[f"{n}_{m}"] = f[f"L1_ffn_{src}"][m * 128:(m + 1) * 128]
    o["base"] = np.concatenate([np.eye(C, dtype=f4) - f4(1.0 / C), np.full((C, C), 1.0 / C, f4), np.eye(128, dtype=f4),
                                np.stack([columns[n] for n in BIAS_COLUMNS], 1)], 1)
    return {k: np.ascontiguousarray(v) for k, v in o.items()}


def kernel(**inputs):
    import concourse.bacc as bacc
    from concourse.bass_utils import run_bass_kernel_spmd

    nc = bacc.Bacc("TRN2", target_bir_lowering=False, num_devices=1)
    arrays = laid_out(inputs)
    args = {n: nc.dram_tensor(f"in_{n}", v.shape, mybir.dt.from_np(v.dtype), kind="ExternalInput").ap()
            for n, v in arrays.items()}
    out = nc.dram_tensor("out_t", (C, T), F32, kind="ExternalOutput").ap()
    decoder_program(nc, args, out)
    r = run_bass_kernel_spmd(nc, [{f"in_{n}": v for n, v in arrays.items()}], core_ids=[0])
    return r.results[0]["out_t"].T.reshape(NB, TQ, C)
```
